# Optimizing a Trainium2 kernel written in Bass

```python
import numpy as np
import jax
import jax.numpy as jnp

def _softmax(x, axis=-1):
    return jax.nn.softmax(x, axis=axis)

def _gelu(x):
    return jax.nn.gelu(x, approximate=True)

def _silu(x):
    return jax.nn.silu(x)

def _sigmoid(x):
    return jax.nn.sigmoid(x)

def _layernorm(x, axis=-1, eps=1e-05):
    m = jnp.mean(x, axis=axis, keepdims=True)
    v = jnp.var(x, axis=axis, keepdims=True)
    return (x - m) / jnp.sqrt(v + eps)

def _scatter_add(tgt, idx, src, axis=0):
    return tgt.at[idx].add(src)

def _segment_sum(src, seg, n):
    return jax.ops.segment_sum(src, seg, n)
kernel_name = 'mk_pixart_seq_d4_seqx_r8_1edab1'

def setup_inputs(seed: int=0):
    np.random.seed(seed)
    _w = jnp.asarray

    def _rec_inputs():
        import jax
        import jax.numpy as jnp
        _rk = jax.random.key(seed)
        x = -0.0002928 + 1 * jax.random.normal(jax.random.fold_in(_rk, 1), (16, 128, 128), jnp.float32)
        _lenS = 128 - jax.random.randint(jax.random.fold_in(_rk, 7), (16,), 0, max(1, 128 // 4) + 1, jnp.int32)
        _lenS2 = 77 - jax.random.randint(jax.random.fold_in(_rk, 8), (16,), 0, max(1, 77 // 4) + 1, jnp.int32)
        cond_1024 = 0.000887014 + 1.03683 * jax.random.normal(jax.random.fold_in(_rk, 11), (16, 128), jnp.float32)
        _ctx_1024P = jax.random.normal(jax.random.fold_in(_rk, 12), (16, 16, 128), jnp.float32)
        _ctx_1024c = jax.random.dirichlet(jax.random.fold_in(_rk, 512), 0.3 * jnp.ones((16,), jnp.float32), (16, 77))
        _ctx_1024t = jnp.einsum('bsk,bkd->bsd', _ctx_1024c, _ctx_1024P)
        _ctx_1024t = _ctx_1024t * jax.lax.rsqrt(jnp.mean(jnp.square(_ctx_1024t)) + 1e-12) * 0.953939
        ctx_1024 = -0.00606593 + 0.997213 * (_ctx_1024t + 0.3 * jax.random.normal(jax.random.fold_in(_rk, 612), (16, 77, 128), jnp.float32))
        _validS = jnp.arange(128)[None, :] < _lenS[:, None]
        _validS2 = jnp.arange(77)[None, :] < _lenS2[:, None]
        _causal = jnp.tril(jnp.ones((128, 128), dtype=bool))
        mask_BxS2_bf1 = jnp.ones((16, 77), dtype=bool)
        mask_SxS_bk0 = jnp.logical_not(jnp.broadcast_to(_validS[0:1, :], (128, 128)))
        return (x, cond_1024, ctx_1024, mask_BxS2_bf1, mask_SxS_bk0)
    x, cond_1024, ctx_1024, mask_BxS2_bf1, mask_SxS_bk0 = _rec_inputs()

    def _L0_xcond_setup():
        import jax, jax.numpy as jnp
        import numpy as np
        B, N, D, H, LC = (2, 128, 128, 16, 77)
        HD = D // H
        BLOCK = 16
        ROPE_BASE = 10000.0
        EPS = 1e-05

        def _block_diff_mask(n, block_size):
            idx = np.arange(2 * n)
            q = idx[:, None]
            kv = idx[None, :]
            fq = q >= n
            fkv = kv >= n
            bq = np.where(fq, (q - n) // block_size, q // block_size)
            bkv = np.where(fkv, (kv - n) // block_size, kv // block_size)
            block_diagonal = (bq == bkv) & (fq == fkv)
            offset_block_causal = (bq > bkv) & fkv & ~fq
            block_causal = (bq >= bkv) & fq & fkv
            return jnp.asarray(block_diagonal | offset_block_causal | block_causal)

        def _rope_tables(n):
            inv_freq = 1.0 / ROPE_BASE ** (np.arange(0, HD, 2, dtype=np.float32) / HD)
            freqs = np.outer(np.arange(n, dtype=np.float32), inv_freq)
            emb = np.concatenate([freqs, freqs], axis=-1)
            cos = jnp.asarray(np.cos(emb), jnp.float32)[None, :, None, :]
            sin = jnp.asarray(np.sin(emb), jnp.float32)[None, :, None, :]
            return (cos, sin)

        def _ln(x, w):
            xf = x.astype(jnp.float32)
            mu = jnp.mean(xf, axis=-1, keepdims=True)
            var = jnp.mean(jnp.square(xf - mu), axis=-1, keepdims=True)
            y = (xf - mu) * jax.lax.rsqrt(var + EPS)
            return y * w[None, None, :]

        def _apply_rope(t, cos, sin):
            t1, t2 = jnp.split(t, 2, axis=-1)
            rot = jnp.concatenate([-t2, t1], axis=-1)
            return t * cos + rot * sin

        def _attn(q, k, v, mask):
            scale = 1.0 / np.sqrt(HD)
            s = jnp.einsum('bqhd,bkhd->bhqk', q, k) * scale
            s = jnp.where(mask, s, jnp.finfo(s.dtype).min)
            a = jax.nn.softmax(s, axis=-1)
            return jnp.einsum('bhqk,bkhd->bqhd', a, v)
        key = jax.random.key(seed)
        ks = jax.random.split(key, 16)
        w = lambda k, shp: jax.random.normal(k, shp, jnp.float32) * 0.02
        inp = {'x': jax.random.normal(ks[0], (B, 2 * N, D), jnp.float32), 'cond_global': jax.random.normal(ks[1], (B, D), jnp.float32), 'cond_tokens': jax.random.normal(ks[2], (B, LC, D), jnp.float32), 'adaLN_W': w(ks[3], (D, 9 * D)), 'adaLN_b': w(ks[4], (9 * D,)), 'norm1_w': jnp.ones((D,), jnp.float32), 'qkv_W': w(ks[5], (D, 3 * D)), 'attn_out_W': w(ks[6], (D, D)), 'normc_w': jnp.ones((D,), jnp.float32), 'cq_W': w(ks[7], (D, D)), 'ck_W': w(ks[8], (D, D)), 'cv_W': w(ks[9], (D, D)), 'co_W': w(ks[10], (D, D)), 'norm2_w': jnp.ones((D,), jnp.float32), 'mlp_W1': w(ks[11], (D, 4 * D)), 'mlp_b1': w(ks[12], (4 * D,)), 'mlp_W2': w(ks[13], (4 * D, D)), 'mlp_b2': w(ks[14], (D,)), 'cond_kv_mask': jnp.ones((B, LC), bool), 'attn_mask': _block_diff_mask(N, BLOCK)}
        return inp
    _L0_xcond_all = _L0_xcond_setup()
    _L0_xcond_in = {k: v for k, v in _L0_xcond_all.items() if k in ('adaLN_W', 'adaLN_b', 'norm1_w', 'qkv_W', 'attn_out_W', 'normc_w', 'cq_W', 'ck_W', 'cv_W', 'co_W', 'norm2_w', 'mlp_W1', 'mlp_b1', 'mlp_W2', 'mlp_b2')}
    del _L0_xcond_all

    def _L1_xcond_setup():
        import jax, jax.numpy as jnp
        import numpy as np
        EPS = 1e-05

        def _ada_ln(x, c, W_ss, b_ss):
            mu = jnp.mean(x, axis=-1, keepdims=True)
            var = jnp.mean((x - mu) ** 2, axis=-1, keepdims=True)
            h = (x - mu) / jnp.sqrt(var + EPS)
            ss = jax.nn.silu(c) @ W_ss + b_ss
            scale, bias = jnp.split(ss, 2, axis=-1)
            return (1.0 + scale)[:, None, :] * h + bias[:, None, :]
        key = jax.random.key(seed)
        ks = jax.random.split(key, 12)
        B, Lq, Lkv, H = (8, 256, 64, 128)
        s = 0.02
        return {'x_q': jax.random.normal(ks[0], (B, Lq, H), jnp.float32), 'x_kv': jax.random.normal(ks[1], (B, Lkv, H), jnp.float32), 't_vec': jax.random.normal(ks[2], (B, H), jnp.float32), 'Wq': jax.random.normal(ks[3], (H, H), jnp.float32) * s, 'bq': jnp.zeros((H,), jnp.float32), 'Wkv': jax.random.normal(ks[4], (H, 2 * H), jnp.float32) * s, 'bkv': jnp.zeros((2 * H,), jnp.float32), 'Wp': jax.random.normal(ks[5], (H, H), jnp.float32) * s, 'bp': jnp.zeros((H,), jnp.float32), 'Wss_q': jax.random.normal(ks[6], (H, 2 * H), jnp.float32) * s, 'bss_q': jnp.zeros((2 * H,), jnp.float32), 'Wss_kv': jax.random.normal(ks[7], (H, 2 * H), jnp.float32) * s, 'bss_kv': jnp.zeros((2 * H,), jnp.float32)}
    _L1_xcond_all = _L1_xcond_setup()
    _L1_xcond_in = {k: v for k, v in _L1_xcond_all.items() if k in ('Wq', 'bq', 'Wkv', 'bkv', 'Wp', 'bp', 'Wss_q', 'bss_q', 'Wss_kv', 'bss_kv')}
    del _L1_xcond_all

    def _L2_xcond_setup():
        import jax, jax.numpy as jnp
        import numpy as np
        EPS = 1e-06
        H = 16

        def layer_norm(x, gamma=None, beta=None):
            x32 = x.astype(jnp.float32)
            mu = jnp.mean(x32, axis=-1, keepdims=True)
            var = jnp.var(x32, axis=-1, keepdims=True)
            y = (x32 - mu) * jax.lax.rsqrt(var + EPS)
            if gamma is not None:
                y = y * gamma + beta
            return y.astype(x.dtype)

        def mha(q, k, v):
            B, Nq, C = q.shape
            d = C // H
            qh = q.reshape(B, Nq, H, d)
            kh = k.reshape(B, k.shape[1], H, d)
            vh = v.reshape(B, v.shape[1], H, d)
            scores = jnp.einsum('bqhd,bkhd->bhqk', qh, kh) / jnp.sqrt(jnp.asarray(d, q.dtype))
            attn = jax.nn.softmax(scores, axis=-1)
            out = jnp.einsum('bhqk,bkhd->bqhd', attn, vh)
            return out.reshape(B, Nq, C)
        key = jax.random.key(seed)
        ks = jax.random.split(key, 24)
        B, N, C, M, Cc = (4, 256, 128, 128, 128)
        hid = 4 * C
        s = 0.02
        return {'x': jax.random.normal(ks[0], (B, N, C), jnp.float32), 'mod': jax.random.normal(ks[1], (B, C), jnp.float32), 'context': jax.random.normal(ks[2], (B, M, Cc), jnp.float32), 'ada_w': jax.random.normal(ks[3], (C, 6 * C), jnp.float32) * s, 'ada_b': jnp.zeros((6 * C,), jnp.float32), 'qkv_w': jax.random.normal(ks[4], (C, 3 * C), jnp.float32) * s, 'qkv_b': jnp.zeros((3 * C,), jnp.float32), 'self_o_w': jax.random.normal(ks[5], (C, C), jnp.float32) * s, 'self_o_b': jnp.zeros((C,), jnp.float32), 'norm2_g': jnp.ones((C,), jnp.float32), 'norm2_b': jnp.zeros((C,), jnp.float32), 'q_w': jax.random.normal(ks[6], (C, C), jnp.float32) * s, 'q_b': jnp.zeros((C,), jnp.float32), 'kv_w': jax.random.normal(ks[7], (Cc, 2 * C), jnp.float32) * s, 'kv_b': jnp.zeros((2 * C,), jnp.float32), 'cross_o_w': jax.random.normal(ks[8], (C, C), jnp.float32) * s, 'cross_o_b': jnp.zeros((C,), jnp.float32), 'mlp_w1': jax.random.normal(ks[9], (C, hid), jnp.float32) * s, 'mlp_b1': jnp.zeros((hid,), jnp.float32), 'mlp_w2': jax.random.normal(ks[10], (hid, C), jnp.float32) * s, 'mlp_b2': jnp.zeros((C,), jnp.float32)}
    _L2_xcond_all = _L2_xcond_setup()
    _L2_xcond_in = {k: v for k, v in _L2_xcond_all.items() if k in ('ada_w', 'ada_b', 'qkv_w', 'qkv_b', 'self_o_w', 'self_o_b', 'norm2_g', 'norm2_b', 'q_w', 'q_b', 'kv_w', 'kv_b', 'cross_o_w', 'cross_o_b', 'mlp_w1', 'mlp_b1', 'mlp_w2', 'mlp_b2')}
    del _L2_xcond_all

    def _L3_xcond_setup():
        import jax, jax.numpy as jnp
        import numpy as np
        H = 128
        RH = 2 * H
        E = 3
        B, T, P = (8, 256, 64)
        LN_EPS = 1e-05

        def _layer_norm(x, gamma, beta):
            mu = jnp.mean(x, axis=-1, keepdims=True)
            var = jnp.mean(jnp.square(x - mu), axis=-1, keepdims=True)
            return (x - mu) * jax.lax.rsqrt(var + LN_EPS) * gamma + beta
        key = jax.random.key(seed)
        ks = jax.random.split(key, 24)
        s = lambda fan_in: 1.0 / np.sqrt(fan_in)
        inp = {'mix_hidden_states': jax.random.normal(ks[0], (B, T, H), jnp.float32), 'global_anchor': jax.random.normal(ks[1], (B, H), jnp.float32), 'prototype_bank': jax.random.normal(ks[2], (B, P, H), jnp.float32), 'ln_gamma': jnp.ones((H,), jnp.float32), 'ln_beta': jnp.zeros((H,), jnp.float32), 'Wq': jax.random.normal(ks[3], (H, H), jnp.float32) * s(H), 'Wk': jax.random.normal(ks[4], (H, H), jnp.float32) * s(H), 'Wv': jax.random.normal(ks[5], (H, H), jnp.float32) * s(H), 'router_W': jax.random.normal(ks[6], (3 * H, E), jnp.float32) * s(3 * H), 'router_b': jnp.zeros((E,), jnp.float32), 'e_w1': jax.random.normal(ks[7], (E, 3 * H, RH), jnp.float32) * s(3 * H), 'e_b1': jnp.zeros((E, RH), jnp.float32), 'e_w2': jax.random.normal(ks[8], (E, RH, H), jnp.float32) * s(RH), 'e_b2': jnp.zeros((E, H), jnp.float32), 'gate_w1': jax.random.normal(ks[9], (3 * H, H), jnp.float32) * s(3 * H), 'gate_b1': jnp.zeros((H,), jnp.float32), 'gate_w2': jax.random.normal(ks[10], (H, H), jnp.float32) * s(H), 'gate_b2': jnp.zeros((H,), jnp.float32), 'out_w': jax.random.normal(ks[11], (H, H), jnp.float32) * s(H), 'out_b': jnp.zeros((H,), jnp.float32)}
        return inp
    _L3_xcond_all = _L3_xcond_setup()
    _L3_xcond_in = {k: v for k, v in _L3_xcond_all.items() if k in ('ln_gamma', 'ln_beta', 'Wq', 'Wk', 'Wv', 'router_W', 'router_b', 'e_w1', 'e_b1', 'e_w2', 'e_b2', 'gate_w1', 'gate_b1', 'gate_w2', 'gate_b2', 'out_w', 'out_b')}
    del _L3_xcond_all
    return {'x': x, 'cond_1024': cond_1024, 'ctx_1024': ctx_1024, 'mask_BxS2_bf1': mask_BxS2_bf1, 'mask_SxS_bk0': mask_SxS_bk0, 'L0_xcond_adaLN_W': _L0_xcond_in['adaLN_W'], 'L0_xcond_adaLN_b': _L0_xcond_in['adaLN_b'], 'L0_xcond_norm1_w': _L0_xcond_in['norm1_w'], 'L0_xcond_qkv_W': _L0_xcond_in['qkv_W'], 'L0_xcond_attn_out_W': _L0_xcond_in['attn_out_W'], 'L0_xcond_normc_w': _L0_xcond_in['normc_w'], 'L0_xcond_cq_W': _L0_xcond_in['cq_W'], 'L0_xcond_ck_W': _L0_xcond_in['ck_W'], 'L0_xcond_cv_W': _L0_xcond_in['cv_W'], 'L0_xcond_co_W': _L0_xcond_in['co_W'], 'L0_xcond_norm2_w': _L0_xcond_in['norm2_w'], 'L0_xcond_mlp_W1': _L0_xcond_in['mlp_W1'], 'L0_xcond_mlp_b1': _L0_xcond_in['mlp_b1'], 'L0_xcond_mlp_W2': _L0_xcond_in['mlp_W2'], 'L0_xcond_mlp_b2': _L0_xcond_in['mlp_b2'], 'L1_xcond_Wq': _L1_xcond_in['Wq'], 'L1_xcond_bq': _L1_xcond_in['bq'], 'L1_xcond_Wkv': _L1_xcond_in['Wkv'], 'L1_xcond_bkv': _L1_xcond_in['bkv'], 'L1_xcond_Wp': _L1_xcond_in['Wp'], 'L1_xcond_bp': _L1_xcond_in['bp'], 'L1_xcond_Wss_q': _L1_xcond_in['Wss_q'], 'L1_xcond_bss_q': _L1_xcond_in['bss_q'], 'L1_xcond_Wss_kv': _L1_xcond_in['Wss_kv'], 'L1_xcond_bss_kv': _L1_xcond_in['bss_kv'], 'L2_xcond_ada_w': _L2_xcond_in['ada_w'], 'L2_xcond_ada_b': _L2_xcond_in['ada_b'], 'L2_xcond_qkv_w': _L2_xcond_in['qkv_w'], 'L2_xcond_qkv_b': _L2_xcond_in['qkv_b'], 'L2_xcond_self_o_w': _L2_xcond_in['self_o_w'], 'L2_xcond_self_o_b': _L2_xcond_in['self_o_b'], 'L2_xcond_norm2_g': _L2_xcond_in['norm2_g'], 'L2_xcond_norm2_b': _L2_xcond_in['norm2_b'], 'L2_xcond_q_w': _L2_xcond_in['q_w'], 'L2_xcond_q_b': _L2_xcond_in['q_b'], 'L2_xcond_kv_w': _L2_xcond_in['kv_w'], 'L2_xcond_kv_b': _L2_xcond_in['kv_b'], 'L2_xcond_cross_o_w': _L2_xcond_in['cross_o_w'], 'L2_xcond_cross_o_b': _L2_xcond_in['cross_o_b'], 'L2_xcond_mlp_w1': _L2_xcond_in['mlp_w1'], 'L2_xcond_mlp_b1': _L2_xcond_in['mlp_b1'], 'L2_xcond_mlp_w2': _L2_xcond_in['mlp_w2'], 'L2_xcond_mlp_b2': _L2_xcond_in['mlp_b2'], 'L3_xcond_ln_gamma': _L3_xcond_in['ln_gamma'], 'L3_xcond_ln_beta': _L3_xcond_in['ln_beta'], 'L3_xcond_Wq': _L3_xcond_in['Wq'], 'L3_xcond_Wk': _L3_xcond_in['Wk'], 'L3_xcond_Wv': _L3_xcond_in['Wv'], 'L3_xcond_router_W': _L3_xcond_in['router_W'], 'L3_xcond_router_b': _L3_xcond_in['router_b'], 'L3_xcond_e_w1': _L3_xcond_in['e_w1'], 'L3_xcond_e_b1': _L3_xcond_in['e_b1'], 'L3_xcond_e_w2': _L3_xcond_in['e_w2'], 'L3_xcond_e_b2': _L3_xcond_in['e_b2'], 'L3_xcond_gate_w1': _L3_xcond_in['gate_w1'], 'L3_xcond_gate_b1': _L3_xcond_in['gate_b1'], 'L3_xcond_gate_w2': _L3_xcond_in['gate_w2'], 'L3_xcond_gate_b2': _L3_xcond_in['gate_b2'], 'L3_xcond_out_w': _L3_xcond_in['out_w'], 'L3_xcond_out_b': _L3_xcond_in['out_b']}

def reference(x, cond_1024, ctx_1024, mask_BxS2_bf1, mask_SxS_bk0, L0_xcond_adaLN_W, L0_xcond_adaLN_b, L0_xcond_norm1_w, L0_xcond_qkv_W, L0_xcond_attn_out_W, L0_xcond_normc_w, L0_xcond_cq_W, L0_xcond_ck_W, L0_xcond_cv_W, L0_xcond_co_W, L0_xcond_norm2_w, L0_xcond_mlp_W1, L0_xcond_mlp_b1, L0_xcond_mlp_W2, L0_xcond_mlp_b2, L1_xcond_Wq, L1_xcond_bq, L1_xcond_Wkv, L1_xcond_bkv, L1_xcond_Wp, L1_xcond_bp, L1_xcond_Wss_q, L1_xcond_bss_q, L1_xcond_Wss_kv, L1_xcond_bss_kv, L2_xcond_ada_w, L2_xcond_ada_b, L2_xcond_qkv_w, L2_xcond_qkv_b, L2_xcond_self_o_w, L2_xcond_self_o_b, L2_xcond_norm2_g, L2_xcond_norm2_b, L2_xcond_q_w, L2_xcond_q_b, L2_xcond_kv_w, L2_xcond_kv_b, L2_xcond_cross_o_w, L2_xcond_cross_o_b, L2_xcond_mlp_w1, L2_xcond_mlp_b1, L2_xcond_mlp_w2, L2_xcond_mlp_b2, L3_xcond_ln_gamma, L3_xcond_ln_beta, L3_xcond_Wq, L3_xcond_Wk, L3_xcond_Wv, L3_xcond_router_W, L3_xcond_router_b, L3_xcond_e_w1, L3_xcond_e_b1, L3_xcond_e_w2, L3_xcond_e_b2, L3_xcond_gate_w1, L3_xcond_gate_b1, L3_xcond_gate_w2, L3_xcond_gate_b2, L3_xcond_out_w, L3_xcond_out_b):
    import jax
    import jax.numpy as jnp

    def _L0_xcond_ref(x, cond_global, cond_tokens, adaLN_W, adaLN_b, norm1_w, qkv_W, attn_out_W, normc_w, cq_W, ck_W, cv_W, co_W, norm2_w, mlp_W1, mlp_b1, mlp_W2, mlp_b2, cond_kv_mask, attn_mask):
        import jax, jax.numpy as jnp
        import numpy as np
        B, N, D, H, LC = (2, 128, 128, 16, 77)
        HD = D // H
        BLOCK = 16
        ROPE_BASE = 10000.0
        EPS = 1e-05

        def _block_diff_mask(n, block_size):
            idx = np.arange(2 * n)
            q = idx[:, None]
            kv = idx[None, :]
            fq = q >= n
            fkv = kv >= n
            bq = np.where(fq, (q - n) // block_size, q // block_size)
            bkv = np.where(fkv, (kv - n) // block_size, kv // block_size)
            block_diagonal = (bq == bkv) & (fq == fkv)
            offset_block_causal = (bq > bkv) & fkv & ~fq
            block_causal = (bq >= bkv) & fq & fkv
            return jnp.asarray(block_diagonal | offset_block_causal | block_causal)

        def _rope_tables(n):
            inv_freq = 1.0 / ROPE_BASE ** (np.arange(0, HD, 2, dtype=np.float32) / HD)
            freqs = np.outer(np.arange(n, dtype=np.float32), inv_freq)
            emb = np.concatenate([freqs, freqs], axis=-1)
            cos = jnp.asarray(np.cos(emb), jnp.float32)[None, :, None, :]
            sin = jnp.asarray(np.sin(emb), jnp.float32)[None, :, None, :]
            return (cos, sin)

        def _ln(x, w):
            xf = x.astype(jnp.float32)
            mu = jnp.mean(xf, axis=-1, keepdims=True)
            var = jnp.mean(jnp.square(xf - mu), axis=-1, keepdims=True)
            y = (xf - mu) * jax.lax.rsqrt(var + EPS)
            return y * w[None, None, :]

        def _apply_rope(t, cos, sin):
            t1, t2 = jnp.split(t, 2, axis=-1)
            rot = jnp.concatenate([-t2, t1], axis=-1)
            return t * cos + rot * sin

        def _attn(q, k, v, mask):
            scale = 1.0 / np.sqrt(HD)
            s = jnp.einsum('bqhd,bkhd->bhqk', q, k) * scale
            s = jnp.where(mask, s, jnp.finfo(s.dtype).min)
            a = jax.nn.softmax(s, axis=-1)
            return jnp.einsum('bhqk,bkhd->bqhd', a, v)
        b, s, d = x.shape
        n = s // 2
        mod = (cond_global @ adaLN_W + adaLN_b)[:, None, :]
        sh_msa, sc_msa, g_msa, sh_x, sc_x, g_x, sh_mlp, sc_mlp, g_mlp = jnp.split(mod, 9, axis=-1)
        x_norm = _ln(x, norm1_w) * (1 + sc_msa) + sh_msa
        cos, sin = _rope_tables(n)

        def qkv(h):
            t = (h @ qkv_W).reshape(b, n, 3, H, HD)
            q, k, v = (t[:, :, 0], t[:, :, 1], t[:, :, 2])
            return (_apply_rope(q, cos, sin), _apply_rope(k, cos, sin), v)
        q1, k1, v1 = qkv(x_norm[:, :n])
        q2, k2, v2 = qkv(x_norm[:, n:])
        q = jnp.concatenate([q1, q2], axis=1)
        k = jnp.concatenate([k1, k2], axis=1)
        v = jnp.concatenate([v1, v2], axis=1)
        self_out = _attn(q, k, v, attn_mask[None, None]).reshape(b, s, d) @ attn_out_W
        x = x + g_msa * self_out
        xc = _ln(x, normc_w) * (1 + sc_x) + sh_x
        qc = (xc @ cq_W).reshape(b, s, H, HD)
        kc = (cond_tokens @ ck_W).reshape(b, LC, H, HD)
        vc = (cond_tokens @ cv_W).reshape(b, LC, H, HD)
        cross = _attn(qc, kc, vc, cond_kv_mask[:, None, None, :]).reshape(b, s, d) @ co_W
        x = x + g_x * cross
        xm = _ln(x, norm2_w) * (1 + sc_mlp) + sh_mlp
        h = jax.nn.gelu(xm @ mlp_W1 + mlp_b1, approximate=True)
        mlp_out = h @ mlp_W2 + mlp_b2
        return x + g_mlp * mlp_out

    def _L1_xcond_ref(x_q, x_kv, t_vec, Wq, bq, Wkv, bkv, Wp, bp, Wss_q, bss_q, Wss_kv, bss_kv):
        import jax, jax.numpy as jnp
        import numpy as np
        EPS = 1e-05

        def _ada_ln(x, c, W_ss, b_ss):
            mu = jnp.mean(x, axis=-1, keepdims=True)
            var = jnp.mean((x - mu) ** 2, axis=-1, keepdims=True)
            h = (x - mu) / jnp.sqrt(var + EPS)
            ss = jax.nn.silu(c) @ W_ss + b_ss
            scale, bias = jnp.split(ss, 2, axis=-1)
            return (1.0 + scale)[:, None, :] * h + bias[:, None, :]
        B, Lq, H = x_q.shape
        Lkv = x_kv.shape[1]
        nh = 16
        dh = H // nh
        xq = _ada_ln(x_q, t_vec, Wss_q, bss_q)
        xkv = _ada_ln(x_kv, t_vec, Wss_kv, bss_kv)
        q = (xq @ Wq + bq).reshape(B, Lq, nh, dh)
        kv = (xkv @ Wkv + bkv).reshape(B, Lkv, 2, nh, dh)
        k = kv[:, :, 0]
        v = kv[:, :, 1]
        scores = jnp.einsum('bqhd,bkhd->bhqk', q, k) / jnp.sqrt(jnp.float32(dh))
        attn = jax.nn.softmax(scores, axis=-1)
        out = jnp.einsum('bhqk,bkhd->bqhd', attn, v).reshape(B, Lq, H)
        return x_q + (out @ Wp + bp)

    def _L2_xcond_ref(x, mod, context, ada_w, ada_b, qkv_w, qkv_b, self_o_w, self_o_b, norm2_g, norm2_b, q_w, q_b, kv_w, kv_b, cross_o_w, cross_o_b, mlp_w1, mlp_b1, mlp_w2, mlp_b2):
        import jax, jax.numpy as jnp
        import numpy as np
        EPS = 1e-06
        H = 16

        def layer_norm(x, gamma=None, beta=None):
            x32 = x.astype(jnp.float32)
            mu = jnp.mean(x32, axis=-1, keepdims=True)
            var = jnp.var(x32, axis=-1, keepdims=True)
            y = (x32 - mu) * jax.lax.rsqrt(var + EPS)
            if gamma is not None:
                y = y * gamma + beta
            return y.astype(x.dtype)

        def mha(q, k, v):
            B, Nq, C = q.shape
            d = C // H
            qh = q.reshape(B, Nq, H, d)
            kh = k.reshape(B, k.shape[1], H, d)
            vh = v.reshape(B, v.shape[1], H, d)
            scores = jnp.einsum('bqhd,bkhd->bhqk', qh, kh) / jnp.sqrt(jnp.asarray(d, q.dtype))
            attn = jax.nn.softmax(scores, axis=-1)
            out = jnp.einsum('bhqk,bkhd->bqhd', attn, vh)
            return out.reshape(B, Nq, C)
        C = x.shape[-1]
        m = jax.nn.silu(mod) @ ada_w + ada_b
        shift_msa, scale_msa, gate_msa, shift_mlp, scale_mlp, gate_mlp = [c[:, None, :] for c in jnp.split(m, 6, axis=-1)]
        h = layer_norm(x)
        h = h * (1.0 + scale_msa) + shift_msa
        qkv = h @ qkv_w + qkv_b
        q, k, v = jnp.split(qkv, 3, axis=-1)
        h = mha(q, k, v) @ self_o_w + self_o_b
        x = x + h * gate_msa
        h = layer_norm(x, norm2_g, norm2_b)
        q = h @ q_w + q_b
        kv = context @ kv_w + kv_b
        k, v = jnp.split(kv, 2, axis=-1)
        h = mha(q, k, v) @ cross_o_w + cross_o_b
        x = x + h
        h = layer_norm(x)
        h = h * (1.0 + scale_mlp) + shift_mlp
        h = jax.nn.gelu(h @ mlp_w1 + mlp_b1) @ mlp_w2 + mlp_b2
        x = x + h * gate_mlp
        return x

    def _L3_xcond_ref(mix_hidden_states, global_anchor, prototype_bank, ln_gamma, ln_beta, Wq, Wk, Wv, router_W, router_b, e_w1, e_b1, e_w2, e_b2, gate_w1, gate_b1, gate_w2, gate_b2, out_w, out_b):
        import jax, jax.numpy as jnp
        import numpy as np
        H = 128
        RH = 2 * H
        E = 3
        B, T, P = (8, 256, 64)
        LN_EPS = 1e-05

        def _layer_norm(x, gamma, beta):
            mu = jnp.mean(x, axis=-1, keepdims=True)
            var = jnp.mean(jnp.square(x - mu), axis=-1, keepdims=True)
            return (x - mu) * jax.lax.rsqrt(var + LN_EPS) * gamma + beta
        x = mix_hidden_states
        nx = _layer_norm(x, ln_gamma, ln_beta)
        q = nx @ Wq
        k = prototype_bank @ Wk
        v = prototype_bank @ Wv
        scores = jnp.einsum('bth,bph->btp', q, k) * H ** (-0.5)
        weights = jax.nn.softmax(scores, axis=-1)
        evidence = jnp.einsum('btp,bph->bth', weights, v)
        anchor = jnp.broadcast_to(global_anchor[:, None, :], nx.shape)
        combined = jnp.concatenate([nx, evidence, anchor], axis=-1)
        router_logits = combined @ router_W + router_b
        router_probs = jax.nn.softmax(router_logits, axis=-1)
        h = jax.nn.silu(jnp.einsum('btc,ecr->bter', combined, e_w1) + e_b1)
        expert_out = jnp.einsum('bter,erh->bteh', h, e_w2) + e_b2
        routed = jnp.sum(expert_out * router_probs[..., None], axis=-2)
        g = jax.nn.sigmoid(jax.nn.silu(combined @ gate_w1 + gate_b1) @ gate_w2 + gate_b2)
        refined_delta = g * (routed @ out_w + out_b)
        return x + refined_delta
    x = _L0_xcond_ref(x, cond_1024, ctx_1024, L0_xcond_adaLN_W, L0_xcond_adaLN_b, L0_xcond_norm1_w, L0_xcond_qkv_W, L0_xcond_attn_out_W, L0_xcond_normc_w, L0_xcond_cq_W, L0_xcond_ck_W, L0_xcond_cv_W, L0_xcond_co_W, L0_xcond_norm2_w, L0_xcond_mlp_W1, L0_xcond_mlp_b1, L0_xcond_mlp_W2, L0_xcond_mlp_b2, mask_BxS2_bf1, mask_SxS_bk0)
    x = _L1_xcond_ref(x, ctx_1024, cond_1024, L1_xcond_Wq, L1_xcond_bq, L1_xcond_Wkv, L1_xcond_bkv, L1_xcond_Wp, L1_xcond_bp, L1_xcond_Wss_q, L1_xcond_bss_q, L1_xcond_Wss_kv, L1_xcond_bss_kv)
    x = _L2_xcond_ref(x, cond_1024, ctx_1024, L2_xcond_ada_w, L2_xcond_ada_b, L2_xcond_qkv_w, L2_xcond_qkv_b, L2_xcond_self_o_w, L2_xcond_self_o_b, L2_xcond_norm2_g, L2_xcond_norm2_b, L2_xcond_q_w, L2_xcond_q_b, L2_xcond_kv_w, L2_xcond_kv_b, L2_xcond_cross_o_w, L2_xcond_cross_o_b, L2_xcond_mlp_w1, L2_xcond_mlp_b1, L2_xcond_mlp_w2, L2_xcond_mlp_b2)
    x = _L3_xcond_ref(x, cond_1024, ctx_1024, L3_xcond_ln_gamma, L3_xcond_ln_beta, L3_xcond_Wq, L3_xcond_Wk, L3_xcond_Wv, L3_xcond_router_W, L3_xcond_router_b, L3_xcond_e_w1, L3_xcond_e_b1, L3_xcond_e_w2, L3_xcond_e_b2, L3_xcond_gate_w1, L3_xcond_gate_b1, L3_xcond_gate_w2, L3_xcond_gate_b2, L3_xcond_out_w, L3_xcond_out_b)
    return x

_drawn_inputs = setup_inputs


def setup_inputs(seed=0):
    import zlib

    import numpy as np

    out = dict(_drawn_inputs(seed))
    spreads = {'L0_xcond_norm1_w': (1.0, 0.6),
     'L0_xcond_normc_w': (1.0, 0.6),
     'L0_xcond_norm2_w': (1.0, 0.6),
     'L1_xcond_bq': (0.0, 2.0),
     'L1_xcond_bkv': (0.0, 1.401),
     'L1_xcond_bp': (0.0, 0.322),
     'L1_xcond_bss_q': (0.0, 2.0),
     'L1_xcond_bss_kv': (0.0, 2.0),
     'L2_xcond_ada_b': (0.0, 0.58),
     'L2_xcond_qkv_b': (0.0, 0.8),
     'L2_xcond_self_o_b': (0.0, 0.508),
     'L2_xcond_norm2_g': (1.0, 0.6),
     'L2_xcond_norm2_b': (0.0, 2.0),
     'L2_xcond_q_b': (0.0, 2.0),
     'L2_xcond_kv_b': (0.0, 2.0),
     'L2_xcond_cross_o_b': (0.0, 0.388),
     'L2_xcond_mlp_b1': (0.0, 0.8),
     'L2_xcond_mlp_b2': (0.0, 0.551),
     'L3_xcond_ln_gamma': (1.0, 0.6),
     'L3_xcond_ln_beta': (0.0, 2.0),
     'L3_xcond_router_b': (0.0, 2.0),
     'L3_xcond_e_b1': (0.0, 1.6),
     'L3_xcond_e_b2': (0.0, 0.8),
     'L3_xcond_gate_b1': (0.0, 2.0),
     'L3_xcond_gate_b2': (0.0, 2.0),
     'L3_xcond_out_b': (0.0, 0.731)}
    factors = {'L0_xcond_adaLN_W': 3.22,
     'L0_xcond_adaLN_b': 8.0,
     'L0_xcond_qkv_W': 6.159,
     'L0_xcond_attn_out_W': 6.103,
     'L0_xcond_cq_W': 8.0,
     'L0_xcond_ck_W': 8.0,
     'L0_xcond_cv_W': 8.0,
     'L0_xcond_co_W': 8.0,
     'L0_xcond_mlp_W1': 4.371,
     'L0_xcond_mlp_b1': 8.0,
     'L0_xcond_mlp_W2': 4.236,
     'L0_xcond_mlp_b2': 8.0,
     'L1_xcond_Wq': 64.0,
     'L1_xcond_Wss_q': 64.0,
     'L1_xcond_Wss_kv': 26.159,
     'L2_xcond_ada_w': 2.79,
     'L2_xcond_qkv_w': 8.0,
     'L2_xcond_self_o_w': 8.0,
     'L2_xcond_q_w': 64.0,
     'L2_xcond_mlp_w1': 6.222,
     'L2_xcond_mlp_w2': 5.686,
     'L1_xcond_Wkv': 2.96,
     'L2_xcond_kv_w': 8.0,
     'L2_xcond_cross_o_w': 3.541,
     'L3_xcond_Wq': 5.321,
     'L3_xcond_Wk': 5.213,
     'L3_xcond_Wv': 2.932,
     'L3_xcond_gate_w1': 4.822,
     'L3_xcond_gate_w2': 3.635}
    for name, (base, spread) in spreads.items():
        noise = np.random.default_rng([zlib.crc32(name.encode()), seed]).standard_normal(out[name].shape)
        drawn = base * np.exp(spread * noise) if base else spread * noise
        out[name] = jnp.asarray(drawn.astype(out[name].dtype))
    for name, factor in factors.items():
        out[name] = (out[name] * factor).astype(out[name].dtype)
    return out
```

```python
from contextlib import ExitStack

import numpy as np

import concourse.bass as bass
from concourse import mybir

F32 = mybir.dt.float32
BF16 = mybir.dt.bfloat16
U8 = mybir.dt.uint8
ACT = mybir.ActivationFunctionType
ALU = mybir.AluOpType
AX = mybir.AxisListType.X

B, T, D, C = 16, 128, 128, 77
H, HD = 16, 8
GB = 4
NS = 2
ITERS = B // (GB * NS)
N = GB * T
NC = GB * C
HALF = T // 2
BIG = 2.0 ** 100

W_PARTS = [("ada0", 9), ("ssq", 2), ("sskv", 2), ("ada2", 6), ("qkv0", 3), ("ao0", 1), ("cq0", 1), ("ck0", 1), ("cv0", 1), ("co0", 1), ("m10", 4),
           ("m20", 4), ("wq1", 1), ("wkv1", 2), ("wp1", 1), ("qkv2", 3),
           ("so2", 1), ("q2", 1), ("kv2", 2), ("co2", 1), ("m12", 4), ("m22", 4), ("q3", 1), ("k3", 1),
           ("v3", 1), ("e1", 18), ("e2", 6), ("g1", 3), ("g2", 1), ("ow3", 1)]
W_AT, _n = {}, 0
for _name, _k in W_PARTS:
    W_AT[_name] = _n
    _n += _k
NW = _n

C_PARTS = [("modb", 21), ("n1", 1), ("nc", 1), ("n2", 1), ("g2", 1), ("b2", 1), ("gam", 1), ("bet", 1),
           ("bq1", 1), ("bk1", 1), ("bv1", 1), ("qb2", 1), ("kb2", 1), ("vb2", 1), ("cq2", 1), ("ck2", 1),
           ("cv2", 1), ("m10", 4), ("m12", 4), ("hmask", 16)]
C_AT, _n = {}, 0
for _name, _k in C_PARTS:
    C_AT[_name] = _n
    _n += _k
NCOL = _n

T_ANCHOR, T_COND, NT = 18, 25, 26
MODS = ([(W_AT["ada0"] + c, 0) for c in (0, 1, 3, 4, 6, 7)] + [(W_AT["ssq"] + c, 1) for c in (0, 1)]
        + [(W_AT["sskv"] + c, 1) for c in (0, 1)] + [(W_AT["ada2"] + c, 1) for c in (0, 1, 3, 4)]
        + [(W_AT["e1"] + 6 * e + 4 + r, 0) for e in range(3) for r in range(2)] + [(W_AT["g1"] + 2, 0)])
NORMS = [(0, 1, "n1"), (2, 3, "nc"), (4, 5, "n2"), (7, 6, None), (9, 8, None), (10, 11, None), None,
         (12, 13, None), None]
GATES = [(W_AT["ada0"] + 2, 0), (W_AT["ada0"] + 5, 0), (W_AT["ada0"] + 8, 0), (W_AT["ada2"] + 2, 1),
         (W_AT["ada2"] + 5, 1)]
NG = len(GATES)
R_M0, R_P1, R_S2, R_C2, R_M2, R_OUT, R_GATE, R_E = 0, 1, 2, 3, 4, 5, 6, 7
NR = 10

STAGES = ["l0", "p0", "a0", "o0", "l1", "p1", "a1", "o1", "l2", "m0", "l3", "l4", "p2", "a2", "o2",
          "l5", "p3", "a3", "o3", "l6", "p4", "a4", "o4", "l7", "m1", "l8", "x3"]
NLN, NAT = 9, 5
ATT = [dict(kw=T, q="qkv0", k=1, v=2, bq=None, bk=None, o="ao0", row=None, gate=0),
       dict(kw=C, q="cq0", k="ck0", v="cv0", bq=None, bk=None, o="co0", row=None, gate=1),
       dict(kw=C, q="wq1", k="wkv1", v=None, bq="bq1", bk="bk1", o="wp1", row=R_P1, gate=None),
       dict(kw=T, q="qkv2", k=1, v=2, bq="qb2", bk="kb2", o="so2", row=R_S2, gate=3),
       dict(kw=C, q="q2", k="kv2", v=None, bq="cq2", bk="ck2", o="co2", row=R_C2, gate=None)]
KBLK = [W_AT["qkv0"] + 1, W_AT["ck0"], W_AT["wkv1"], W_AT["qkv2"] + 1, W_AT["kv2"]]
VBLK = [W_AT["qkv0"] + 2, W_AT["cv0"], W_AT["wkv1"] + 1, W_AT["qkv2"] + 2, W_AT["kv2"] + 1]


def bank_jobs(stage):
    if stage[0] == "l":
        return ["t"]
    if stage == "p0":
        return ["qa", "qb", "ka", "kb", "v"]
    if stage[0] == "p":
        return ["q", "k", "v"]
    if stage[0] == "o":
        return ["y"]
    if stage[0] == "m":
        return ["h0", "h1", "h2", "h3", "y"]
    if stage == "x3":
        return (["q", "k", "v", "s", "pt", "ev", "lg", "lt"] + [f"h{c}" for c in range(7)]
                + ["e0", "e1", "e2", "rt", "g", "y"])
    return []


LIN_AT, _n = {}, 0
for _st in STAGES:
    for _s in range(NS):
        for _job in bank_jobs(_st):
            LIN_AT[(_st, _s, _job)] = _n
            _n += 1
LIN_JOBS = _n
assert LIN_JOBS % 2 == 0


def lin_bank(st, s, job):
    return LIN_AT[(st, s, job)] % 2


def lin_turn(it, st, s, job):
    return it * (LIN_JOBS // 2) + LIN_AT[(st, s, job)] // 2 + 1


def nth(it, k, s, kinds, b=0, per=1):
    return it * (kinds * NS * per) + (k * NS + s) * per + b + 1


def build(nc, x_in, ctx_in, ctxT_in, condT_in, w_in, col_in, row_in, rw_in, rb_in, gb_in, mqk_in, mkq_in,
          mc_in, cos_in, sin_in, ident_in, ind_in, onesp_in, out):
    ctx = ExitStack()
    with ctx:
        def sb(name, shape, dt=F32):
            return ctx.enter_context(nc.sbuf_tensor(name, shape, dt))

        def ps(name, shape, dt=F32):
            return ctx.enter_context(nc.psum_tensor(name, shape, dt))

        def sem(name):
            return ctx.enter_context(nc.semaphore(name))

        lin = ps("lin", [128, 2, 512])
        sco = ps("sco", [128, 2, 512])
        sct = ps("sct", [128, 2, 512])
        avp = ps("avp", [128, 512])
        mtp = ps("mtp", [128, 1024], BF16)

        W = sb("W", [128, NW, 128])
        Wrot = sb("Wrot", [128, 2, 128])
        col = sb("col", [128, NCOL])
        row = sb("row", [1, NR, 128])
        rw = sb("rw", [128, 3, 3])
        rb = sb("rb", [3, 1])
        condT = sb("condT", [128, B])
        scondT = sb("scondT", [128, B])
        modv = sb("modv", [128, 21, B])
        tab = sb("tab", [128, NT, B])
        cosT = sb("cosT", [128, T])
        sinT = sb("sinT", [128, T])
        ident = sb("ident", [128, 128])
        identb = sb("identb", [128, 128], BF16)
        onef = sb("onef", [1, 128])
        oneb = sb("oneb", [1, 512], BF16)
        ind48 = sb("ind48", [48, H])
        indb = sb("indb", [48, H, 128], BF16)
        onesp = sb("onesp", [128, 4, 32])
        mqk8 = sb("mqk8", [128, T], U8)
        mkq8 = sb("mkq8", [128, T], U8)
        mc8 = sb("mc8", [1, B * C], U8)
        mqk = sb("mqk", [128, T], BF16)
        mkq = sb("mkq", [128, T], BF16)
        mcb = sb("mcb", [1, B * C], BF16)
        mhalf = sb("mhalf", [128, GB])

        xs, ctxs, ctxT, gbc, tabg, mcg = [], [], [], [], [], []
        mv, bst, rstd, xn, hT, qT, qb, kT, t1, Vp, oT, hid = [], [], [], [], [], [], [], [], [], [], [], []
        for s in range(NS):
            xs.append(sb(f"x{s}", [128, GB, D]))
            ctxs.append(sb(f"ctx{s}", [C, GB, D]))
            ctxT.append(sb(f"ctxT{s}", [128, GB, C]))
            gbc.append(sb(f"gbc{s}", [128, GB, NG * 128]))
            tabg.append(sb(f"tabg{s}", [128, NT, GB]))
            mcg.append(sb(f"mcg{s}", [1, GB, C], BF16))
            mv.append(sb(f"mv{s}", [128, GB, 2]))
            bst.append(sb(f"bst{s}", [128, GB, 6]))
            rstd.append(sb(f"rstd{s}", [128, 2, GB]))
            xn.append(sb(f"xn{s}", [128, GB, D]))
            hT.append(sb(f"hT{s}", [128, N]))
            qT.append(sb(f"qT{s}", [128, N]))
            qb.append(sb(f"qb{s}", [128, N], BF16))
            kT.append(sb(f"kT{s}", [128, N]))
            Vp.append(sb(f"Vp{s}", [128, GB, H, 32]))
            oT.append(sb(f"oT{s}", [128, N]))
            hid.append(sb(f"hid{s}", [128, 7, N]))
            t1.append(hid[s][:, 0:4, :])
        mx3 = [sb(f"mx3{s}", [128, 4, GB]) for s in range(NS)]
        pr3 = [sb(f"pr3{s}", [128, 3, GB, 3]) for s in range(NS)]
        lgT = [sb(f"lgT{s}", [3, N]) for s in range(NS)]

        kbd = sb("kbd", [128, 2, H, 128])
        kbb = sb("kbb", [128, 2, H, 128], BF16)
        P1 = sb("P1", [128, H, T])
        P = [W[:, 0:H, :], P1[:]]
        gbrow, grow = (P1[0:B, i * NG:(i + 1) * NG, :].rearrange("p g d -> p (g d)") for i in range(2))
        mx = sb("mx", [128, H])
        mhl = sb("mhl", [128, 48], BF16)
        mT = sb("mT", [48, T], BF16)
        rden = sb("rden", [128, T])

        gdram = nc.dram_tensor("gate_rows", (B, NG * 128), F32, kind="Internal").ap()

        loaded = sem("loaded")
        gate_rows_out = sem("gate_rows_out")
        x_in_s = [sem(f"x_loaded{s}") for s in range(NS)]
        g_in_s = [sem(f"gates_loaded{s}") for s in range(NS)]
        stored = [sem(f"stored{s}") for s in range(NS)]
        zeroed = sem("zeroed")
        silu_done = sem("silu_done")
        mods_done, modv_done, tab_done = sem("mods_done"), sem("modv_done"), sem("tab_done")
        gates_mm, grow_done = sem("gates_mm"), sem("grow_done")
        setup_dve = sem("setup_dve")
        bias_mm = sem("bias_mm")
        group_tab = sem("group_tab")
        lin_full = [sem(f"lin_full{i}") for i in range(2)]
        lin_free = [sem(f"lin_free{i}") for i in range(2)]
        ln_bn, ln_stats, ln_eps, ln_rstd, ln_xn = (sem(n) for n in ("ln_bn", "ln_stats", "ln_eps", "ln_rstd", "ln_xn"))
        rope_parts, rope_q, rope_k, qb_ready = (sem(n) for n in ("rope_parts", "rope_q", "rope_k", "qb_ready"))
        kbd_ready, kbb_ready = sem("kbd_ready"), sem("kbb_ready")
        s_full, s_free, m_ready, mhi_ready, m_split, mt_full, mt_ready = (sem(n) for n in (
            "s_full", "s_free", "m_ready", "mhi_ready", "m_split", "mt_full", "mt_ready"))
        st_full, st_free, av_full, rden_ready, av_free = (sem(n) for n in (
            "st_full", "st_free", "av_full", "rden_ready", "av_free"))
        x_ready = sem("x_ready")
        x3_max, x3_neg, x3_sum, x3_rec, x3_p = (sem(n) for n in ("x3_max", "x3_neg", "x3_sum", "x3_rec", "x3_p"))
        r3_max, r3_exp, r3_sum, r3_rec, r3_p = (sem(n) for n in ("r3_max", "r3_exp", "r3_sum", "r3_rec", "r3_p"))

        NCONST = 18
        GATED = ["o0", "o1", "m0", "o3", "m1", "x3"]
        gate_of = {"o0": 0, "o1": 1, "m0": 2, "o3": 3, "m1": 4}

        def wblk(name, k=0, n=1):
            a = W_AT[name] + k
            return W[:, a, :] if n == 1 else W[:, a:a + n, :]

        def c_(name, k=0):
            a = C_AT[name] + k
            return col[:, a:a + 1]

        def hold(eng):
            eng.nop(nofuse=True)

        def lin_ready(eng, it, st, s, job):
            eng.wait_ge(lin_full[lin_bank(st, s, job)], lin_turn(it, st, s, job))

        def lin_taken(eng, it, st, s, job):
            eng.wait_ge(lin_free[lin_bank(st, s, job)], lin_turn(it, st, s, job) + 1)
            hold(eng)

        def lin_ap(st, s, job, p=128):
            return lin[0:p, lin_bank(st, s, job), :]

        def diag(s, kw):
            v = Vp[s][0:kw]
            return bass.AP(tensor=v.tensor, offset=v.offset, ap=[list(v.ap[0]), [128, 16], [40, 4], [1, 8]])

        def res_ready(eng, it, st, s):
            before = {"l0": None, "l1": "o0", "l2": "o1", "l3": "m0", "l5": "o2", "l6": "o3", "l7": "o4", "l8": "m1"}[st]
            if before in GATED:
                eng.wait_ge(x_ready, nth(it, GATED.index(before), s, len(GATED)))
            elif before:
                lin_taken(eng, it, before, s, "y")

        block = ctx.enter_context(nc.Block())

        @block.sync
        def _(sp):
            for dst, src in ((condT, condT_in), (ident, ident_in), (col, col_in), (row, row_in), (rw, rw_in),
                             (rb, rb_in), (gbrow, gb_in), (cosT, cos_in), (sinT, sin_in), (ind48, ind_in),
                             (onesp, onesp_in), (mqk8, mqk_in), (mkq8, mkq_in), (mc8, mc_in)):
                sp.dma_start(dst if dst is gbrow else dst[:], src).then_inc(loaded, 16)
            for i in range(4):
                a, b = NW * i // 4, NW * (i + 1) // 4
                sp.dma_start(W[:, a:b, :], w_in[:, a:b, :]).then_inc(loaded, 16)
            sp.wait_ge(grow_done, 1)
            sp.dma_start(gdram, grow).then_inc(gate_rows_out, 16)
            sp.wait_ge(gate_rows_out, 16)
            with sp.Fori(0, ITERS) as it:
                for s in range(NS):
                    base = it * (NS * GB) + s * GB
                    sp.dma_start(xs[s][:], x_in[:, bass.ds(base, GB), :]).then_inc(x_in_s[s], 16)
                    sp.dma_start(ctxs[s][:], ctx_in[:, bass.ds(base, GB), :]).then_inc(x_in_s[s], 16)
                    sp.dma_start(ctxT[s][:], ctxT_in[:, bass.ds(base, GB), :]).then_inc(x_in_s[s], 16)
                    gsrc = gdram[bass.ds(base, GB), :]
                    sp.dma_start(gbc[s][:], gsrc.partition_broadcast(128)).then_inc(g_in_s[s], 16)
                for s in range(NS):
                    sp.wait_ge(x_ready, nth(it, GATED.index("x3"), s, len(GATED)))
                    hold(sp)
                    base = it * (NS * GB) + s * GB
                    sp.dma_start(out[:, bass.ds(base, GB), :], xs[s][:]).then_inc(stored[s], 16)
                for s in range(NS):
                    sp.wait_ge(stored[s], it * 16 + 16)
                    hold(sp)

        @block.gpsimd
        def _(pool):
            nc.gpsimd.memset(mhalf[:], -0.5).then_inc(zeroed, 1)
            for s in range(NS):
                nc.gpsimd.memset(Vp[s][:], 0.0).then_inc(zeroed, 1)
            pool.wait_ge(loaded, 16 * NCONST)
            pool.wait_ge(zeroed, 1 + NS)
            hm = col[:, C_AT["hmask"]:C_AT["hmask"] + H].unsqueeze(2)

            def norm(it, k, s):
                t = C if k == 4 else 128
                eps = 1e-6 if k in (5, 6, 7) else 1e-5
                pool.wait_ge(ln_stats, nth(it, k, s, NLN))
                hold(pool)
                nc.gpsimd.tensor_scalar(rstd[s][0:t, 0, :], mv[s][0:t, :, 1], eps, None, ALU.add).then_inc(ln_eps, 1)
                pool.wait_ge(ln_eps, nth(it, k, s, NLN))
                nc.gpsimd.tensor_tensor(rstd[s][0:t, 1, :], rstd[s][0:t, 0, :], mhalf[0:t, :],
                                        ALU.pow).then_inc(ln_rstd, 1)

            def attention(it, a, s):
                kw = ATT[a]["kw"]
                st = f"p{a}"
                if a == 0:
                    pool.wait_ge(rope_k, nth(it, 0, s, 1))
                else:
                    lin_taken(pool, it, st, s, "k")
                for b in range(GB):
                    j = (a * NS + s) * GB + b
                    if j >= 2:
                        pool.wait_ge(st_full, it * (NAT * NS * GB * 4) + 4 * (j - 1))
                    k = kT[s][:, b * kw:(b + 1) * kw].unsqueeze(1)
                    nc.gpsimd.tensor_tensor(kbd[:, j % 2, :, 0:kw], k.broadcast_to([128, H, kw]),
                                            hm.broadcast_to([128, H, kw]), ALU.mult).then_inc(kbd_ready, 1)

            with pool.Fori(0, ITERS) as it:
                for st in STAGES:
                    for s in range(NS):
                        if st[0] == "l":
                            norm(it, int(st[1:]), s)
                        elif st[0] == "a":
                            attention(it, int(st[1:]), s)

        @block.scalar
        def _(act):
            act.wait_ge(loaded, 16 * NCONST)
            nc.scalar.activation(scondT[:], condT[:], ACT.Silu).then_inc(silu_done, 1)

            def copy_out(it, st, s, job, dst, src, bias=None):
                lin_ready(act, it, st, s, job)
                kw = {} if bias is None else {"bias": bias}
                nc.scalar.activation(dst, src, ACT.Identity, **kw).then_inc(lin_free[lin_bank(st, s, job)], 1)

            def norm(it, k, s):
                st, t = f"l{k}", (C if k == 4 else 128)
                lin_ready(act, it, st, s, "t")
                src = lin_ap(st, s, "t")
                dst = hid[s][:, 5, :] if k == 4 else hT[s][:]
                for b in range(GB):
                    i = nc.scalar.activation(dst[:, b * t:(b + 1) * t], src[:, b * t:(b + 1) * t], ACT.Identity,
                                             bias=tabg[s][:, 2 * k + 1, b:b + 1], scale=tabg[s][:, 2 * k, b:b + 1])
                i.then_inc(lin_free[lin_bank(st, s, "t")], 1)

            def project(it, a, s):
                A, st = ATT[a], f"p{a}"
                n = GB * A["kw"]
                if a > 0:
                    copy_out(it, st, s, "q", qT[s][:], lin_ap(st, s, "q"), c_(A["bq"]) if A["bq"] else None)
                    copy_out(it, st, s, "k", kT[s][:, 0:n], lin_ap(st, s, "k")[:, 0:n], c_(A["bk"]) if A["bk"] else None)

            def attention(it, a, s):
                kw = ATT[a]["kw"]

                def narrow(b):
                    j = (a * NS + s) * GB + b
                    act.wait_ge(kbd_ready, nth(it, a, s, NAT, b, GB))
                    nc.scalar.activation(kbb[:, j % 2, :, 0:kw], kbd[:, j % 2, :, 0:kw],
                                         ACT.Identity).then_inc(kbb_ready, 1)

                narrow(0)
                for b in range(GB):
                    if b + 1 < GB:
                        narrow(b + 1)
                    j = (a * NS + s) * GB + b
                    for g in range(4):
                        act.wait_ge(st_full, nth(it, a, s, NAT, 4 * b + g, GB * 4))
                        nc.scalar.activation(P[j % 2][0:kw, 4 * g:4 * g + 4, :],
                                             sct[0:kw, g % 2, :].rearrange("p (h q) -> p h q", h=4),
                                             ACT.Exp, scale=float(HD) ** -0.5).then_inc(st_free, 1)

            def mlp(it, k, s):
                st = f"m{k}"
                for c in range(4):
                    lin_ready(act, it, st, s, f"h{c}")
                    nc.scalar.activation(hid[s][:, c, :], lin_ap(st, s, f"h{c}"), ACT.Gelu_apprx_tanh,
                                         bias=c_("m10" if k == 0 else "m12", c)).then_inc(
                                             lin_free[lin_bank(st, s, f"h{c}")], 1)

            def mixture(it, s):
                st = "x3"
                copy_out(it, st, s, "k", kT[s][:, 0:NC], lin_ap(st, s, "k")[:, 0:NC])
                act.wait_ge(x3_neg, nth(it, 0, s, 1))
                lin_ready(act, it, st, s, "s")
                for b in range(GB):
                    i = nc.scalar.activation(xn[s][:, b, 0:C], lin_ap(st, s, "s")[:, b * C:(b + 1) * C], ACT.Exp,
                                             bias=mx3[s][:, 1, b:b + 1], scale=float(D) ** -0.5)
                i.then_inc(lin_free[lin_bank(st, s, "s")], 1)
                copy_out(it, st, s, "ev", kT[s][:], lin_ap(st, s, "ev"))
                copy_out(it, st, s, "lg", lgT[s][:], lin_ap(st, s, "lg", 3), rb[:])
                lin_taken(act, it, st, s, "lt")
                nc.scalar.activation(pr3[s][:, 1], pr3[s][:, 0], ACT.Exp).then_inc(r3_exp, 1)
                for c in range(7):
                    job = f"h{c}"
                    lin_ready(act, it, st, s, job)
                    for b in range(GB):
                        i = nc.scalar.activation(hid[s][:, c, b * T:(b + 1) * T], lin_ap(st, s, job)[:, b * T:(b + 1) * T],
                                                 ACT.Silu, bias=tabg[s][:, T_ANCHOR + c, b:b + 1])
                    i.then_inc(lin_free[lin_bank(st, s, job)], 1)
                copy_out(it, st, s, "rt", oT[s][:], lin_ap(st, s, "rt"))
                lin_ready(act, it, st, s, "g")
                nc.scalar.activation(hid[s][:, 5, :], lin_ap(st, s, "g"), ACT.Sigmoid).then_inc(
                    lin_free[lin_bank(st, s, "g")], 1)

            with act.Fori(0, ITERS) as it:
                for st in STAGES:
                    for s in range(NS):
                        k = int(st[1:])
                        if st == "l0":
                            act.wait_ge(group_tab, nth(it, 0, s, 1))
                        if st[0] == "l":
                            norm(it, k, s)
                        elif st[0] == "p":
                            project(it, k, s)
                        elif st[0] == "a":
                            attention(it, k, s)
                        elif st[0] == "m":
                            mlp(it, k, s)
                        elif st == "x3":
                            mixture(it, s)

        @block.vector
        def _(dve):
            v = nc.vector
            n_setup = [0]

            def chain(i):
                n_setup[0] += 1
                i.then_inc(setup_dve, 1)
                dve.wait_ge(setup_dve, n_setup[0])

            v.memset(onef[:], 1.0).then_inc(lin_free[0], 1)
            v.memset(rden[:], 0.0).then_inc(lin_free[1], 1)
            v.memset(oneb[:], 1.0).then_inc(s_free, 2)
            v.memset(mhl[:], 0.0).then_inc(st_free, 2)
            chain(v.memset(mx[:], 0.0))
            v.memset(mT[:], 0.0).then_inc(av_free, 1)
            dve.wait_ge(loaded, 16 * NCONST)
            v.tensor_copy(identb[:], ident[:])
            v.tensor_copy(indb[:], ind48[:].unsqueeze(2).broadcast_to([48, H, 128]))
            for dst, src in ((mqk, mqk8), (mkq, mkq8), (mcb, mc8)):
                v.tensor_scalar(dst[:], src[:], -1.0, BIG, ALU.add, ALU.mult)
            for i in range(2):
                wv = wblk("qkv0", i).rearrange("p (h t j) -> p h t j", t=2, j=4)
                rv = Wrot[:, i, :].rearrange("p (h t j) -> p h t j", t=2, j=4)
                v.tensor_scalar(rv[:, :, 0, :], wv[:, :, 1, :], -1.0, None, ALU.mult)
                i_ = v.tensor_copy(rv[:, :, 1, :], wv[:, :, 0, :])
            chain(i_)
            dve.wait_ge(mods_done, 1)
            chain(v.tensor_tensor(modv[:], lin[:, 0, 0:21 * B].rearrange("p (c b) -> p c b", b=B),
                                  col[:, 0:21].unsqueeze(2).broadcast_to([128, 21, B]), ALU.add))
            for k, site in enumerate(NORMS):
                if site is None:
                    for r, nm in enumerate(("g2", "b2") if k == 6 else ("gam", "bet")):
                        v.tensor_copy(tab[:, 2 * k + r, :], c_(nm).broadcast_to([128, B]))
                    continue
                shift, scale, wcol = site
                w = c_(wcol) if wcol else 1.0
                v.tensor_scalar(tab[:, 2 * k, :], modv[:, scale, :], 1.0, w, ALU.add, ALU.mult)
                v.tensor_copy(tab[:, 2 * k + 1, :], modv[:, shift, :])
            v.tensor_copy(tab[:, T_ANCHOR:T_ANCHOR + 7, :], modv[:, 14:21, :])
            chain(v.tensor_copy(tab[:, T_COND, :], condT[:]))
            dve.wait_ge(gates_mm, 1)
            for i in range(NG):
                i_ = v.tensor_tensor(grow[:, i * 128:(i + 1) * 128],
                                     (lin[0:B, 1, i * 128:(i + 1) * 128] if i < 4 else avp[0:B, 0:128]),
                                     gbrow[:, i * 128:(i + 1) * 128], ALU.add)
            i_.then_inc(grow_done, 1)
            dve.wait_ge(bias_mm, 1)
            for i, r in enumerate((R_P1, R_S2, R_C2)):
                i_ = v.tensor_tensor(row[:, r, :], sco[0:1, 0, i * 128:(i + 1) * 128], row[:, r, :], ALU.add)
            i_.then_inc(tab_done, 1)

            def norm(it, k, s):
                t = C if k == 4 else 128
                src = ctxs[s] if k == 4 else xs[s]
                if k == 0:
                    base = it * (NS * GB) + s * GB
                    dve.wait_ge(x_in_s[s], it * 48 + 48)
                    v.tensor_copy(tabg[s][:], tab[:, :, bass.ds(base, GB)])
                    v.tensor_copy(mcg[s][:].rearrange("p b c -> p (b c)"),
                                  mcb[:, bass.ds(base * C, GB * C)]).then_inc(group_tab, 1)
                if k != 4:
                    res_ready(dve, it, f"l{k}", s)
                for b in range(GB):
                    i = v.bn_stats(bst[s][0:t, b, :], src[0:t, b, :])
                i.then_inc(ln_bn, 1)
                dve.wait_ge(ln_bn, nth(it, k, s, NLN))
                hold(dve)
                for b in range(GB):
                    i = v.bn_aggr(mv[s][0:t, b, :], bst[s][0:t, b, :])
                i.then_inc(ln_stats, 1)
                dve.wait_ge(ln_stats, nth(it, k, s, NLN))
                dve.wait_ge(ln_rstd, nth(it, k, s, NLN))
                for b in range(GB):
                    i = v.tensor_scalar((ctxs if k == 4 else xn)[s][0:t, b, :], src[0:t, b, :], mv[s][0:t, b, 0:1],
                                        rstd[s][0:t, 1, b:b + 1], ALU.subtract, ALU.mult)
                i.then_inc(ln_xn, 1)

            def values(it, a, s):
                st, kw = f"p{a}", ATT[a]["kw"]
                lin_ready(dve, it, st, s, "v")
                v.tensor_copy(diag(s, kw), lin_ap(st, s, "v", kw).rearrange(
                    "p (c h d) -> p c h d", h=4, d=8)).then_inc(lin_free[lin_bank(st, s, "v")], 1)

            def project(it, a, s):
                st = f"p{a}"
                if a == 0:
                    for r, (ja, jb, dst, done) in enumerate((("qa", "qb", qT, rope_q), ("ka", "kb", kT, rope_k))):
                        for u, (job, tbl) in enumerate(((ja, cosT), (jb, sinT))):
                            lin_ready(dve, it, st, s, job)
                            i = v.tensor_tensor(t1[s][:, 2 * r + u, :].rearrange("p (b t) -> p b t", b=GB),
                                                lin_ap(st, s, job).rearrange("p (b t) -> p b t", b=GB),
                                                tbl[:].unsqueeze(1).broadcast_to([128, GB, T]), ALU.mult)
                            i.then_inc(lin_free[lin_bank(st, s, job)], 1)
                        lin_taken(dve, it, st, s, ja)
                        lin_taken(dve, it, st, s, jb)
                        v.tensor_tensor(dst[s][:], t1[s][:, 2 * r, :], t1[s][:, 2 * r + 1, :], ALU.add).then_inc(done, 1)
                    dve.wait_ge(rope_q, nth(it, 0, s, 1))
                else:
                    lin_taken(dve, it, st, s, "q")
                v.tensor_copy(qb[s][:], qT[s][:]).then_inc(qb_ready, 1)
                values(it, a, s)

            def attention(it, a, s):
                kw = ATT[a]["kw"]

                def maxima(b, g):
                    dve.wait_ge(s_full, nth(it, a, s, NAT, 4 * b + g, GB * 4))
                    v.tensor_reduce(mx[:, 4 * g:4 * g + 4],
                                    sco[:, g % 2, 0:4 * kw].rearrange("p (h k) -> p h k", h=4), AX,
                                    ALU.max).then_inc(s_free, 1)

                def split(b):
                    n = nth(it, a, s, NAT, b, GB)
                    dve.wait_ge(s_free, nth(it, a, s, NAT, 4 * b + 3, GB * 4) + 2)
                    v.tensor_copy(mhl[:, 0:16], mx[:]).then_inc(mhi_ready, 1)
                    dve.wait_ge(mhi_ready, n)
                    v.tensor_tensor(mhl[:, 32:48], mx[:], mhl[:, 0:16], ALU.subtract).then_inc(m_split, 1)

                def turned(b):
                    dve.wait_ge(mt_full, nth(it, a, s, NAT, b, GB))
                    v.tensor_copy(mT[:], mtp[0:48, 0:T]).then_inc(mt_ready, 1)

                def normalise(b):
                    n = nth(it, a, s, NAT, b, GB)
                    dve.wait_ge(av_full, n)
                    v.reciprocal(rden[:], avp[:, T:2 * T]).then_inc(rden_ready, 1)
                    dve.wait_ge(rden_ready, n)
                    v.tensor_tensor(oT[s][:, b * T:(b + 1) * T], avp[:, 0:T], rden[:], ALU.mult).then_inc(av_free, 1)

                for g in range(4):
                    maxima(0, g)
                split(0)
                turned(0)
                for b in range(GB):
                    if b + 1 < GB:
                        for g in range(4):
                            maxima(b + 1, g)
                        split(b + 1)
                    if b > 0:
                        normalise(b - 1)
                    if b + 1 < GB:
                        turned(b + 1)
                normalise(GB - 1)

            def add_result(it, st, s, gate):
                lin_ready(dve, it, st, s, "y")
                y = lin_ap(st, s, "y").rearrange("p (b d) -> p b d", b=GB)
                free = lin_free[lin_bank(st, s, "y")]
                if gate is None:
                    v.tensor_tensor(xs[s][:], xs[s][:], y, ALU.add).then_inc(free, 1)
                else:
                    v.tensor_tensor(t1[s][:, 0, :].rearrange("p (b d) -> p b d", b=GB), y, gate, ALU.mult).then_inc(free, 1)
                    lin_taken(dve, it, st, s, "y")
                    v.tensor_tensor(xs[s][:], xs[s][:], t1[s][:, 0, :].rearrange("p (b d) -> p b d", b=GB),
                                    ALU.add).then_inc(x_ready, 1)

            def mixture(it, s):
                st = "x3"
                one = nth(it, 0, s, 1)
                lin_ready(dve, it, st, s, "q")
                v.tensor_copy(qT[s][:], lin_ap(st, s, "q")).then_inc(lin_free[lin_bank(st, s, "q")], 1)
                lin_ready(dve, it, st, s, "v")
                v3 = hid[s][0:C, 6, :]
                v.tensor_copy(v3, lin_ap(st, s, "v", C)).then_inc(lin_free[lin_bank(st, s, "v")], 1)
                lin_ready(dve, it, st, s, "s")
                v.tensor_reduce(mx3[s][:, 0, :], lin_ap(st, s, "s")[:, 0:NC].rearrange("p (b c) -> p b c", b=GB), AX,
                                ALU.max).then_inc(x3_max, 1)
                dve.wait_ge(x3_max, one)
                v.tensor_scalar(mx3[s][:, 1, :], mx3[s][:, 0, :], -float(D) ** -0.5, None, ALU.mult).then_inc(x3_neg, 1)
                lin_taken(dve, it, st, s, "s")
                v.tensor_reduce(mx3[s][:, 2, :], xn[s][:, :, 0:C], AX, ALU.add).then_inc(x3_sum, 1)
                dve.wait_ge(x3_sum, one)
                v.reciprocal(mx3[s][:, 3, :], mx3[s][:, 2, :]).then_inc(x3_rec, 1)
                dve.wait_ge(x3_rec, one)
                v.tensor_tensor(xn[s][:, :, 0:C], xn[s][:, :, 0:C],
                                mx3[s][:, 3, :].unsqueeze(2).broadcast_to([128, GB, C]), ALU.mult).then_inc(x3_p, 1)
                lin_ready(dve, it, st, s, "pt")
                v.tensor_copy(oT[s][0:C, :], lin_ap(st, s, "pt", C)).then_inc(lin_free[lin_bank(st, s, "pt")], 1)
                lin_ready(dve, it, st, s, "lt")
                lt = lin_ap(st, s, "lt")[:, 0:3 * GB].rearrange("p (b e) -> p b e", e=3)
                v.tensor_reduce(mx3[s][:, 0, :], lt, AX, ALU.max).then_inc(r3_max, 1)
                dve.wait_ge(r3_max, one)
                v.tensor_tensor(pr3[s][:, 0], lt, mx3[s][:, 0, :].unsqueeze(2).broadcast_to([128, GB, 3]),
                                ALU.subtract).then_inc(lin_free[lin_bank(st, s, "lt")], 1)
                dve.wait_ge(r3_exp, one)
                v.tensor_reduce(mx3[s][:, 1, :], pr3[s][:, 1], AX, ALU.add).then_inc(r3_sum, 1)
                dve.wait_ge(r3_sum, one)
                v.reciprocal(mx3[s][:, 2, :], mx3[s][:, 1, :]).then_inc(r3_rec, 1)
                dve.wait_ge(r3_rec, one)
                v.tensor_tensor(pr3[s][:, 2], pr3[s][:, 1], mx3[s][:, 2, :].unsqueeze(2).broadcast_to([128, GB, 3]),
                                ALU.mult).then_inc(r3_p, 1)
                dve.wait_ge(r3_p, one)
                for e in range(3):
                    lin_ready(dve, it, st, s, f"e{e}")
                    if e:
                        lin_taken(dve, it, st, s, f"e{e - 1}")
                    src = lin_ap(st, s, f"e{e}")
                    for b in range(GB):
                        p = pr3[s][:, 2, b, e:e + 1]
                        if e == 0:
                            i = v.tensor_scalar(xn[s][:, b, :], src[:, b * D:(b + 1) * D], p, None, ALU.mult)
                        else:
                            i = v.scalar_tensor_tensor(out=xn[s][:, b, :], in0=src[:, b * D:(b + 1) * D], scalar=p,
                                                       in1=xn[s][:, b, :], op0=ALU.mult, op1=ALU.add)
                    i.then_inc(lin_free[lin_bank(st, s, f"e{e}")], 1)
                lin_taken(dve, it, st, s, "g")
                add_result(it, st, s, hid[s][:, 5, :].rearrange("p (b d) -> p b d", b=GB))

            with dve.Fori(0, ITERS) as it:
                for st in STAGES:
                    for s in range(NS):
                        k = int(st[1:])
                        if st[0] == "l":
                            norm(it, k, s)
                        elif st[0] == "p":
                            project(it, k, s)
                        elif st[0] == "a":
                            attention(it, k, s)
                        elif st[0] in "om":
                            if st == "o0":
                                dve.wait_ge(g_in_s[s], it * 16 + 16)
                            g = gate_of.get(st)
                            add_result(it, st, s, None if g is None else gbc[s][:, :, g * 128:(g + 1) * 128])
                        elif st == "x3":
                            mixture(it, s)

        @block.tensor
        def _(pe):
            mm = nc.tensor.matmul
            pe.wait_ge(loaded, 16 * NCONST)
            pe.wait_ge(silu_done, 1)
            pe.wait_ge(lin_free[0], 1)
            pe.wait_ge(lin_free[1], 1)
            for c, (blk, silu) in enumerate(MODS):
                i = mm(lin[:, 0, c * B:(c + 1) * B], W[:, blk, :], (scondT if silu else condT)[:], start=True, stop=True)
            i.then_inc(mods_done, 1)
            for c, (blk, silu) in enumerate(GATES):
                dst = lin[0:B, 1, c * 128:(c + 1) * 128] if c < 4 else avp[0:B, 0:128]
                i = mm(dst, (scondT if silu else condT)[:], W[:, blk, :], start=True, stop=True)
            i.then_inc(gates_mm, 1)
            for c, (cn, wn) in enumerate((("bv1", "wp1"), ("vb2", "so2"), ("cv2", "co2"))):
                i = mm(sco[0:1, 0, c * 128:(c + 1) * 128], c_(cn), wblk(wn), start=True, stop=True)
            i.then_inc(bias_mm, 1)
            pe.wait_ge(tab_done, 1)

            def take(it, st, s, job):
                pe.wait_ge(lin_free[lin_bank(st, s, job)], lin_turn(it, st, s, job))

            def give(st, s, job, i):
                i.then_inc(lin_full[lin_bank(st, s, job)], 1)

            def linear(it, st, s, job, parts, n, m=128):
                take(it, st, s, job)
                for c, (w, a) in enumerate(parts):
                    i = mm(lin_ap(st, s, job, m)[:, 0:n], w, a, start=(c == 0), stop=(c == len(parts) - 1))
                give(st, s, job, i)

            def tokens(it, st, s, job, src, wts, bias=None, t=T):
                take(it, st, s, job)
                o = lin_ap(st, s, job, t)
                if bias is not None:
                    mm(o.rearrange("p (b d) -> p b d", b=GB), onef[:, 0:t],
                       row[:, bias, :].unsqueeze(1).broadcast_to([1, GB, 128]), start=True, stop=False,
                       skip_group_check=True)
                for b in range(GB):
                    for c, (a, w) in enumerate(zip(src, wts)):
                        i = mm(o[:, b * 128:(b + 1) * 128], a[:, b * t:(b + 1) * t], w,
                               start=(c == 0 and bias is None), stop=(c == len(wts) - 1), skip_group_check=True)
                give(st, s, job, i)

            def norm(it, k, s):
                st, t = f"l{k}", (C if k == 4 else 128)
                take(it, st, s, "t")
                pe.wait_ge(ln_xn, nth(it, k, s, NLN))
                for b in range(GB):
                    i = nc.tensor.transpose(lin_ap(st, s, "t")[:, b * t:(b + 1) * t],
                                            (ctxs if k == 4 else xn)[s][0:t, b, :], ident[0:t, 0:t])
                give(st, s, "t", i)

            def project(it, a, s):
                st, A = f"p{a}", ATT[a]
                n = GB * A["kw"]
                own = a in (0, 3)
                if a == 2:
                    lin_taken(pe, it, "l3", s, "t")
                lin_taken(pe, it, {0: "l0", 1: "l1", 2: "l4", 3: "l5", 4: "l6"}[a], s, "t")
                h = hT[s][:]
                if a == 0:
                    linear(it, st, s, "qa", [(wblk("qkv0", 0), h)], N)
                    linear(it, st, s, "qb", [(Wrot[:, 0, :], h)], N)
                    linear(it, st, s, "ka", [(wblk("qkv0", 1), h)], N)
                    linear(it, st, s, "kb", [(Wrot[:, 1, :], h)], N)
                else:
                    linear(it, st, s, "q", [(wblk(A["q"]), h)], N)
                kv = h if own else (hid[s][:, 5, 0:NC] if a == 2 else ctxT[s][:].rearrange("p b c -> p (b c)"))
                if a > 0:
                    linear(it, st, s, "k", [(W[:, KBLK[a], :], kv)], n)
                tokens(it, st, s, "v", [kv], [W[:, VBLK[a], :]], t=A["kw"])

            def attention(it, a, s):
                kw = ATT[a]["kw"]

                def jth(b):
                    return (a * NS + s) * GB + b

                def scores(b, g):
                    if g == 0:
                        pe.wait_ge(kbb_ready, nth(it, a, s, NAT, b, GB))
                    pe.wait_ge(s_free, nth(it, a, s, NAT, 4 * b + g, GB * 4))
                    o = sco[:, g % 2, 0:4 * kw].rearrange("p (h k) -> p h k", h=4)
                    i = mm(o, qb[s][:, b * T:(b + 1) * T], kbb[:, jth(b) % 2, 4 * g:4 * g + 4, 0:kw],
                           start=True, stop=(a > 1))
                    if a == 0:
                        i = mm(o, identb[:], mqk[:].unsqueeze(1).broadcast_to([128, 4, T]), start=False, stop=True)
                    elif a == 1:
                        i = mm(o, oneb[:, 0:T], mcg[s][:, b, :].unsqueeze(1).broadcast_to([1, 4, C]),
                               start=False, stop=True)
                    i.then_inc(s_full, 1)

                def turn(b):
                    pe.wait_ge(m_split, nth(it, a, s, NAT, b, GB))
                    hold(pe)
                    nc.tensor.transpose(mtp[0:48, 0:T], mhl[:], identb[:]).then_inc(mt_full, 1)

                def scores_t(b, g):
                    if g == 0:
                        pe.wait_ge(mt_ready, nth(it, a, s, NAT, b, GB))
                    pe.wait_ge(st_free, nth(it, a, s, NAT, 4 * b + g, GB * 4))
                    o = sct[0:kw, g % 2, :]
                    for hh in range(4):
                        mm(o[:, hh * T:(hh + 1) * T], kbd[:, jth(b) % 2, 4 * g + hh, 0:kw], qT[s][:, b * T:(b + 1) * T],
                           start=(hh == 0), stop=False, skip_group_check=True)
                    oh = o.rearrange("p (h q) -> p h q", h=4)
                    if a == 0:
                        mm(oh, identb[:], mkq[:].unsqueeze(1).broadcast_to([128, 4, T]), start=False, stop=False,
                           skip_group_check=True)
                    elif a == 1:
                        mm(o, mcg[s][:, b, :], oneb[:], start=False, stop=False, skip_group_check=True)
                    for hh in range(4):
                        i = mm(o[:, hh * T:(hh + 1) * T], indb[:, 4 * g + hh, 0:kw], mT[:], start=False,
                               stop=(hh == 3), skip_group_check=True)
                    i.then_inc(st_full, 1)

                def av(b):
                    pe.wait_ge(st_free, nth(it, a, s, NAT, 4 * b + 3, GB * 4) + 2)
                    pe.wait_ge(av_free, nth(it, a, s, NAT, b, GB))
                    for part in range(2):
                        for hh in range(4):
                            for g in range(4):
                                w = Vp[s][0:kw, b, 4 * g + hh, :] if part == 0 else onesp[0:kw, hh, :]
                                i = mm(avp[32 * g:32 * g + 32, part * T:(part + 1) * T], w,
                                       P[jth(b) % 2][0:kw, 4 * g + hh, :], start=(hh == 0), stop=(hh == 3),
                                       skip_group_check=True)
                    i.then_inc(av_full, 1)

                pe.wait_ge(qb_ready, nth(it, a, s, NAT))
                if a == 0:
                    pe.wait_ge(rope_q, nth(it, 0, s, 1))
                lin_taken(pe, it, f"p{a}", s, "v")
                for g in range(4):
                    scores(0, g)
                turn(0)
                for b in range(GB):
                    for g in range(4):
                        scores_t(b, g)
                        if b + 1 < GB:
                            scores(b + 1, g)
                    if b > 0:
                        av(b - 1)
                    if b + 1 < GB:
                        turn(b + 1)
                av(GB - 1)

            def outproj(it, a, s):
                pe.wait_ge(av_free, nth(it, a, s, NAT, GB - 1, GB) + 1)
                tokens(it, f"o{a}", s, "y", [oT[s][:]], [wblk(ATT[a]["o"])], ATT[a]["row"])

            def mlp(it, k, s):
                st = f"m{k}"
                w1, w2 = ("m10", "m20") if k == 0 else ("m12", "m22")
                lin_taken(pe, it, "l2" if k == 0 else "l7", s, "t")
                for c in range(4):
                    linear(it, st, s, f"h{c}", [(wblk(w1, c), hT[s][:])], N)
                for c in range(4):
                    lin_taken(pe, it, st, s, f"h{c}")
                tokens(it, st, s, "y", [hid[s][:, c, :] for c in range(4)], [wblk(w2, c) for c in range(4)],
                       R_M0 if k == 0 else R_M2)

            def mixture(it, s):
                st = "x3"
                h, ev, ct = hT[s][:], kT[s][:], ctxT[s][:].rearrange("p b c -> p (b c)")
                lin_taken(pe, it, "l8", s, "t")
                linear(it, st, s, "q", [(wblk("q3"), h)], N)
                linear(it, st, s, "k", [(wblk("k3"), ct)], NC)
                tokens(it, st, s, "v", [ct], [wblk("v3")], t=C)
                for job in ("q", "k"):
                    lin_taken(pe, it, st, s, job)
                take(it, st, s, "s")
                for b in range(GB):
                    i = mm(lin_ap(st, s, "s")[:, b * C:(b + 1) * C], qT[s][:, b * T:(b + 1) * T],
                           kT[s][:, b * C:(b + 1) * C], start=True, stop=True)
                give(st, s, "s", i)
                take(it, st, s, "pt")
                pe.wait_ge(x3_p, nth(it, 0, s, 1))
                for b in range(GB):
                    i = nc.tensor.transpose(lin_ap(st, s, "pt", C)[:, b * T:(b + 1) * T], xn[s][:, b, 0:C], ident[:])
                give(st, s, "pt", i)
                for job in ("v", "pt"):
                    lin_taken(pe, it, st, s, job)
                take(it, st, s, "ev")
                for b in range(GB):
                    i = mm(lin_ap(st, s, "ev")[:, b * T:(b + 1) * T], hid[s][0:C, 6, b * D:(b + 1) * D],
                           oT[s][0:C, b * T:(b + 1) * T], start=True, stop=True)
                give(st, s, "ev", i)
                lin_taken(pe, it, st, s, "ev")
                anchor = tabg[s][:, T_COND, :].unsqueeze(2).broadcast_to([128, GB, T])
                linear(it, st, s, "lg", [(rw[:, 0, :], h), (rw[:, 1, :], ev), (rw[:, 2, :], anchor)], N, m=3)
                lin_taken(pe, it, st, s, "lg")
                take(it, st, s, "lt")
                hold(pe)
                for b in range(GB):
                    i = nc.tensor.transpose(lin_ap(st, s, "lt")[:, 3 * b:3 * b + 3], lgT[s][:, b * T:(b + 1) * T],
                                            ident[0:3, 0:3])
                give(st, s, "lt", i)
                for c in range(7):
                    e, r = c // 2, c % 2
                    w0, w1 = (wblk("e1", 6 * e + r), wblk("e1", 6 * e + 2 + r)) if c < 6 else (wblk("g1", 0), wblk("g1", 1))
                    linear(it, st, s, f"h{c}", [(w0, h), (w1, ev)], N)
                for e in range(3):
                    for r in range(2):
                        lin_taken(pe, it, st, s, f"h{2 * e + r}")
                    tokens(it, st, s, f"e{e}", [hid[s][:, 2 * e + r, :] for r in range(2)],
                           [wblk("e2", 2 * e + r) for r in range(2)], R_E + e)
                take(it, st, s, "rt")
                lin_taken(pe, it, st, s, "e2")
                for b in range(GB):
                    i = nc.tensor.transpose(lin_ap(st, s, "rt")[:, b * T:(b + 1) * T], xn[s][:, b, :], ident[:])
                give(st, s, "rt", i)
                lin_taken(pe, it, st, s, "h6")
                tokens(it, st, s, "g", [hid[s][:, 6, :]], [wblk("g2")], R_GATE)
                lin_taken(pe, it, st, s, "rt")
                tokens(it, st, s, "y", [oT[s][:]], [wblk("ow3")], R_OUT)

            with pe.Fori(0, ITERS) as it:
                for st in STAGES:
                    for s in range(NS):
                        k = int(st[1:])
                        if st == "l0":
                            pe.wait_ge(group_tab, nth(it, 0, s, 1))
                        if st[0] == "l":
                            norm(it, k, s)
                        elif st[0] == "p":
                            project(it, k, s)
                        elif st[0] == "a":
                            attention(it, k, s)
                        elif st[0] == "o":
                            outproj(it, k, s)
                        elif st[0] == "m":
                            mlp(it, k, s)
                        elif st == "x3":
                            mixture(it, s)


def shape_constants():
    inv = 1.0 / 10000.0 ** (np.arange(0, HD, 2, dtype=np.float32) / HD)
    freqs = np.outer(np.arange(HALF, dtype=np.float32), inv)
    emb = np.concatenate([freqs, freqs], axis=-1)
    cos = np.tile(np.cos(emb).astype(np.float32).T, (H, 2))
    sin = np.tile(np.sin(emb).astype(np.float32).T, (H, 2))
    ind = np.zeros((48, H), np.float32)
    ind[np.arange(H), np.arange(H)] = -1.0
    ind[32 + np.arange(H), np.arange(H)] = -1.0
    onesp = np.zeros((128, 4, 32), np.float32)
    for hh in range(4):
        onesp[:, hh, 8 * hh:8 * hh + 8] = 1.0
    hmask = (np.arange(128)[:, None] // HD == np.arange(H)[None, :]).astype(np.float32)
    return np.ascontiguousarray(cos), np.ascontiguousarray(sin), np.eye(128, dtype=np.float32), ind, onesp, hmask


def kernel(**inputs):
    import concourse.bacc as bacc
    from concourse.bass_utils import run_bass_kernel_spmd

    a = {k: np.asarray(v) for k, v in inputs.items()}
    cos, sin, ident, ind, onesp, hmask = shape_constants()

    def blocks(w):
        r, c = w.shape[0] // 128, w.shape[1] // 128
        return w.reshape(r, 128, c, 128).transpose(1, 0, 2, 3).reshape(128, r * c, 128)

    e1, e2 = a["L3_xcond_e_w1"], a["L3_xcond_e_w2"]
    parts = {"ada0": a["L0_xcond_adaLN_W"], "qkv0": a["L0_xcond_qkv_W"], "ao0": a["L0_xcond_attn_out_W"],
             "cq0": a["L0_xcond_cq_W"], "ck0": a["L0_xcond_ck_W"], "cv0": a["L0_xcond_cv_W"],
             "co0": a["L0_xcond_co_W"], "m10": a["L0_xcond_mlp_W1"], "m20": a["L0_xcond_mlp_W2"],
             "wq1": a["L1_xcond_Wq"], "wkv1": a["L1_xcond_Wkv"], "wp1": a["L1_xcond_Wp"],
             "ssq": a["L1_xcond_Wss_q"], "sskv": a["L1_xcond_Wss_kv"], "ada2": a["L2_xcond_ada_w"],
             "qkv2": a["L2_xcond_qkv_w"], "so2": a["L2_xcond_self_o_w"], "q2": a["L2_xcond_q_w"],
             "kv2": a["L2_xcond_kv_w"], "co2": a["L2_xcond_cross_o_w"], "m12": a["L2_xcond_mlp_w1"],
             "m22": a["L2_xcond_mlp_w2"], "q3": a["L3_xcond_Wq"], "k3": a["L3_xcond_Wk"], "v3": a["L3_xcond_Wv"],
             "g1": a["L3_xcond_gate_w1"], "g2": a["L3_xcond_gate_w2"], "ow3": a["L3_xcond_out_w"]}
    wl = []
    for name, n in W_PARTS:
        if name == "e1":
            wl += [blocks(e1[e]) for e in range(3)]
        elif name == "e2":
            wl += [blocks(e2[e]) for e in range(3)]
        else:
            wl.append(blocks(parts[name]))
            assert wl[-1].shape[1] == n
    w = np.ascontiguousarray(np.concatenate(wl, axis=1))

    def cols(v):
        return v.reshape(-1, 128).T

    b0, b2 = a["L0_xcond_adaLN_b"].reshape(9, 128), a["L2_xcond_ada_b"].reshape(6, 128)
    modb = np.concatenate([b0[[0, 1, 3, 4, 6, 7]], a["L1_xcond_bss_q"].reshape(2, 128),
                           a["L1_xcond_bss_kv"].reshape(2, 128), b2[[0, 1, 3, 4]],
                           a["L3_xcond_e_b1"].reshape(6, 128), a["L3_xcond_gate_b1"].reshape(1, 128)])
    cparts = {"modb": modb, "n1": a["L0_xcond_norm1_w"], "nc": a["L0_xcond_normc_w"], "n2": a["L0_xcond_norm2_w"],
              "g2": a["L2_xcond_norm2_g"], "b2": a["L2_xcond_norm2_b"], "gam": a["L3_xcond_ln_gamma"],
              "bet": a["L3_xcond_ln_beta"], "bq1": a["L1_xcond_bq"], "bk1": a["L1_xcond_bkv"][:128],
              "bv1": a["L1_xcond_bkv"][128:], "qb2": a["L2_xcond_qkv_b"][:128], "kb2": a["L2_xcond_qkv_b"][128:256],
              "vb2": a["L2_xcond_qkv_b"][256:], "cq2": a["L2_xcond_q_b"], "ck2": a["L2_xcond_kv_b"][:128],
              "cv2": a["L2_xcond_kv_b"][128:], "m10": a["L0_xcond_mlp_b1"], "m12": a["L2_xcond_mlp_b1"]}
    col = np.ascontiguousarray(np.concatenate([hmask if n == "hmask" else cols(cparts[n]) for n, _ in C_PARTS], axis=1))
    row = np.ascontiguousarray(np.stack([a["L0_xcond_mlp_b2"], a["L1_xcond_bp"], a["L2_xcond_self_o_b"],
                                         a["L2_xcond_cross_o_b"], a["L2_xcond_mlp_b2"], a["L3_xcond_out_b"],
                                         a["L3_xcond_gate_b2"], *a["L3_xcond_e_b2"]])[None])
    gb = np.concatenate([b0[2], b0[5], b0[8], b2[2], b2[5]])
    gb = np.ascontiguousarray(np.broadcast_to(gb[None], (B, NG * 128)))
    rw = np.ascontiguousarray(a["L3_xcond_router_W"].reshape(3, 128, 3).transpose(1, 0, 2))
    rb = np.ascontiguousarray(a["L3_xcond_router_b"].reshape(3, 1))
    m2, mc = a["mask_SxS_bk0"], a["mask_BxS2_bf1"]
    arrays = [("x", np.ascontiguousarray(a["x"].transpose(1, 0, 2))),
              ("ctx", np.ascontiguousarray(a["ctx_1024"].transpose(1, 0, 2))),
              ("ctxT", np.ascontiguousarray(a["ctx_1024"].transpose(2, 0, 1))),
              ("condT", np.ascontiguousarray(a["cond_1024"].T)), ("w", w), ("col", col), ("row", row), ("rw", rw),
              ("rb", rb), ("gb", gb), ("mqk", np.ascontiguousarray(m2)), ("mkq", np.ascontiguousarray(m2.T)),
              ("mc", np.ascontiguousarray(mc.reshape(1, B * C))), ("cos", cos), ("sin", sin),
              ("ident", ident), ("ind", ind), ("onesp", onesp)]
    nc = bacc.Bacc("TRN2", target_bir_lowering=False, num_devices=1)
    ins, args = {}, []
    for name, arr in arrays:
        ins[f"in_{name}"] = arr
        dt = U8 if arr.dtype == bool else mybir.dt.from_np(arr.dtype)
        args.append(nc.dram_tensor(f"in_{name}", arr.shape, dt, kind="ExternalInput").ap())
    out = nc.dram_tensor("out", (T, B, D), F32, kind="ExternalOutput").ap()
    build(nc, *args, out)
    r = run_bass_kernel_spmd(nc, [ins], core_ids=[0])
    return np.ascontiguousarray(r.results[0]["out"].transpose(1, 0, 2))
```

```python
from contextlib import ExitStack

import numpy as np

import concourse.bass as bass
from concourse import mybir

F32 = mybir.dt.float32
BF16 = mybir.dt.bfloat16
U8 = mybir.dt.uint8
ACT = mybir.ActivationFunctionType
ALU = mybir.AluOpType
AX = mybir.AxisListType.X

B, T, D, C = 16, 128, 128, 77
H, HD = 16, 8
GB = 4
NS = 2
ITERS = B // (GB * NS)
N = GB * T
NC = GB * C
HALF = T // 2
BIG = 2.0 ** 100

W_PARTS = [("ada0", 9), ("ssq", 2), ("sskv", 2), ("ada2", 6), ("qkv0", 3), ("ao0", 1), ("cq0", 1), ("ck0", 1), ("cv0", 1), ("co0", 1), ("m10", 4),
           ("m20", 4), ("wq1", 1), ("wkv1", 2), ("wp1", 1), ("qkv2", 3),
           ("so2", 1), ("q2", 1), ("kv2", 2), ("co2", 1), ("m12", 4), ("m22", 4), ("q3", 1), ("k3", 1),
           ("v3", 1), ("e1", 18), ("e2", 6), ("g1", 3), ("g2", 1), ("ow3", 1)]
W_AT, _n = {}, 0
for _name, _k in W_PARTS:
    W_AT[_name] = _n
    _n += _k
NW = _n

C_PARTS = [("modb", 21), ("n1", 1), ("nc", 1), ("n2", 1), ("g2", 1), ("b2", 1), ("gam", 1), ("bet", 1),
           ("bq1", 1), ("bk1", 1), ("bv1", 1), ("qb2", 1), ("kb2", 1), ("vb2", 1), ("cq2", 1), ("ck2", 1),
           ("cv2", 1), ("m10", 4), ("m12", 4), ("hmask", 16)]
C_AT, _n = {}, 0
for _name, _k in C_PARTS:
    C_AT[_name] = _n
    _n += _k
NCOL = _n

T_ANCHOR, T_COND, NT = 18, 25, 26
MODS = ([(W_AT["ada0"] + c, 0) for c in (0, 1, 3, 4, 6, 7)] + [(W_AT["ssq"] + c, 1) for c in (0, 1)]
        + [(W_AT["sskv"] + c, 1) for c in (0, 1)] + [(W_AT["ada2"] + c, 1) for c in (0, 1, 3, 4)]
        + [(W_AT["e1"] + 6 * e + 4 + r, 0) for e in range(3) for r in range(2)] + [(W_AT["g1"] + 2, 0)])
NORMS = [(0, 1, "n1"), (2, 3, "nc"), (4, 5, "n2"), (7, 6, None), (9, 8, None), (10, 11, None), None,
         (12, 13, None), None]
GATES = [(W_AT["ada0"] + 2, 0), (W_AT["ada0"] + 5, 0), (W_AT["ada0"] + 8, 0), (W_AT["ada2"] + 2, 1),
         (W_AT["ada2"] + 5, 1)]
NG = len(GATES)
R_M0, R_P1, R_S2, R_C2, R_M2, R_OUT, R_GATE, R_E = 0, 1, 2, 3, 4, 5, 6, 7
NR = 10

NLN, NAT = 9, 5
ATT = [dict(kw=T, q="qkv0", k=1, v=2, bq=None, bk=None, o="ao0", row=None, gate=0),
       dict(kw=C, q="cq0", k="ck0", v="cv0", bq=None, bk=None, o="co0", row=None, gate=1),
       dict(kw=C, q="wq1", k="wkv1", v=None, bq="bq1", bk="bk1", o="wp1", row=R_P1, gate=None),
       dict(kw=T, q="qkv2", k=1, v=2, bq="qb2", bk="kb2", o="so2", row=R_S2, gate=3),
       dict(kw=C, q="q2", k="kv2", v=None, bq="cq2", bk="ck2", o="co2", row=R_C2, gate=None)]
KBLK = [W_AT["qkv0"] + 1, W_AT["ck0"], W_AT["wkv1"], W_AT["qkv2"] + 1, W_AT["kv2"]]
VBLK = [W_AT["qkv0"] + 2, W_AT["cv0"], W_AT["wkv1"] + 1, W_AT["qkv2"] + 2, W_AT["kv2"] + 1]


def norm_parts(k):
    return [(f"l{k}", "stat"), (f"l{k}", "apply"), (f"l{k}", "t")]


X3_PARTS = ["q", "k", "v", "s", "pt", "ev", "lg", "lt"] + [f"h{c}" for c in range(7)] + ["e0", "e1", "e2", "rt", "g", "y"]
BETWEEN = [
    norm_parts(0) + [("p0", "k"), ("p0", "q"), ("p0", "v")],
    [("p1", "k"), ("p1", "v"), ("o0", "y")] + norm_parts(1) + [("p1", "q")],
    norm_parts(4)[:2] + [("o1", "y"), ("l4", "t")] + norm_parts(2)[:2] + [("p2", "k"), ("l2", "t"), ("p2", "v")]
    + [("m0", f"h{c}") for c in range(4)] + [("m0", "y")] + norm_parts(3) + [("p2", "q")],
    [("o2", "y")] + norm_parts(5) + [("p3", "k"), ("p3", "q"), ("p3", "v")],
    [("p4", "k"), ("p4", "v"), ("o3", "y")] + norm_parts(6) + [("p4", "q")],
    [("x3", "k"), ("x3", "v"), ("o4", "y")] + norm_parts(7) + [("m1", f"h{c}") for c in range(4)] + [("m1", "y")]
    + norm_parts(8) + [("x3", j) for j in X3_PARTS if j not in ("k", "v")],
]
JOBS = NAT * NS * GB


def merge(k, s_att, between, s_bet, first, last):
    out, done = [], 0
    for i in range(4 * GB):
        out.append(("A", (k * NS + s_att) * GB + i // 4, i % 4))
        upto = len(between) * (i - first + 1) // (last - first + 1) if first <= i <= last else (
            len(between) if i > last else 0)
        while done < upto:
            out.append(("B", between[done], s_bet))
            done += 1
    return out


UNITS = [("B", u, 0) for u in BETWEEN[0]] + [("START", None, None)]
for _k in range(NAT):
    UNITS += merge(_k, 0, BETWEEN[_k], 1, 0 if _k == 0 else 3, 10)
    UNITS += merge(_k, 1, BETWEEN[_k + 1], 0, 3, 10 if _k + 1 < NAT else 15)
UNITS += [("END", None, None)] + [("B", u, 1) for u in BETWEEN[NAT]]

LIN_AT, _n = {}, 0
for _kind, _u, _s in UNITS:
    if _kind == "B" and _u[1] not in ("stat", "apply"):
        for _job in ([_u[1] + "a", _u[1] + "b"] if _u in (("p0", "q"), ("p0", "k")) else [_u[1]]):
            LIN_AT[(_u[0], _s, _job)] = _n
            _n += 1
LIN_JOBS = _n
assert LIN_JOBS % 2 == 0


def lin_bank(st, s, job):
    return LIN_AT[(st, s, job)] % 2


def lin_turn(it, st, s, job):
    return it * (LIN_JOBS // 2) + LIN_AT[(st, s, job)] // 2 + 1


LN_ORDER = [(int(u[0][1:]), s) for kind, u, s in UNITS if kind == "B" and u[1] == "stat"]
GATED = ["o0", "o1", "m0", "o3", "m1", "x3"]
GATED_ORDER = [(u[0], s) for kind, u, s in UNITS if kind == "B" and u[1] == "y" and u[0] in GATED]


def norm_turn(it, k, s):
    return it * len(LN_ORDER) + LN_ORDER.index((k, s)) + 1


def gated_turn(it, st, s):
    return it * len(GATED_ORDER) + GATED_ORDER.index((st, s)) + 1


def job_turn(it, j, part=0, per=1):
    return it * (JOBS * per) + j * per + part + 1


def job_of(j):
    return j // (NS * GB), j // GB % NS, j % GB


def nth(it, k, s, kinds, b=0, per=1):
    return it * (kinds * NS * per) + (k * NS + s) * per + b + 1


def build(nc, x_in, ctx_in, ctxT_in, condT_in, w_in, col_in, row_in, rw_in, rb_in, gb_in, mqk_in, mkq_in,
          mc_in, cos_in, sin_in, ident_in, ind_in, onesp_in, out):
    ctx = ExitStack()
    with ctx:
        def sb(name, shape, dt=F32):
            return ctx.enter_context(nc.sbuf_tensor(name, shape, dt))

        def ps(name, shape, dt=F32):
            return ctx.enter_context(nc.psum_tensor(name, shape, dt))

        def sem(name):
            return ctx.enter_context(nc.semaphore(name))

        lin = ps("lin", [128, 2, 512])
        sco = ps("sco", [128, 2, 512])
        sct = ps("sct", [128, 2, 512])
        avp = ps("avp", [128, 512])
        mtp = ps("mtp", [128, 1024], BF16)

        W = sb("W", [128, NW, 128])
        Wrot = sb("Wrot", [128, 2, 128])
        col = sb("col", [128, NCOL])
        rw = sb("rw", [128, 3, 3])
        rb = sb("rb", [3, 1])
        condT = sb("condT", [128, B])
        scondT = sb("scondT", [128, B])
        modv = sb("modv", [128, 21, B])
        tab = sb("tab", [128, NT, B])
        cosT = sb("cosT", [128, T])
        sinT = sb("sinT", [128, T])
        ident = sb("ident", [128, 128])
        identb = sb("identb", [128, 128], BF16)
        rowb = sb("rowb", [128, NR, 128], BF16)
        oneb = sb("oneb", [128, 512], BF16)
        ind48 = sb("ind48", [128, H])
        indb = sb("indb", [128, H, 128], BF16)
        onesp = sb("onesp", [128, 4, 32])
        mqk8 = sb("mqk8", [128, T], U8)
        mkq8 = sb("mkq8", [128, T], U8)
        mc8 = sb("mc8", [1, B * C], U8)
        mqk = sb("mqk", [128, T], BF16)
        mkq = sb("mkq", [128, T], BF16)
        mcb = sb("mcb", [1, B * C], BF16)
        mhalf = sb("mhalf", [128, GB])

        xs, ctxs, ctxT, gbc, tabg, mcg = [], [], [], [], [], []
        mv, bst, rstd, xn, hT, qT, qb, kT, t1, Vp, oT, hid = [], [], [], [], [], [], [], [], [], [], [], []
        for s in range(NS):
            xs.append(sb(f"x{s}", [128, GB, D]))
            ctxs.append(sb(f"ctx{s}", [C, GB, D]))
            ctxT.append(sb(f"ctxT{s}", [128, GB, C]))
            gbc.append(sb(f"gbc{s}", [128, GB, NG * 128]))
            tabg.append(sb(f"tabg{s}", [128, NT, GB]))
            mcg.append(sb(f"mcg{s}", [128, GB, C], BF16))
            mv.append(sb(f"mv{s}", [128, GB, 2]))
            bst.append(sb(f"bst{s}", [128, GB, 6]))
            rstd.append(sb(f"rstd{s}", [128, 2, GB]))
            xn.append(sb(f"xn{s}", [128, GB, D]))
            hT.append(sb(f"hT{s}", [128, N]))
            qT.append(sb(f"qT{s}", [128, N]))
            qb.append(sb(f"qb{s}", [128, N], BF16))
            kT.append(sb(f"kT{s}", [128, N]))
            Vp.append(sb(f"Vp{s}", [128, GB, H, 32]))
            oT.append(sb(f"oT{s}", [128, N]))
            hid.append(sb(f"hid{s}", [128, 7, N]))
            t1.append(hid[s][:, 0:4, :])
        row = hid[0][0:1].rearrange("p c n -> p (c n)")[:, 0:NR * 128].rearrange("p (r d) -> p r d", r=NR)
        rowr = hid[1][0:1].rearrange("p c n -> p (c n)")[:, 0:2 * NR * 128].rearrange("p (t r d) -> p t r d", t=2, r=NR)
        mx3 = [sb(f"mx3{s}", [128, 4, GB]) for s in range(NS)]
        pr3 = [sb(f"pr3{s}", [128, 3, GB, 3]) for s in range(NS)]
        lgT = [sb(f"lgT{s}", [3, N]) for s in range(NS)]

        kbd = sb("kbd", [128, 3, H, 128])
        kbb = sb("kbb", [128, 2, H, 128], BF16)
        rows3 = kbb[0:1].rearrange("p i h k -> p (i h k)")[:, 0:2 * NR * 128].rearrange("p (t r d) -> p t r d", t=2, r=NR)
        P1 = sb("P1", [128, H, T])
        P = [W[:, 0:H, :], P1[:]]
        gbrow, grow = (P1[0:B, i * NG:(i + 1) * NG, :].rearrange("p g d -> p (g d)") for i in range(2))
        mx = sb("mx", [128, H])
        mhl = sb("mhl", [128, 128], BF16)
        mT = sb("mT", [128, T], BF16)
        rden = sb("rden", [128, T])

        gdram = nc.dram_tensor("gate_rows", (B, NG * 128), F32, kind="Internal").ap()

        loaded = sem("loaded")
        gate_rows_out = sem("gate_rows_out")
        x_in_s = [sem(f"x_loaded{s}") for s in range(NS)]
        g_in_s = [sem(f"gates_loaded{s}") for s in range(NS)]
        stored = [sem(f"stored{s}") for s in range(NS)]
        zeroed = sem("zeroed")
        silu_done = sem("silu_done")
        mods_done, modv_done, tab_done = sem("mods_done"), sem("modv_done"), sem("tab_done")
        gates_mm, grow_done = sem("gates_mm"), sem("grow_done")
        setup_dve = sem("setup_dve")
        rows_in = sem("rows_in")
        bias_mm = sem("bias_mm")
        group_tab = sem("group_tab")
        lin_full = [sem(f"lin_full{i}") for i in range(2)]
        lin_free = [sem(f"lin_free{i}") for i in range(2)]
        ln_bn, ln_stats, ln_eps, ln_rstd, ln_xn = (sem(n) for n in ("ln_bn", "ln_stats", "ln_eps", "ln_rstd", "ln_xn"))
        rope_parts, rope_q, rope_k, qb_ready = (sem(n) for n in ("rope_parts", "rope_q", "rope_k", "qb_ready"))
        kbd_ready, kbb_ready = sem("kbd_ready"), sem("kbb_ready")
        s_full, s_free, m_ready, mhi_ready, m_split, mt_full, mt_ready = (sem(n) for n in (
            "s_full", "s_free", "m_ready", "mhi_ready", "m_split", "mt_full", "mt_ready"))
        st_full, st_free, av_full, rden_ready, av_free = (sem(n) for n in (
            "st_full", "st_free", "av_full", "rden_ready", "av_free"))
        x_ready = sem("x_ready")
        x3_max, x3_neg, x3_sum, x3_rec, x3_p = (sem(n) for n in ("x3_max", "x3_neg", "x3_sum", "x3_rec", "x3_p"))
        r3_max, r3_exp, r3_sum, r3_rec, r3_p = (sem(n) for n in ("r3_max", "r3_exp", "r3_sum", "r3_rec", "r3_p"))

        NCONST = 18
        gate_of = {"o0": 0, "o1": 1, "m0": 2, "o3": 3, "m1": 4}

        def wblk(name, k=0, n=1):
            a = W_AT[name] + k
            return W[:, a, :] if n == 1 else W[:, a:a + n, :]

        def c_(name, k=0):
            a = C_AT[name] + k
            return col[:, a:a + 1]

        def hold(eng):
            eng.nop(nofuse=True)

        def lin_ready(eng, it, st, s, job):
            eng.wait_ge(lin_full[lin_bank(st, s, job)], lin_turn(it, st, s, job))

        def lin_taken(eng, it, st, s, job):
            eng.wait_ge(lin_free[lin_bank(st, s, job)], lin_turn(it, st, s, job) + 1)
            hold(eng)

        def lin_ap(st, s, job, p=128):
            return lin[0:p, lin_bank(st, s, job), :]

        def diag(s, kw):
            v = Vp[s][0:kw]
            return bass.AP(tensor=v.tensor, offset=v.offset, ap=[list(v.ap[0]), [128, 16], [40, 4], [1, 8]])

        def res_ready(eng, it, st, s):
            before = {"l0": None, "l1": "o0", "l2": "o1", "l3": "m0", "l5": "o2", "l6": "o3", "l7": "o4", "l8": "m1"}[st]
            if before in GATED:
                eng.wait_ge(x_ready, gated_turn(it, before, s))
            elif before:
                lin_taken(eng, it, before, s, "y")

        block = ctx.enter_context(nc.Block())

        @block.sync
        def _(sp):
            for dst, src in ((condT, condT_in), (ident, ident_in), (col, col_in), (row, row_in), (rw, rw_in),
                             (rb, rb_in), (gbrow, gb_in), (cosT, cos_in), (sinT, sin_in), (ind48, ind_in),
                             (onesp, onesp_in), (mqk8, mqk_in), (mkq8, mkq_in), (mc8, mc_in)):
                sp.dma_start(dst if dst is gbrow or dst is row else dst[:], src).then_inc(loaded, 16)
            for i in range(4):
                a, b = NW * i // 4, NW * (i + 1) // 4
                sp.dma_start(W[:, a:b, :], w_in[:, a:b, :]).then_inc(loaded, 16)
            sp.wait_ge(tab_done, 1)
            sp.dma_start(rowb[1:3], rows3).then_inc(rows_in, 16)
            sp.wait_ge(grow_done, 1)
            sp.dma_start(gdram, grow).then_inc(gate_rows_out, 16)
            sp.wait_ge(gate_rows_out, 16)
            with sp.Fori(0, ITERS) as it:
                for s in range(NS):
                    base = it * (NS * GB) + s * GB
                    sp.dma_start(xs[s][:], x_in[:, bass.ds(base, GB), :]).then_inc(x_in_s[s], 16)
                    sp.dma_start(ctxs[s][:], ctx_in[:, bass.ds(base, GB), :]).then_inc(x_in_s[s], 16)
                    sp.dma_start(ctxT[s][:], ctxT_in[:, bass.ds(base, GB), :]).then_inc(x_in_s[s], 16)
                    gsrc = gdram[bass.ds(base, GB), :]
                    sp.dma_start(gbc[s][:], gsrc.partition_broadcast(128)).then_inc(g_in_s[s], 16)
                for s in range(NS):
                    sp.wait_ge(x_ready, gated_turn(it, "x3", s))
                    hold(sp)
                    base = it * (NS * GB) + s * GB
                    sp.dma_start(out[:, bass.ds(base, GB), :], xs[s][:]).then_inc(stored[s], 16)
                for s in range(NS):
                    sp.wait_ge(stored[s], it * 16 + 16)
                    hold(sp)

        @block.gpsimd
        def _(pool):
            nc.gpsimd.memset(mhalf[:], -0.5).then_inc(zeroed, 1)
            for s in range(NS):
                nc.gpsimd.memset(Vp[s][:], 0.0).then_inc(zeroed, 1)
            pool.wait_ge(loaded, 16 * NCONST)
            pool.wait_ge(zeroed, 1 + NS)
            hm = col[:, C_AT["hmask"]:C_AT["hmask"] + H].unsqueeze(2)

            def norm(it, k, s):
                t = C if k == 4 else 128
                eps = 1e-6 if k in (5, 6, 7) else 1e-5
                pool.wait_ge(ln_stats, norm_turn(it, k, s))
                hold(pool)
                nc.gpsimd.tensor_scalar(rstd[s][0:t, 0, :], mv[s][0:t, :, 1], eps, None, ALU.add).then_inc(ln_eps, 1)
                pool.wait_ge(ln_eps, norm_turn(it, k, s))
                nc.gpsimd.tensor_tensor(rstd[s][0:t, 1, :], rstd[s][0:t, 0, :], mhalf[0:t, :],
                                        ALU.pow).then_inc(ln_rstd, 1)

            def keys(it, j, half):
                a, s, b = job_of(j)
                kw = ATT[a]["kw"]
                if a == 0:
                    pool.wait_ge(rope_k, nth(it, 0, s, 1))
                else:
                    lin_taken(pool, it, f"p{a}", s, "k")
                if j >= 3:
                    pool.wait_ge(st_full, job_turn(it, j - 3, 3, 4))
                h0 = 8 * half
                k = kT[s][:, b * kw:(b + 1) * kw].unsqueeze(1)
                nc.gpsimd.tensor_tensor(kbd[:, j % 3, h0:h0 + 8, 0:kw], k.broadcast_to([128, 8, kw]),
                                        hm[:, h0:h0 + 8].broadcast_to([128, 8, kw]), ALU.mult).then_inc(kbd_ready, 1)

            with pool.Fori(0, ITERS) as it:
                for kind, u, s in UNITS:
                    if kind == "START":
                        for j in range(2):
                            keys(it, j, 0)
                            keys(it, j, 1)
                    elif kind == "A" and s in (0, 2) and u + 2 < JOBS:
                        keys(it, u + 2, s // 2)
                    elif kind == "B" and u[1] == "stat":
                        norm(it, int(u[0][1:]), s)

        @block.scalar
        def _(act):
            act.wait_ge(loaded, 16 * NCONST)
            nc.scalar.activation(scondT[:], condT[:], ACT.Silu).then_inc(silu_done, 1)

            def copy_out(it, st, s, job, dst, src, bias=None):
                lin_ready(act, it, st, s, job)
                kw = {} if bias is None else {"bias": bias}
                nc.scalar.activation(dst, src, ACT.Identity, **kw).then_inc(lin_free[lin_bank(st, s, job)], 1)

            def norm(it, k, s):
                st, t = f"l{k}", (C if k == 4 else 128)
                lin_ready(act, it, st, s, "t")
                src = lin_ap(st, s, "t")
                dst = hid[s][:, 5, :] if k == 4 else hT[s][:]
                for b in range(GB):
                    i = nc.scalar.activation(dst[:, b * t:(b + 1) * t], src[:, b * t:(b + 1) * t], ACT.Identity,
                                             bias=tabg[s][:, 2 * k + 1, b:b + 1], scale=tabg[s][:, 2 * k, b:b + 1])
                i.then_inc(lin_free[lin_bank(st, s, "t")], 1)

            def project(it, a, s, part):
                A, st = ATT[a], f"p{a}"
                if a > 0 and part != "v":
                    dst, n, bias = (qT, N, A["bq"]) if part == "q" else (kT, GB * A["kw"], A["bk"])
                    copy_out(it, st, s, part, dst[s][:, 0:n], lin_ap(st, s, part)[:, 0:n], c_(bias) if bias else None)

            def narrow(it, j, half):
                kw = ATT[job_of(j)[0]]["kw"]
                h0 = 8 * half
                act.wait_ge(kbd_ready, job_turn(it, j, half, 2))
                nc.scalar.activation(kbb[:, j % 2, h0:h0 + 8, 0:kw], kbd[:, j % 3, h0:h0 + 8, 0:kw],
                                     ACT.Identity).then_inc(kbb_ready, 1)

            def exps(it, j, g):
                kw = ATT[job_of(j)[0]]["kw"]
                act.wait_ge(st_full, job_turn(it, j, g, 4))
                nc.scalar.activation(P[j % 2][0:kw, 4 * g:4 * g + 4, :],
                                     sct[0:kw, g % 2, :].rearrange("p (h q) -> p h q", h=4),
                                     ACT.Exp, scale=float(HD) ** -0.5).then_inc(st_free, 1)

            def mlp(it, k, s, c):
                st = f"m{k}"
                lin_ready(act, it, st, s, f"h{c}")
                nc.scalar.activation(hid[s][:, c, :], lin_ap(st, s, f"h{c}"), ACT.Gelu_apprx_tanh,
                                     bias=c_("m10" if k == 0 else "m12", c)).then_inc(
                                         lin_free[lin_bank(st, s, f"h{c}")], 1)

            def mixture(it, s, part):
                st = "x3"
                if part == "k":
                    copy_out(it, st, s, "k", kT[s][:, 0:NC], lin_ap(st, s, "k")[:, 0:NC])
                elif part == "s":
                    act.wait_ge(x3_neg, nth(it, 0, s, 1))
                    lin_ready(act, it, st, s, "s")
                    for b in range(GB):
                        i = nc.scalar.activation(xn[s][:, b, 0:C], lin_ap(st, s, "s")[:, b * C:(b + 1) * C], ACT.Exp,
                                                 bias=mx3[s][:, 1, b:b + 1], scale=float(D) ** -0.5)
                    i.then_inc(lin_free[lin_bank(st, s, "s")], 1)
                elif part == "ev":
                    copy_out(it, st, s, "ev", kT[s][:], lin_ap(st, s, "ev"))
                elif part == "lg":
                    copy_out(it, st, s, "lg", lgT[s][:], lin_ap(st, s, "lg", 3), rb[:])
                elif part == "lt":
                    lin_taken(act, it, st, s, "lt")
                    nc.scalar.activation(pr3[s][:, 1], pr3[s][:, 0], ACT.Exp).then_inc(r3_exp, 1)
                elif part[0] == "h":
                    c = int(part[1:])
                    lin_ready(act, it, st, s, part)
                    for b in range(GB):
                        i = nc.scalar.activation(hid[s][:, c, b * T:(b + 1) * T],
                                                 lin_ap(st, s, part)[:, b * T:(b + 1) * T],
                                                 ACT.Silu, bias=tabg[s][:, T_ANCHOR + c, b:b + 1])
                    i.then_inc(lin_free[lin_bank(st, s, part)], 1)
                elif part == "rt":
                    copy_out(it, st, s, "rt", oT[s][:], lin_ap(st, s, "rt"))
                elif part == "g":
                    lin_ready(act, it, st, s, "g")
                    nc.scalar.activation(hid[s][:, 5, :], lin_ap(st, s, "g"), ACT.Sigmoid).then_inc(
                        lin_free[lin_bank(st, s, "g")], 1)

            with act.Fori(0, ITERS) as it:
                for kind, u, s in UNITS:
                    if kind == "START":
                        for j, half in ((0, 0), (0, 1), (1, 0)):
                            narrow(it, j, half)
                    elif kind == "A":
                        if s == 0 and u + 1 < JOBS:
                            narrow(it, u + 1, 1)
                        exps(it, u, s)
                        if s == 3 and u + 2 < JOBS:
                            narrow(it, u + 2, 0)
                    elif kind == "B":
                        st, part = u
                        k = int(st[1:])
                        if u == ("l0", "t"):
                            act.wait_ge(group_tab, nth(it, 0, s, 1))
                        if part == "t":
                            norm(it, k, s)
                        elif st[0] == "p":
                            project(it, k, s, part)
                        elif st[0] == "m" and part != "y":
                            mlp(it, k, s, int(part[1:]))
                        elif st == "x3":
                            mixture(it, s, part)

        @block.vector
        def _(dve):
            v = nc.vector
            n_setup = [0]

            def chain(i):
                n_setup[0] += 1
                i.then_inc(setup_dve, 1)
                dve.wait_ge(setup_dve, n_setup[0])

            v.memset(rowb[:], 0.0).then_inc(lin_free[0], 1)
            for s in range(NS):
                v.memset(mcg[s][:], 0.0)
            v.memset(rden[:], 0.0).then_inc(lin_free[1], 1)
            v.memset(oneb[:], 1.0).then_inc(s_free, 2)
            v.memset(mhl[:], 0.0).then_inc(st_free, 2)
            chain(v.memset(mx[:], 0.0))
            v.memset(mT[:], 0.0).then_inc(av_free, 1)
            dve.wait_ge(loaded, 16 * NCONST)
            v.tensor_copy(identb[:], ident[:])
            v.tensor_copy(indb[:], ind48[:].unsqueeze(2).broadcast_to([128, H, 128]))
            for dst, src in ((mqk, mqk8), (mkq, mkq8), (mcb, mc8)):
                v.tensor_scalar(dst[:], src[:], -1.0, BIG, ALU.add, ALU.mult)
            for i in range(2):
                wv = wblk("qkv0", i).rearrange("p (h t j) -> p h t j", t=2, j=4)
                rv = Wrot[:, i, :].rearrange("p (h t j) -> p h t j", t=2, j=4)
                v.tensor_scalar(rv[:, :, 0, :], wv[:, :, 1, :], -1.0, None, ALU.mult)
                i_ = v.tensor_copy(rv[:, :, 1, :], wv[:, :, 0, :])
            chain(i_)
            dve.wait_ge(mods_done, 1)
            chain(v.tensor_tensor(modv[:], lin[:, 0, 0:21 * B].rearrange("p (c b) -> p c b", b=B),
                                  col[:, 0:21].unsqueeze(2).broadcast_to([128, 21, B]), ALU.add))
            for k, site in enumerate(NORMS):
                if site is None:
                    for r, nm in enumerate(("g2", "b2") if k == 6 else ("gam", "bet")):
                        v.tensor_copy(tab[:, 2 * k + r, :], c_(nm).broadcast_to([128, B]))
                    continue
                shift, scale, wcol = site
                w = c_(wcol) if wcol else 1.0
                v.tensor_scalar(tab[:, 2 * k, :], modv[:, scale, :], 1.0, w, ALU.add, ALU.mult)
                v.tensor_copy(tab[:, 2 * k + 1, :], modv[:, shift, :])
            v.tensor_copy(tab[:, T_ANCHOR:T_ANCHOR + 7, :], modv[:, 14:21, :])
            chain(v.tensor_copy(tab[:, T_COND, :], condT[:]))
            dve.wait_ge(gates_mm, 1)
            for i in range(NG):
                i_ = v.tensor_tensor(grow[:, i * 128:(i + 1) * 128],
                                     (lin[0:B, 1, i * 128:(i + 1) * 128] if i < 4 else avp[0:B, 0:128]),
                                     gbrow[:, i * 128:(i + 1) * 128], ALU.add)
            i_.then_inc(grow_done, 1)
            dve.wait_ge(bias_mm, 1)
            for i, r in enumerate((R_P1, R_S2, R_C2)):
                i_ = v.tensor_tensor(row[:, r, :], sco[0:1, 0, i * 128:(i + 1) * 128], row[:, r, :], ALU.add)
            chain(i_)
            chain(v.tensor_copy(rowb[0:1], row))
            chain(v.tensor_tensor(rowr[:, 0], row, rowb[0:1], ALU.subtract))
            chain(v.tensor_copy(rows3[:, 0], rowr[:, 0]))
            chain(v.tensor_tensor(rowr[:, 1], rowr[:, 0], rows3[:, 0], ALU.subtract))
            v.tensor_copy(rows3[:, 1], rowr[:, 1]).then_inc(tab_done, 1)

            def statistics(it, k, s):
                t = C if k == 4 else 128
                src = ctxs[s] if k == 4 else xs[s]
                if k == 0:
                    base = it * (NS * GB) + s * GB
                    dve.wait_ge(x_in_s[s], it * 48 + 48)
                    v.tensor_copy(tabg[s][:], tab[:, :, bass.ds(base, GB)])
                    v.tensor_copy(mcg[s][0:1].rearrange("p b c -> p (b c)"),
                                  mcb[:, bass.ds(base * C, GB * C)]).then_inc(group_tab, 1)
                if k != 4:
                    res_ready(dve, it, f"l{k}", s)
                for b in range(GB):
                    i = v.bn_stats(bst[s][0:t, b, :], src[0:t, b, :])
                i.then_inc(ln_bn, 1)
                dve.wait_ge(ln_bn, norm_turn(it, k, s))
                hold(dve)
                for b in range(GB):
                    i = v.bn_aggr(mv[s][0:t, b, :], bst[s][0:t, b, :])
                i.then_inc(ln_stats, 1)

            def apply(it, k, s):
                t = C if k == 4 else 128
                src = ctxs[s] if k == 4 else xs[s]
                dve.wait_ge(ln_stats, norm_turn(it, k, s))
                dve.wait_ge(ln_rstd, norm_turn(it, k, s))
                for b in range(GB):
                    i = v.tensor_scalar((ctxs if k == 4 else xn)[s][0:t, b, :], src[0:t, b, :], mv[s][0:t, b, 0:1],
                                        rstd[s][0:t, 1, b:b + 1], ALU.subtract, ALU.mult)
                i.then_inc(ln_xn, 1)

            def values(it, a, s):
                st, kw = f"p{a}", ATT[a]["kw"]
                lin_ready(dve, it, st, s, "v")
                v.tensor_copy(diag(s, kw), lin_ap(st, s, "v", kw).rearrange(
                    "p (c h d) -> p c h d", h=4, d=8)).then_inc(lin_free[lin_bank(st, s, "v")], 1)

            def project(it, a, s, part):
                st = f"p{a}"
                if part == "v":
                    values(it, a, s)
                    return
                if a == 0:
                    r, dst, done = (0, qT, rope_q) if part == "q" else (1, kT, rope_k)
                    for u, (job, tbl) in enumerate(((part + "a", cosT), (part + "b", sinT))):
                        lin_ready(dve, it, st, s, job)
                        v.tensor_tensor(t1[s][:, 2 * r + u, :].rearrange("p (b t) -> p b t", b=GB),
                                        lin_ap(st, s, job).rearrange("p (b t) -> p b t", b=GB),
                                        tbl[:].unsqueeze(1).broadcast_to([128, GB, T]), ALU.mult).then_inc(
                                            lin_free[lin_bank(st, s, job)], 1)
                    lin_taken(dve, it, st, s, part + "a")
                    lin_taken(dve, it, st, s, part + "b")
                    v.tensor_tensor(dst[s][:], t1[s][:, 2 * r, :], t1[s][:, 2 * r + 1, :], ALU.add).then_inc(done, 1)
                if part == "q":
                    if a == 0:
                        dve.wait_ge(rope_q, nth(it, 0, s, 1))
                    else:
                        lin_taken(dve, it, st, s, "q")
                    v.tensor_copy(qb[s][:], qT[s][:]).then_inc(qb_ready, 1)

            def maxima(it, j, g):
                kw = ATT[job_of(j)[0]]["kw"]
                dve.wait_ge(s_full, job_turn(it, j, g, 4))
                v.tensor_reduce(mx[:, 4 * g:4 * g + 4],
                                sco[:, g % 2, 0:4 * kw].rearrange("p (h k) -> p h k", h=4), AX,
                                ALU.max).then_inc(s_free, 1)

            def split(it, j):
                dve.wait_ge(s_free, job_turn(it, j, 3, 4) + 2)
                v.tensor_copy(mhl[:, 0:16], mx[:]).then_inc(mhi_ready, 1)
                dve.wait_ge(mhi_ready, job_turn(it, j))
                v.tensor_tensor(mhl[:, 32:48], mx[:], mhl[:, 0:16], ALU.subtract).then_inc(m_split, 1)

            def turned(it, j):
                dve.wait_ge(mt_full, job_turn(it, j))
                v.tensor_copy(mT[:], mtp[:, 0:T]).then_inc(mt_ready, 1)

            def normalise(it, j):
                _, s, b = job_of(j)
                n = job_turn(it, j)
                dve.wait_ge(av_full, n)
                v.reciprocal(rden[:], avp[:, T:2 * T]).then_inc(rden_ready, 1)
                dve.wait_ge(rden_ready, n)
                v.tensor_tensor(oT[s][:, b * T:(b + 1) * T], avp[:, 0:T], rden[:], ALU.mult).then_inc(av_free, 1)

            def add_result(it, st, s, gate):
                lin_ready(dve, it, st, s, "y")
                y = lin_ap(st, s, "y").rearrange("p (b d) -> p b d", b=GB)
                free = lin_free[lin_bank(st, s, "y")]
                if gate is None:
                    v.tensor_tensor(xs[s][:], xs[s][:], y, ALU.add).then_inc(free, 1)
                else:
                    v.tensor_tensor(t1[s][:, 0, :].rearrange("p (b d) -> p b d", b=GB), y, gate, ALU.mult).then_inc(free, 1)
                    lin_taken(dve, it, st, s, "y")
                    v.tensor_tensor(xs[s][:], xs[s][:], t1[s][:, 0, :].rearrange("p (b d) -> p b d", b=GB),
                                    ALU.add).then_inc(x_ready, 1)

            def mixture(it, s, part):
                st = "x3"
                one = nth(it, 0, s, 1)
                if part == "q":
                    lin_ready(dve, it, st, s, "q")
                    v.tensor_copy(qT[s][:], lin_ap(st, s, "q")).then_inc(lin_free[lin_bank(st, s, "q")], 1)
                elif part == "v":
                    lin_ready(dve, it, st, s, "v")
                    v.tensor_copy(hid[s][0:C, 6, :], lin_ap(st, s, "v", C)).then_inc(lin_free[lin_bank(st, s, "v")], 1)
                elif part == "s":
                    lin_ready(dve, it, st, s, "s")
                    v.tensor_reduce(mx3[s][:, 0, :], lin_ap(st, s, "s")[:, 0:NC].rearrange("p (b c) -> p b c", b=GB), AX,
                                    ALU.max).then_inc(x3_max, 1)
                    dve.wait_ge(x3_max, one)
                    v.tensor_scalar(mx3[s][:, 1, :], mx3[s][:, 0, :], -float(D) ** -0.5, None,
                                    ALU.mult).then_inc(x3_neg, 1)
                elif part == "pt":
                    lin_taken(dve, it, st, s, "s")
                    v.tensor_reduce(mx3[s][:, 2, :], xn[s][:, :, 0:C], AX, ALU.add).then_inc(x3_sum, 1)
                    dve.wait_ge(x3_sum, one)
                    v.reciprocal(mx3[s][:, 3, :], mx3[s][:, 2, :]).then_inc(x3_rec, 1)
                    dve.wait_ge(x3_rec, one)
                    v.tensor_tensor(xn[s][:, :, 0:C], xn[s][:, :, 0:C],
                                    mx3[s][:, 3, :].unsqueeze(2).broadcast_to([128, GB, C]), ALU.mult).then_inc(x3_p, 1)
                    lin_ready(dve, it, st, s, "pt")
                    v.tensor_copy(oT[s][0:C, :], lin_ap(st, s, "pt", C)).then_inc(lin_free[lin_bank(st, s, "pt")], 1)
                elif part == "lt":
                    lin_ready(dve, it, st, s, "lt")
                    lt = lin_ap(st, s, "lt")[:, 0:3 * GB].rearrange("p (b e) -> p b e", e=3)
                    v.tensor_reduce(mx3[s][:, 0, :], lt, AX, ALU.max).then_inc(r3_max, 1)
                    dve.wait_ge(r3_max, one)
                    v.tensor_tensor(pr3[s][:, 0], lt, mx3[s][:, 0, :].unsqueeze(2).broadcast_to([128, GB, 3]),
                                    ALU.subtract).then_inc(lin_free[lin_bank(st, s, "lt")], 1)
                elif part == "h2":
                    dve.wait_ge(r3_exp, one)
                    v.tensor_reduce(mx3[s][:, 1, :], pr3[s][:, 1], AX, ALU.add).then_inc(r3_sum, 1)
                    dve.wait_ge(r3_sum, one)
                    v.reciprocal(mx3[s][:, 2, :], mx3[s][:, 1, :]).then_inc(r3_rec, 1)
                    dve.wait_ge(r3_rec, one)
                    v.tensor_tensor(pr3[s][:, 2], pr3[s][:, 1], mx3[s][:, 2, :].unsqueeze(2).broadcast_to([128, GB, 3]),
                                    ALU.mult).then_inc(r3_p, 1)
                elif part[0] == "e" and part != "ev":
                    e = int(part[1:])
                    lin_ready(dve, it, st, s, part)
                    if e == 0:
                        dve.wait_ge(r3_p, one)
                    else:
                        lin_taken(dve, it, st, s, f"e{e - 1}")
                    src = lin_ap(st, s, part)
                    for b in range(GB):
                        p = pr3[s][:, 2, b, e:e + 1]
                        if e == 0:
                            i = v.tensor_scalar(xn[s][:, b, :], src[:, b * D:(b + 1) * D], p, None, ALU.mult)
                        else:
                            i = v.scalar_tensor_tensor(out=xn[s][:, b, :], in0=src[:, b * D:(b + 1) * D], scalar=p,
                                                       in1=xn[s][:, b, :], op0=ALU.mult, op1=ALU.add)
                    i.then_inc(lin_free[lin_bank(st, s, part)], 1)
                elif part == "y":
                    lin_taken(dve, it, st, s, "g")
                    add_result(it, st, s, hid[s][:, 5, :].rearrange("p (b d) -> p b d", b=GB))

            with dve.Fori(0, ITERS) as it:
                for kind, u, s in UNITS:
                    if kind == "START":
                        for g in range(4):
                            maxima(it, 0, g)
                        split(it, 0)
                        turned(it, 0)
                    elif kind == "A":
                        if u + 1 < JOBS:
                            maxima(it, u + 1, s)
                        if s == 3:
                            if u + 1 < JOBS:
                                split(it, u + 1)
                                turned(it, u + 1)
                            if u > 0:
                                normalise(it, u - 1)
                    elif kind == "END":
                        normalise(it, JOBS - 1)
                    elif kind == "B":
                        st, part = u
                        k = int(st[1:])
                        if part == "stat":
                            statistics(it, k, s)
                        elif part == "apply":
                            apply(it, k, s)
                        elif st[0] == "p":
                            project(it, k, s, part)
                        elif st[0] in "om" and part == "y":
                            if st == "o0":
                                dve.wait_ge(g_in_s[s], it * 16 + 16)
                            g = gate_of.get(st)
                            add_result(it, st, s, None if g is None else gbc[s][:, :, g * 128:(g + 1) * 128])
                        elif st == "x3":
                            mixture(it, s, part)

        @block.tensor
        def _(pe):
            mm = nc.tensor.matmul
            pe.wait_ge(loaded, 16 * NCONST)
            pe.wait_ge(silu_done, 1)
            pe.wait_ge(lin_free[0], 1)
            pe.wait_ge(lin_free[1], 1)
            for c, (blk, silu) in enumerate(MODS):
                i = mm(lin[:, 0, c * B:(c + 1) * B], W[:, blk, :], (scondT if silu else condT)[:], start=True, stop=True)
            i.then_inc(mods_done, 1)
            for c, (blk, silu) in enumerate(GATES):
                dst = lin[0:B, 1, c * 128:(c + 1) * 128] if c < 4 else avp[0:B, 0:128]
                i = mm(dst, (scondT if silu else condT)[:], W[:, blk, :], start=True, stop=True)
            i.then_inc(gates_mm, 1)
            for c, (cn, wn) in enumerate((("bv1", "wp1"), ("vb2", "so2"), ("cv2", "co2"))):
                i = mm(sco[0:1, 0, c * 128:(c + 1) * 128], c_(cn), wblk(wn), start=True, stop=True)
            i.then_inc(bias_mm, 1)
            pe.wait_ge(rows_in, 16)

            def take(it, st, s, job):
                pe.wait_ge(lin_free[lin_bank(st, s, job)], lin_turn(it, st, s, job))

            def give(st, s, job, i):
                i.then_inc(lin_full[lin_bank(st, s, job)], 1)

            def linear(it, st, s, job, parts, n, m=128):
                take(it, st, s, job)
                for c, (w, a) in enumerate(parts):
                    i = mm(lin_ap(st, s, job, m)[:, 0:n], w, a, start=(c == 0), stop=(c == len(parts) - 1))
                give(st, s, job, i)

            def tokens(it, st, s, job, src, wts, bias=None, t=T):
                take(it, st, s, job)
                o = lin_ap(st, s, job, t)
                if bias is not None:
                    mm(o.rearrange("p (b d) -> p b d", b=GB), oneb[:, 0:t],
                       rowb[:, bias, :].unsqueeze(1).broadcast_to([128, GB, 128]), start=True, stop=False,
                       skip_group_check=True)
                for b in range(GB):
                    for c, (a, w) in enumerate(zip(src, wts)):
                        i = mm(o[:, b * 128:(b + 1) * 128], a[:, b * t:(b + 1) * t], w,
                               start=(c == 0 and bias is None), stop=(c == len(wts) - 1), skip_group_check=True)
                give(st, s, job, i)

            def norm(it, k, s):
                st, t = f"l{k}", (C if k == 4 else 128)
                take(it, st, s, "t")
                pe.wait_ge(ln_xn, norm_turn(it, k, s))
                for b in range(GB):
                    i = nc.tensor.transpose(lin_ap(st, s, "t")[:, b * t:(b + 1) * t],
                                            (ctxs if k == 4 else xn)[s][0:t, b, :], ident[0:t, 0:t])
                give(st, s, "t", i)

            def project(it, a, s, part):
                st, A = f"p{a}", ATT[a]
                n = GB * A["kw"]
                own = a in (0, 3)
                norm_of = {0: "l0", 1: "l1", 2: "l3", 3: "l5", 4: "l6"}[a]
                if part == "q" or own:
                    lin_taken(pe, it, norm_of, s, "t")
                elif a == 2:
                    lin_taken(pe, it, "l4", s, "t")
                h = hT[s][:]
                kv = h if own else (hid[s][:, 5, 0:NC] if a == 2 else ctxT[s][:].rearrange("p b c -> p (b c)"))
                if a == 0 and part != "v":
                    i = 0 if part == "q" else 1
                    linear(it, st, s, part + "a", [(wblk("qkv0", i), h)], N)
                    linear(it, st, s, part + "b", [(Wrot[:, i, :], h)], N)
                elif part == "q":
                    linear(it, st, s, "q", [(wblk(A["q"]), h)], N)
                elif part == "k":
                    linear(it, st, s, "k", [(W[:, KBLK[a], :], kv)], n)
                else:
                    tokens(it, st, s, "v", [kv], [W[:, VBLK[a], :]], t=A["kw"])

            def scores(it, j, g):
                a, s, b = job_of(j)
                kw = ATT[a]["kw"]
                if b == 0 and g == 0:
                    pe.wait_ge(qb_ready, nth(it, a, s, NAT))
                    if a == 0:
                        pe.wait_ge(rope_q, nth(it, 0, s, 1))
                if g % 2 == 0:
                    pe.wait_ge(kbb_ready, job_turn(it, j, g // 2, 2))
                pe.wait_ge(s_free, job_turn(it, j, g, 4))
                o = sco[:, g % 2, 0:4 * kw].rearrange("p (h k) -> p h k", h=4)
                i = mm(o, qb[s][:, b * T:(b + 1) * T], kbb[:, j % 2, 4 * g:4 * g + 4, 0:kw], start=True, stop=(a > 1))
                if a == 0:
                    i = mm(o, identb[:], mqk[:].unsqueeze(1).broadcast_to([128, 4, T]), start=False, stop=True)
                elif a == 1:
                    i = mm(o, oneb[:, 0:T], mcg[s][:, b, :].unsqueeze(1).broadcast_to([128, 4, C]),
                           start=False, stop=True)
                i.then_inc(s_full, 1)

            def turn(it, j):
                pe.wait_ge(m_split, job_turn(it, j))
                nc.tensor.transpose(mtp[:, 0:T], mhl[:], identb[:]).then_inc(mt_full, 1)

            def scores_t(it, j, g):
                a, s, b = job_of(j)
                kw = ATT[a]["kw"]
                if g == 0:
                    pe.wait_ge(mt_ready, job_turn(it, j))
                pe.wait_ge(st_free, job_turn(it, j, g, 4))
                o = sct[0:kw, g % 2, :]
                for hh in range(4):
                    mm(o[:, hh * T:(hh + 1) * T], kbd[:, j % 3, 4 * g + hh, 0:kw], qT[s][:, b * T:(b + 1) * T],
                       start=(hh == 0), stop=False, skip_group_check=True)
                if a == 0:
                    mm(o.rearrange("p (h q) -> p h q", h=4), identb[:], mkq[:].unsqueeze(1).broadcast_to([128, 4, T]),
                       start=False, stop=False, skip_group_check=True)
                elif a == 1:
                    mm(o, mcg[s][:, b, :], oneb[:], start=False, stop=False, skip_group_check=True)
                for hh in range(4):
                    i = mm(o[:, hh * T:(hh + 1) * T], indb[:, 4 * g + hh, 0:kw], mT[:], start=False,
                           stop=(hh == 3), skip_group_check=True)
                i.then_inc(st_full, 1)

            def av(it, j, part):
                a, s, b = job_of(j)
                kw = ATT[a]["kw"]
                if part == 0:
                    lin_taken(pe, it, f"p{a}", s, "v")
                    pe.wait_ge(st_free, job_turn(it, j, 3, 4) + 2)
                    pe.wait_ge(av_free, job_turn(it, j))
                for hh in range(4):
                    for g in range(4):
                        w = Vp[s][0:kw, b, 4 * g + hh, :] if part == 0 else onesp[0:kw, hh, :]
                        i = mm(avp[32 * g:32 * g + 32, part * T:(part + 1) * T], w,
                               P[j % 2][0:kw, 4 * g + hh, :], start=(hh == 0), stop=(hh == 3), skip_group_check=True)
                if part == 1:
                    i.then_inc(av_full, 1)

            def outproj(it, a, s):
                pe.wait_ge(av_free, job_turn(it, (a * NS + s) * GB + GB - 1) + 1)
                tokens(it, f"o{a}", s, "y", [oT[s][:]], [wblk(ATT[a]["o"])], ATT[a]["row"])

            def mlp(it, k, s, part):
                st = f"m{k}"
                w1, w2 = ("m10", "m20") if k == 0 else ("m12", "m22")
                if part != "y":
                    if part == "h0":
                        lin_taken(pe, it, "l2" if k == 0 else "l7", s, "t")
                    linear(it, st, s, part, [(wblk(w1, int(part[1:])), hT[s][:])], N)
                    return
                for c in range(4):
                    lin_taken(pe, it, st, s, f"h{c}")
                tokens(it, st, s, "y", [hid[s][:, c, :] for c in range(4)], [wblk(w2, c) for c in range(4)],
                       R_M0 if k == 0 else R_M2)

            def mixture(it, s, part):
                st = "x3"
                h, ev, ct = hT[s][:], kT[s][:], ctxT[s][:].rearrange("p b c -> p (b c)")
                if part == "q":
                    lin_taken(pe, it, "l8", s, "t")
                    linear(it, st, s, "q", [(wblk("q3"), h)], N)
                elif part == "k":
                    linear(it, st, s, "k", [(wblk("k3"), ct)], NC)
                elif part == "v":
                    tokens(it, st, s, "v", [ct], [wblk("v3")], t=C)
                elif part == "s":
                    for job in ("q", "k"):
                        lin_taken(pe, it, st, s, job)
                    take(it, st, s, "s")
                    for b in range(GB):
                        i = mm(lin_ap(st, s, "s")[:, b * C:(b + 1) * C], qT[s][:, b * T:(b + 1) * T],
                               kT[s][:, b * C:(b + 1) * C], start=True, stop=True)
                    give(st, s, "s", i)
                elif part == "pt":
                    take(it, st, s, "pt")
                    pe.wait_ge(x3_p, nth(it, 0, s, 1))
                    for b in range(GB):
                        i = nc.tensor.transpose(lin_ap(st, s, "pt", C)[:, b * T:(b + 1) * T], xn[s][:, b, 0:C], ident[:])
                    give(st, s, "pt", i)
                elif part == "ev":
                    for job in ("v", "pt"):
                        lin_taken(pe, it, st, s, job)
                    take(it, st, s, "ev")
                    for b in range(GB):
                        i = mm(lin_ap(st, s, "ev")[:, b * T:(b + 1) * T], hid[s][0:C, 6, b * D:(b + 1) * D],
                               oT[s][0:C, b * T:(b + 1) * T], start=True, stop=True)
                    give(st, s, "ev", i)
                elif part == "lg":
                    lin_taken(pe, it, st, s, "ev")
                    anchor = tabg[s][:, T_COND, :].unsqueeze(2).broadcast_to([128, GB, T])
                    linear(it, st, s, "lg", [(rw[:, 0, :], h), (rw[:, 1, :], ev), (rw[:, 2, :], anchor)], N, m=3)
                elif part == "lt":
                    lin_taken(pe, it, st, s, "lg")
                    take(it, st, s, "lt")
                    hold(pe)
                    for b in range(GB):
                        i = nc.tensor.transpose(lin_ap(st, s, "lt")[:, 3 * b:3 * b + 3], lgT[s][:, b * T:(b + 1) * T],
                                                ident[0:3, 0:3])
                    give(st, s, "lt", i)
                elif part[0] == "h":
                    c = int(part[1:])
                    e, r = c // 2, c % 2
                    w0, w1 = (wblk("e1", 6 * e + r), wblk("e1", 6 * e + 2 + r)) if c < 6 else (wblk("g1", 0), wblk("g1", 1))
                    linear(it, st, s, part, [(w0, h), (w1, ev)], N)
                elif part[0] == "e":
                    e = int(part[1:])
                    for r in range(2):
                        lin_taken(pe, it, st, s, f"h{2 * e + r}")
                    tokens(it, st, s, part, [hid[s][:, 2 * e + r, :] for r in range(2)],
                           [wblk("e2", 2 * e + r) for r in range(2)], R_E + e)
                elif part == "rt":
                    take(it, st, s, "rt")
                    lin_taken(pe, it, st, s, "e2")
                    for b in range(GB):
                        i = nc.tensor.transpose(lin_ap(st, s, "rt")[:, b * T:(b + 1) * T], xn[s][:, b, :], ident[:])
                    give(st, s, "rt", i)
                elif part == "g":
                    lin_taken(pe, it, st, s, "h6")
                    tokens(it, st, s, "g", [hid[s][:, 6, :]], [wblk("g2")], R_GATE)
                elif part == "y":
                    lin_taken(pe, it, st, s, "rt")
                    tokens(it, st, s, "y", [oT[s][:]], [wblk("ow3")], R_OUT)

            with pe.Fori(0, ITERS) as it:
                for kind, u, s in UNITS:
                    if kind == "START":
                        for g in range(4):
                            scores(it, 0, g)
                        turn(it, 0)
                    elif kind == "A":
                        if s == 3 and u + 1 < JOBS:
                            scores(it, u + 1, s)
                        scores_t(it, u, s)
                        if s < 3 and u + 1 < JOBS:
                            scores(it, u + 1, s)
                        if s == 3:
                            if u > 0:
                                av(it, u - 1, 0)
                            if u + 1 < JOBS:
                                turn(it, u + 1)
                            if u > 0:
                                av(it, u - 1, 1)
                    elif kind == "END":
                        av(it, JOBS - 1, 0)
                        av(it, JOBS - 1, 1)
                    elif kind == "B":
                        st, part = u
                        k = int(st[1:])
                        if u == ("l0", "t") or u == ("p1", "k"):
                            pe.wait_ge(group_tab, nth(it, 0, s, 1))
                        if part == "t":
                            norm(it, k, s)
                        elif st[0] == "p":
                            project(it, k, s, part)
                        elif st[0] == "o":
                            outproj(it, k, s)
                        elif st[0] == "m":
                            mlp(it, k, s, part)
                        elif st == "x3":
                            mixture(it, s, part)


def shape_constants():
    inv = 1.0 / 10000.0 ** (np.arange(0, HD, 2, dtype=np.float32) / HD)
    freqs = np.outer(np.arange(HALF, dtype=np.float32), inv)
    emb = np.concatenate([freqs, freqs], axis=-1)
    cos = np.tile(np.cos(emb).astype(np.float32).T, (H, 2))
    sin = np.tile(np.sin(emb).astype(np.float32).T, (H, 2))
    ind = np.zeros((128, H), np.float32)
    ind[np.arange(H), np.arange(H)] = -1.0
    ind[32 + np.arange(H), np.arange(H)] = -1.0
    onesp = np.zeros((128, 4, 32), np.float32)
    for hh in range(4):
        onesp[:, hh, 8 * hh:8 * hh + 8] = 1.0
    hmask = (np.arange(128)[:, None] // HD == np.arange(H)[None, :]).astype(np.float32)
    return np.ascontiguousarray(cos), np.ascontiguousarray(sin), np.eye(128, dtype=np.float32), ind, onesp, hmask


def kernel(**inputs):
    import concourse.bacc as bacc
    from concourse.bass_utils import run_bass_kernel_spmd

    a = {k: np.asarray(v) for k, v in inputs.items()}
    cos, sin, ident, ind, onesp, hmask = shape_constants()

    def blocks(w):
        r, c = w.shape[0] // 128, w.shape[1] // 128
        return w.reshape(r, 128, c, 128).transpose(1, 0, 2, 3).reshape(128, r * c, 128)

    e1, e2 = a["L3_xcond_e_w1"], a["L3_xcond_e_w2"]
    parts = {"ada0": a["L0_xcond_adaLN_W"], "qkv0": a["L0_xcond_qkv_W"], "ao0": a["L0_xcond_attn_out_W"],
             "cq0": a["L0_xcond_cq_W"], "ck0": a["L0_xcond_ck_W"], "cv0": a["L0_xcond_cv_W"],
             "co0": a["L0_xcond_co_W"], "m10": a["L0_xcond_mlp_W1"], "m20": a["L0_xcond_mlp_W2"],
             "wq1": a["L1_xcond_Wq"], "wkv1": a["L1_xcond_Wkv"], "wp1": a["L1_xcond_Wp"],
             "ssq": a["L1_xcond_Wss_q"], "sskv": a["L1_xcond_Wss_kv"], "ada2": a["L2_xcond_ada_w"],
             "qkv2": a["L2_xcond_qkv_w"], "so2": a["L2_xcond_self_o_w"], "q2": a["L2_xcond_q_w"],
             "kv2": a["L2_xcond_kv_w"], "co2": a["L2_xcond_cross_o_w"], "m12": a["L2_xcond_mlp_w1"],
             "m22": a["L2_xcond_mlp_w2"], "q3": a["L3_xcond_Wq"], "k3": a["L3_xcond_Wk"], "v3": a["L3_xcond_Wv"],
             "g1": a["L3_xcond_gate_w1"], "g2": a["L3_xcond_gate_w2"], "ow3": a["L3_xcond_out_w"]}
    wl = []
    for name, n in W_PARTS:
        if name == "e1":
            wl += [blocks(e1[e]) for e in range(3)]
        elif name == "e2":
            wl += [blocks(e2[e]) for e in range(3)]
        else:
            wl.append(blocks(parts[name]))
            assert wl[-1].shape[1] == n
    w = np.ascontiguousarray(np.concatenate(wl, axis=1))

    def cols(v):
        return v.reshape(-1, 128).T

    b0, b2 = a["L0_xcond_adaLN_b"].reshape(9, 128), a["L2_xcond_ada_b"].reshape(6, 128)
    modb = np.concatenate([b0[[0, 1, 3, 4, 6, 7]], a["L1_xcond_bss_q"].reshape(2, 128),
                           a["L1_xcond_bss_kv"].reshape(2, 128), b2[[0, 1, 3, 4]],
                           a["L3_xcond_e_b1"].reshape(6, 128), a["L3_xcond_gate_b1"].reshape(1, 128)])
    cparts = {"modb": modb, "n1": a["L0_xcond_norm1_w"], "nc": a["L0_xcond_normc_w"], "n2": a["L0_xcond_norm2_w"],
              "g2": a["L2_xcond_norm2_g"], "b2": a["L2_xcond_norm2_b"], "gam": a["L3_xcond_ln_gamma"],
              "bet": a["L3_xcond_ln_beta"], "bq1": a["L1_xcond_bq"], "bk1": a["L1_xcond_bkv"][:128],
              "bv1": a["L1_xcond_bkv"][128:], "qb2": a["L2_xcond_qkv_b"][:128], "kb2": a["L2_xcond_qkv_b"][128:256],
              "vb2": a["L2_xcond_qkv_b"][256:], "cq2": a["L2_xcond_q_b"], "ck2": a["L2_xcond_kv_b"][:128],
              "cv2": a["L2_xcond_kv_b"][128:], "m10": a["L0_xcond_mlp_b1"], "m12": a["L2_xcond_mlp_b1"]}
    col = np.ascontiguousarray(np.concatenate([hmask if n == "hmask" else cols(cparts[n]) for n, _ in C_PARTS], axis=1))
    row = np.ascontiguousarray(np.stack([a["L0_xcond_mlp_b2"], a["L1_xcond_bp"], a["L2_xcond_self_o_b"],
                                         a["L2_xcond_cross_o_b"], a["L2_xcond_mlp_b2"], a["L3_xcond_out_b"],
                                         a["L3_xcond_gate_b2"], *a["L3_xcond_e_b2"]])[None])
    gb = np.concatenate([b0[2], b0[5], b0[8], b2[2], b2[5]])
    gb = np.ascontiguousarray(np.broadcast_to(gb[None], (B, NG * 128)))
    rw = np.ascontiguousarray(a["L3_xcond_router_W"].reshape(3, 128, 3).transpose(1, 0, 2))
    rb = np.ascontiguousarray(a["L3_xcond_router_b"].reshape(3, 1))
    m2, mc = a["mask_SxS_bk0"], a["mask_BxS2_bf1"]
    arrays = [("x", np.ascontiguousarray(a["x"].transpose(1, 0, 2))),
              ("ctx", np.ascontiguousarray(a["ctx_1024"].transpose(1, 0, 2))),
              ("ctxT", np.ascontiguousarray(a["ctx_1024"].transpose(2, 0, 1))),
              ("condT", np.ascontiguousarray(a["cond_1024"].T)), ("w", w), ("col", col), ("row", row), ("rw", rw),
              ("rb", rb), ("gb", gb), ("mqk", np.ascontiguousarray(m2)), ("mkq", np.ascontiguousarray(m2.T)),
              ("mc", np.ascontiguousarray(mc.reshape(1, B * C))), ("cos", cos), ("sin", sin),
              ("ident", ident), ("ind", ind), ("onesp", onesp)]
    nc = bacc.Bacc("TRN2", target_bir_lowering=False, num_devices=1)
    ins, args = {}, []
    for name, arr in arrays:
        ins[f"in_{name}"] = arr
        dt = U8 if arr.dtype == bool else mybir.dt.from_np(arr.dtype)
        args.append(nc.dram_tensor(f"in_{name}", arr.shape, dt, kind="ExternalInput").ap())
    out = nc.dram_tensor("out", (T, B, D), F32, kind="ExternalOutput").ap()
    build(nc, *args, out)
    r = run_bass_kernel_spmd(nc, [ins], core_ids=[0])
    return np.ascontiguousarray(r.results[0]["out"].transpose(1, 0, 2))
```

```python
from contextlib import ExitStack

import numpy as np

import concourse.bass as bass
from concourse import mybir

F32 = mybir.dt.float32
BF16 = mybir.dt.bfloat16
U8 = mybir.dt.uint8
ACT = mybir.ActivationFunctionType
ALU = mybir.AluOpType
AX = mybir.AxisListType.X

B, T, D, C = 16, 128, 128, 77
H, HD = 16, 8
GB = 4
NS = 2
ITERS = B // (GB * NS)
N = GB * T
NC = GB * C
HALF = T // 2
BIG = 2.0 ** 100

S_PARTS = [("ada0", 9), ("ssq", 2), ("sskv", 2), ("ada2", 6), ("e1a", 6), ("g1a", 1)]
W_PARTS = [("qkv0", 3), ("wp1", 1), ("so2", 1), ("co2", 1), ("ck0", 1), ("cv0", 1), ("ao0", 1), ("cq0", 1),
           ("co0", 1), ("wkv1", 2), ("m10", 4), ("m20", 4), ("wq1", 1), ("qkv2", 3), ("q2", 1), ("kv2", 2),
           ("m12", 4), ("m22", 4), ("q3", 1), ("k3", 1), ("v3", 1), ("e1", 12), ("e2", 6), ("g1", 2), ("g2", 1),
           ("ow3", 1)]
NW_FIRST = 8


def block_table(parts):
    at, n = {}, 0
    for name, k in parts:
        at[name] = n
        n += k
    return at, n


S_AT, NSW = block_table(S_PARTS)
W_AT, NW = block_table(W_PARTS)

C_PARTS = [("modb", 21), ("n1", 1), ("nc", 1), ("n2", 1), ("g2", 1), ("b2", 1), ("gam", 1), ("bet", 1),
           ("bq1", 1), ("bk1", 1), ("bv1", 1), ("qb2", 1), ("kb2", 1), ("vb2", 1), ("cq2", 1), ("ck2", 1),
           ("cv2", 1), ("m10", 4), ("m12", 4), ("hmask", 16)]
C_AT, NCOL = block_table(C_PARTS)

T_ANCHOR, T_COND, NT = 18, 25, 26
MODS = ([(S_AT["ada0"] + c, 0) for c in (0, 1, 3, 4, 6, 7)] + [(S_AT["ssq"] + c, 1) for c in (0, 1)]
        + [(S_AT["sskv"] + c, 1) for c in (0, 1)] + [(S_AT["ada2"] + c, 1) for c in (0, 1, 3, 4)]
        + [(S_AT["e1a"] + c, 0) for c in range(6)] + [(S_AT["g1a"], 0)])
NORMS = [(0, 1, "n1"), (2, 3, "nc"), (4, 5, "n2"), (7, 6, None), (9, 8, None), (10, 11, None), None,
         (12, 13, None), None]
GATES = [(S_AT["ada0"] + 2, 0), (S_AT["ada0"] + 5, 0), (S_AT["ada0"] + 8, 0), (S_AT["ada2"] + 2, 1),
         (S_AT["ada2"] + 5, 1)]
NG = len(GATES)
R_M0, R_P1, R_S2, R_C2, R_M2, R_OUT, R_GATE, R_E = 0, 1, 2, 3, 4, 5, 6, 7
NR = 10
FOLDED = [(R_P1, "bv1", "wp1"), (R_S2, "vb2", "so2"), (R_C2, "cv2", "co2")]

NLN, NAT = 9, 5
ATT = [dict(kw=T, q="qkv0", k=1, v=2, bq=None, bk=None, o="ao0", row=None, gate=0),
       dict(kw=C, q="cq0", k="ck0", v="cv0", bq=None, bk=None, o="co0", row=None, gate=1),
       dict(kw=C, q="wq1", k="wkv1", v=None, bq="bq1", bk="bk1", o="wp1", row=R_P1, gate=None),
       dict(kw=T, q="qkv2", k=1, v=2, bq="qb2", bk="kb2", o="so2", row=R_S2, gate=3),
       dict(kw=C, q="q2", k="kv2", v=None, bq="cq2", bk="ck2", o="co2", row=R_C2, gate=None)]
KBLK = [W_AT["qkv0"] + 1, W_AT["ck0"], W_AT["wkv1"], W_AT["qkv2"] + 1, W_AT["kv2"]]
VBLK = [W_AT["qkv0"] + 2, W_AT["cv0"], W_AT["wkv1"] + 1, W_AT["qkv2"] + 2, W_AT["kv2"] + 1]


def norm_parts(k):
    return [(f"l{k}", "stat"), (f"l{k}", "apply"), (f"l{k}", "t")]


X3_PARTS = ["q", "k", "v", "s", "pt", "ev", "lg", "lt"] + [f"h{c}" for c in range(7)] + ["e0", "e1", "e2", "rt", "g", "y"]
def at(quarter, *units):
    return [(quarter, u) for u in units]


FIRST = [(("l0", "stat"), 0), (("l0", "stat"), 1), (("l0", "apply"), 0), (("l0", "t"), 0), (("l0", "apply"), 1),
         (("p0", "k"), 0), (("l0", "t"), 1), (("p0", "q"), 0), (("p0", "k"), 1), (("p0", "v"), 0)]
BETWEEN = [
    at(3, ("p0", "q")) + at(7, ("p0", "v")),
    at(3, ("p1", "k")) + at(4, ("o0", "y"), ("l1", "stat")) + at(6, ("p1", "v"), ("l1", "apply")) + at(8, ("l1", "t"))
    + at(10, ("p1", "q")),
    at(1, ("l4", "stat")) + at(3, ("l4", "apply"), ("o1", "y"), ("l2", "stat")) + at(4, ("l4", "t"))
    + at(5, ("l2", "apply")) + at(6, ("p2", "k")) + at(7, ("l2", "t"), *[("m0", f"h{c}") for c in range(4)])
    + at(8, ("m0", "y"), ("l3", "stat")) + at(9, ("p2", "v")) + at(10, ("l3", "apply"))
    + at(11, ("l3", "t"), ("p2", "q")),
    at(4, ("o2", "y"), ("l5", "stat")) + at(6, ("l5", "apply")) + at(8, ("l5", "t"))
    + at(9, ("p3", "k"), ("p3", "q")) + at(10, ("p3", "v")),
    at(4, ("p4", "k"), ("o3", "y"), ("l6", "stat")) + at(6, ("p4", "v"), ("l6", "apply")) + at(8, ("l6", "t"))
    + at(10, ("p4", "q")),
    at(3, ("x3", "k")) + at(4, ("o4", "y")) + at(6, ("l7", "stat")) + at(8, ("l7", "apply")) + at(9, ("x3", "v")),
]
assert all(a[0] <= b[0] for stages in BETWEEN for a, b in zip(stages, stages[1:]))
LAST = ([("l7", "t")] + [("m1", f"h{c}") for c in range(4)] + [("m1", "y")] + norm_parts(8)
        + [("x3", j) for j in X3_PARTS if j not in ("k", "v")])
JOBS = NAT * NS * GB


def merge(k, s_att, between, s_bet):
    out = []
    for i in range(4 * GB):
        out.append(("A", (k * NS + s_att) * GB + i // 4, i % 4))
        out += [("B", u, s_bet) for quarter, u in between if quarter == i]
    return out


def weave(a, b):
    out, done = [], 0
    for i, u in enumerate(b):
        while done < len(a) * (i + 1) // len(b):
            out.append(a[done])
            done += 1
        out.append(u)
    return out


UNITS = [("B", u, s) for u, s in FIRST] + [("START", None, None)]
for _k in range(NAT):
    UNITS += merge(_k, 0, BETWEEN[_k], 1) + merge(_k, 1, BETWEEN[_k + 1], 0)
UNITS += [("END", None, None)] + weave([("B", u, 0) for u in LAST],
                                       [("B", u, 1) for u in [u for _, u in BETWEEN[NAT]] + LAST])

LIN_AT, _n = {}, 0
for _kind, _u, _s in UNITS:
    if _kind == "B" and _u[1] not in ("stat", "apply"):
        for _job in ([_u[1] + "a", _u[1] + "b"] if _u in (("p0", "q"), ("p0", "k")) else [_u[1]]):
            LIN_AT[(_u[0], _s, _job)] = _n
            _n += 1
LIN_JOBS = _n
assert LIN_JOBS % 2 == 0


def lin_bank(st, s, job):
    return LIN_AT[(st, s, job)] % 2


def lin_turn(it, st, s, job):
    return it * (LIN_JOBS // 2) + LIN_AT[(st, s, job)] // 2 + 1


LN_ORDER = [(int(u[0][1:]), s) for kind, u, s in UNITS if kind == "B" and u[1] == "stat"]
assert all(LN_ORDER == [(int(u[0][1:]), s) for kind, u, s in UNITS if kind == "B" and u[0][0] == "l" and u[1] == part]
           for part in ("apply", "t")), "a norm's steps are counted in the order of its statistics"
GATED = ["o0", "o1", "m0", "o3", "m1", "x3"]
GATED_ORDER = [(u[0], s) for kind, u, s in UNITS if kind == "B" and u[1] == "y" and u[0] in GATED]


def norm_turn(it, k, s):
    return it * len(LN_ORDER) + LN_ORDER.index((k, s)) + 1


def gated_turn(it, st, s):
    return it * len(GATED_ORDER) + GATED_ORDER.index((st, s)) + 1


def job_turn(it, j, part=0, per=1):
    return it * (JOBS * per) + j * per + part + 1


def job_of(j):
    return j // (NS * GB), j // GB % NS, j % GB


def nth(it, k, s, kinds, b=0, per=1):
    return it * (kinds * NS * per) + (k * NS + s) * per + b + 1


def build(nc, x_in, ctx_in, ctxT_in, condT_in, ws_in, w_in, col_in, vcol_in, row_in, rw_in, rb_in, gb_in, mqk_in, mkq_in,
          mc_in, cos_in, sin_in, ident_in, ind_in, onesp_in, out):
    ctx = ExitStack()
    with ctx:
        def sb(name, shape, dt=F32):
            return ctx.enter_context(nc.sbuf_tensor(name, shape, dt))

        def ps(name, shape, dt=F32):
            return ctx.enter_context(nc.psum_tensor(name, shape, dt))

        def sem(name):
            return ctx.enter_context(nc.semaphore(name))

        lin = ps("lin", [128, 2, 512])
        sco = ps("sco", [128, 2, 512])
        sct = ps("sct", [128, 2, 512])
        avp = ps("avp", [128, 512])
        mtp = ps("mtp", [128, 1024], BF16)

        W = sb("W", [128, NW, 128])
        Wrot = sb("Wrot", [128, 2, 128])
        col = sb("col", [128, NCOL])
        rw = sb("rw", [128, 3, 3])
        rb = sb("rb", [3, 1])
        condT = sb("condT", [128, B])
        scondT = sb("scondT", [128, B])
        modv = sb("modv", [128, 21, B])
        tab = sb("tab", [128, NT, B])
        cosT = sb("cosT", [128, T])
        sinT = sb("sinT", [128, T])
        ident = sb("ident", [128, 128])
        identb = sb("identb", [128, 128], BF16)
        rowb = sb("rowb", [128, NR, 128], BF16)
        oneb = sb("oneb", [128, 512], BF16)
        ind48 = sb("ind48", [128, H])
        indb = sb("indb", [128, H, 128], BF16)
        onesp = sb("onesp", [128, 4, 32])
        mqk8 = sb("mqk8", [128, T], U8)
        mkq8 = sb("mkq8", [128, T], U8)
        mc8 = sb("mc8", [1, B * C], U8)
        mqk = sb("mqk", [128, T], BF16)
        mkq = sb("mkq", [128, T], BF16)
        mcb = sb("mcb", [1, B * C], BF16)
        mhalf = sb("mhalf", [128, GB])

        xin, xs, ctxs, ctxT, gbc, tabg, mcg = [], [], [], [], [], [], []
        mv, bst, rstd, xn, hT, qT, qb, kT, t1, Vp, oT, hid = [], [], [], [], [], [], [], [], [], [], [], []
        for s in range(NS):
            xin.append(sb(f"xin{s}", [128, GB, D]))
            xs.append(sb(f"x{s}", [128, GB, D]))
            ctxs.append(sb(f"ctx{s}", [C, GB, D]))
            ctxT.append(sb(f"ctxT{s}", [128, GB, C]))
            gbc.append(sb(f"gbc{s}", [128, GB, NG * 128]))
            tabg.append(sb(f"tabg{s}", [128, NT, GB]))
            mcg.append(sb(f"mcg{s}", [128, GB, C], BF16))
            mv.append(sb(f"mv{s}", [128, GB, 2]))
            bst.append(sb(f"bst{s}", [128, GB, 6]))
            rstd.append(sb(f"rstd{s}", [128, 2, GB]))
            xn.append(sb(f"xn{s}", [128, GB, D]))
            hT.append(sb(f"hT{s}", [128, N]))
            qT.append(sb(f"qT{s}", [128, N]))
            qb.append(sb(f"qb{s}", [128, N], BF16))
            kT.append(sb(f"kT{s}", [128, N]))
            Vp.append(sb(f"Vp{s}", [128, GB, H, 32]))
            oT.append(sb(f"oT{s}", [128, N]))
            hid.append(sb(f"hid{s}", [128, 7, N]))
            t1.append(hid[s][:, 0:4, :])
        WS = hid[1][:].rearrange("p c n -> p (c n)")[:, 0:NSW * 128].rearrange("p (k d) -> p k d", d=128)
        row, row_left, row_left2 = (hid[0][0:NR, 4, i * D:(i + 1) * D] for i in range(3))
        row_part = sb("row_part", [NR, 3, D], BF16)
        vcol = hid[0][:, 5, 0:3 * NR].rearrange("p (c r) -> p c r", r=NR)
        mx3 = [sb(f"mx3{s}", [128, 4, GB]) for s in range(NS)]
        pr3 = [sb(f"pr3{s}", [128, 3, GB, 3]) for s in range(NS)]
        lgT = [sb(f"lgT{s}", [3, N]) for s in range(NS)]

        kbd = sb("kbd", [128, 3, H, 128])
        kbb = sb("kbb", [128, 2, H, 128], BF16)
        P = [sb(f"P{i}", [128, H, T]) for i in range(2)]
        gbrow, grow = (P[1][0:B, i * NG:(i + 1) * NG, :].rearrange("p g d -> p (g d)") for i in range(2))
        mx = sb("mx", [128, H])
        mhl = sb("mhl", [128, 128], BF16)
        mT = sb("mT", [128, T], BF16)
        rden = sb("rden", [128, T])

        gdram = nc.dram_tensor("gate_rows", (B, NG * 128), F32, kind="Internal").ap()

        cond_in, consts_in, w_first_in, w_rest_in = (sem(n) for n in ("cond_in", "consts_in", "w_first_in", "w_rest_in"))
        gate_rows_out = sem("gate_rows_out")
        x_in_s = [sem(f"x_loaded{s}") for s in range(NS)]
        ctx_in_s = [sem(f"ctx_loaded{s}") for s in range(NS)]
        g_in_s = [sem(f"gates_loaded{s}") for s in range(NS)]
        stored = [sem(f"stored{s}") for s in range(NS)]
        zeroed = sem("zeroed")
        silu_done = sem("silu_done")
        mods_done, modv_done, tab_done = sem("mods_done"), sem("modv_done"), sem("tab_done")
        gates_mm, grow_done = sem("gates_mm"), sem("grow_done")
        setup_dve = sem("setup_dve")
        rows_done, rows_in = sem("rows_done"), sem("rows_in")
        bias_mm = sem("bias_mm")
        group_tab = sem("group_tab")
        lin_full = [sem(f"lin_full{i}") for i in range(2)]
        lin_free = [sem(f"lin_free{i}") for i in range(2)]
        ln_bn, ln_stats, ln_eps, ln_rstd, ln_xn = (sem(n) for n in ("ln_bn", "ln_stats", "ln_eps", "ln_rstd", "ln_xn"))
        rope_parts, rope_q, rope_k, qb_ready = (sem(n) for n in ("rope_parts", "rope_q", "rope_k", "qb_ready"))
        kbd_ready, kbb_ready = sem("kbd_ready"), sem("kbb_ready")
        s_full, s_free, m_ready, mhi_ready, m_split, mt_full, mt_ready = (sem(n) for n in (
            "s_full", "s_free", "m_ready", "mhi_ready", "m_split", "mt_full", "mt_ready"))
        st_full, st_free, av_full, rden_ready, av_free = (sem(n) for n in (
            "st_full", "st_free", "av_full", "rden_ready", "av_free"))
        x_ready = sem("x_ready")
        x3_max, x3_neg, x3_sum, x3_rec, x3_p = (sem(n) for n in ("x3_max", "x3_neg", "x3_sum", "x3_rec", "x3_p"))
        r3_max, r3_exp, r3_sum, r3_rec, r3_p = (sem(n) for n in ("r3_max", "r3_exp", "r3_sum", "r3_rec", "r3_p"))

        NCOND, NCONST, NREST = 4, 13, 3
        gate_of = {"o0": 0, "o1": 1, "m0": 2, "o3": 3, "m1": 4}

        def wblk(name, k=0, n=1):
            a = W_AT[name] + k
            return W[:, a, :] if n == 1 else W[:, a:a + n, :]

        def c_(name, k=0):
            a = C_AT[name] + k
            return col[:, a:a + 1]

        def hold(eng):
            eng.nop(nofuse=True)

        def lin_ready(eng, it, st, s, job):
            eng.wait_ge(lin_full[lin_bank(st, s, job)], lin_turn(it, st, s, job))

        def lin_taken(eng, it, st, s, job):
            eng.wait_ge(lin_free[lin_bank(st, s, job)], lin_turn(it, st, s, job) + 1)
            hold(eng)

        def lin_ap(st, s, job, p=128):
            return lin[0:p, lin_bank(st, s, job), :]

        def diag(s, kw):
            v = Vp[s][0:kw]
            return bass.AP(tensor=v.tensor, offset=v.offset, ap=[list(v.ap[0]), [128, 16], [40, 4], [1, 8]])

        def res_ready(eng, it, st, s):
            before = {"l0": None, "l1": "o0", "l2": "o1", "l3": "m0", "l5": "o2", "l6": "o3", "l7": "o4", "l8": "m1"}[st]
            if before in GATED:
                eng.wait_ge(x_ready, gated_turn(it, before, s))
            elif before:
                lin_taken(eng, it, before, s, "y")

        block = ctx.enter_context(nc.Block())

        @block.sync
        def _(sp):
            for dst, src in ((condT[:], condT_in), (col[:], col_in), (WS[:, 0:13, :], ws_in[:, 0:13, :]),
                             (WS[:, 13:NSW, :], ws_in[:, 13:NSW, :])):
                sp.dma_start(dst, src).then_inc(cond_in, 16)
            sp.dma_start(xin[0][:], x_in[:, 0:GB, :]).then_inc(x_in_s[0], 16)
            for dst, src in ((ident[:], ident_in), (mqk8[:], mqk_in), (mkq8[:], mkq_in), (mc8[:], mc_in),
                             (ind48[:], ind_in), (row, row_in), (vcol, vcol_in), (gbrow, gb_in), (cosT[:], cos_in),
                             (sinT[:], sin_in), (onesp[:], onesp_in), (rw[:], rw_in), (rb[:], rb_in)):
                sp.dma_start(dst, src).then_inc(consts_in, 16)
            for s in range(1, NS):
                sp.dma_start(xin[s][:], x_in[:, s * GB:(s + 1) * GB, :]).then_inc(x_in_s[s], 16)

            def groups(it, more):
                for s in range(NS):
                    base = it * (NS * GB) + s * GB
                    sp.dma_start(ctxs[s][:], ctx_in[:, bass.ds(base, GB), :]).then_inc(ctx_in_s[s], 16)
                    sp.dma_start(ctxT[s][:], ctxT_in[:, bass.ds(base, GB), :]).then_inc(ctx_in_s[s], 16)
                sp.wait_ge(gate_rows_out, 16)
                for s in range(NS):
                    base = it * (NS * GB) + s * GB
                    gsrc = gdram[bass.ds(base, GB), :]
                    sp.dma_start(gbc[s][:], gsrc.partition_broadcast(128)).then_inc(g_in_s[s], 16)
                if more:
                    for s in range(NS):
                        sp.wait_ge(x_ready, gated_turn(it, "o0", s))
                        hold(sp)
                        base = (it + 1) * (NS * GB) + s * GB
                        sp.dma_start(xin[s][:], x_in[:, bass.ds(base, GB), :]).then_inc(x_in_s[s], 16)
                for s in range(NS):
                    sp.wait_ge(x_ready, gated_turn(it, "x3", s))
                    hold(sp)
                    base = it * (NS * GB) + s * GB
                    sp.dma_start(out[:, bass.ds(base, GB), :], xs[s][:]).then_inc(stored[s], 16)
                for s in range(NS):
                    sp.wait_ge(stored[s], it * 16 + 16)
                    if more:
                        hold(sp)

            with sp.Fori(0, ITERS - 1) as it:
                groups(it, True)
            groups(ITERS - 1, False)

        @block.gpsimd
        def _(pool):
            nc.gpsimd.memset(mhalf[:], -0.5).then_inc(zeroed, 1)
            for s in range(NS):
                nc.gpsimd.memset(Vp[s][:], 0.0).then_inc(zeroed, 1)
            pool.wait_ge(cond_in, 16 * NCOND)
            pool.wait_ge(zeroed, 1 + NS)
            hm = col[:, C_AT["hmask"]:C_AT["hmask"] + H].unsqueeze(2)

            def norm(it, k, s):
                t = C if k == 4 else 128
                eps = 1e-6 if k in (5, 6, 7) else 1e-5
                pool.wait_ge(ln_stats, norm_turn(it, k, s))
                hold(pool)
                nc.gpsimd.tensor_scalar(rstd[s][0:t, 0, :], mv[s][0:t, :, 1], eps, None, ALU.add).then_inc(ln_eps, 1)
                pool.wait_ge(ln_eps, norm_turn(it, k, s))
                nc.gpsimd.tensor_tensor(rstd[s][0:t, 1, :], rstd[s][0:t, 0, :], mhalf[0:t, :],
                                        ALU.pow).then_inc(ln_rstd, 1)

            def keys(it, j, half):
                a, s, b = job_of(j)
                kw = ATT[a]["kw"]
                if a == 0:
                    pool.wait_ge(rope_k, nth(it, 0, s, 1))
                else:
                    lin_taken(pool, it, f"p{a}", s, "k")
                if j >= 3:
                    pool.wait_ge(st_full, job_turn(it, j - 3, 3, 4))
                h0 = 8 * half
                k = kT[s][:, b * kw:(b + 1) * kw].unsqueeze(1)
                nc.gpsimd.tensor_tensor(kbd[:, j % 3, h0:h0 + 8, 0:kw], k.broadcast_to([128, 8, kw]),
                                        hm[:, h0:h0 + 8].broadcast_to([128, 8, kw]), ALU.mult).then_inc(kbd_ready, 1)

            with pool.Fori(0, ITERS) as it:
                for kind, u, s in UNITS:
                    if kind == "START":
                        for j in range(2):
                            keys(it, j, 0)
                            keys(it, j, 1)
                    elif kind == "A" and s in (0, 2) and u + 2 < JOBS:
                        keys(it, u + 2, s // 2)
                    elif kind == "B" and u[1] == "stat":
                        norm(it, int(u[0][1:]), s)

        @block.scalar
        def _(act):
            act.wait_ge(cond_in, 16 * NCOND)
            nc.scalar.activation(scondT[:], condT[:], ACT.Silu).then_inc(silu_done, 1)
            act.dma_start(W[:, 0:NW_FIRST, :], w_in[:, 0:NW_FIRST, :]).then_inc(w_first_in, 16)
            for i in range(NREST):
                a, b = (NW_FIRST + (NW - NW_FIRST) * k // NREST for k in (i, i + 1))
                act.dma_start(W[:, a:b, :], w_in[:, a:b, :]).then_inc(w_rest_in, 16)
            act.wait_ge(grow_done, 1)
            act.dma_start(gdram, grow).then_inc(gate_rows_out, 16)
            act.wait_ge(rows_done, 1)
            for i in range(3):
                act.dma_start(rowb[i:i + 1], row_part[:, i, :]).then_inc(rows_in, 16)
            act.wait_ge(consts_in, 16 * NCONST)

            def copy_out(it, st, s, job, dst, src, bias=None):
                lin_ready(act, it, st, s, job)
                kw = {} if bias is None else {"bias": bias}
                nc.scalar.activation(dst, src, ACT.Identity, **kw).then_inc(lin_free[lin_bank(st, s, job)], 1)

            def norm(it, k, s):
                st, t = f"l{k}", (C if k == 4 else 128)
                lin_ready(act, it, st, s, "t")
                src = lin_ap(st, s, "t")
                dst = hid[s][:, 5, :] if k == 4 else hT[s][:]
                for b in range(GB):
                    i = nc.scalar.activation(dst[:, b * t:(b + 1) * t], src[:, b * t:(b + 1) * t], ACT.Identity,
                                             bias=tabg[s][:, 2 * k + 1, b:b + 1], scale=tabg[s][:, 2 * k, b:b + 1])
                i.then_inc(lin_free[lin_bank(st, s, "t")], 1)

            def project(it, a, s, part):
                A, st = ATT[a], f"p{a}"
                if a > 0 and part != "v":
                    dst, n, bias = (qT, N, A["bq"]) if part == "q" else (kT, GB * A["kw"], A["bk"])
                    copy_out(it, st, s, part, dst[s][:, 0:n], lin_ap(st, s, part)[:, 0:n], c_(bias) if bias else None)

            def narrow(it, j, half):
                kw = ATT[job_of(j)[0]]["kw"]
                h0 = 8 * half
                act.wait_ge(kbd_ready, job_turn(it, j, half, 2))
                nc.scalar.activation(kbb[:, j % 2, h0:h0 + 8, 0:kw], kbd[:, j % 3, h0:h0 + 8, 0:kw],
                                     ACT.Identity).then_inc(kbb_ready, 1)

            def exps(it, j, g):
                kw = ATT[job_of(j)[0]]["kw"]
                act.wait_ge(st_full, job_turn(it, j, g, 4))
                nc.scalar.activation(P[j % 2][0:kw, 4 * g:4 * g + 4, :],
                                     sct[0:kw, g % 2, :].rearrange("p (h q) -> p h q", h=4),
                                     ACT.Exp, scale=float(HD) ** -0.5).then_inc(st_free, 1)

            def mlp(it, k, s, c):
                st = f"m{k}"
                lin_ready(act, it, st, s, f"h{c}")
                nc.scalar.activation(hid[s][:, c, :], lin_ap(st, s, f"h{c}"), ACT.Gelu_apprx_tanh,
                                     bias=c_("m10" if k == 0 else "m12", c)).then_inc(
                                         lin_free[lin_bank(st, s, f"h{c}")], 1)

            def mixture(it, s, part):
                st = "x3"
                if part == "k":
                    copy_out(it, st, s, "k", kT[s][:, 0:NC], lin_ap(st, s, "k")[:, 0:NC])
                elif part == "s":
                    act.wait_ge(x3_neg, nth(it, 0, s, 1))
                    lin_ready(act, it, st, s, "s")
                    for b in range(GB):
                        i = nc.scalar.activation(xn[s][:, b, 0:C], lin_ap(st, s, "s")[:, b * C:(b + 1) * C], ACT.Exp,
                                                 bias=mx3[s][:, 1, b:b + 1], scale=float(D) ** -0.5)
                    i.then_inc(lin_free[lin_bank(st, s, "s")], 1)
                elif part == "ev":
                    copy_out(it, st, s, "ev", kT[s][:], lin_ap(st, s, "ev"))
                elif part == "lg":
                    copy_out(it, st, s, "lg", lgT[s][:], lin_ap(st, s, "lg", 3), rb[:])
                elif part == "lt":
                    lin_taken(act, it, st, s, "lt")
                    nc.scalar.activation(pr3[s][:, 1], pr3[s][:, 0], ACT.Exp).then_inc(r3_exp, 1)
                elif part[0] == "h":
                    c = int(part[1:])
                    lin_ready(act, it, st, s, part)
                    for b in range(GB):
                        i = nc.scalar.activation(hid[s][:, c, b * T:(b + 1) * T],
                                                 lin_ap(st, s, part)[:, b * T:(b + 1) * T],
                                                 ACT.Silu, bias=tabg[s][:, T_ANCHOR + c, b:b + 1])
                    i.then_inc(lin_free[lin_bank(st, s, part)], 1)
                elif part == "rt":
                    copy_out(it, st, s, "rt", oT[s][:], lin_ap(st, s, "rt"))
                elif part == "g":
                    lin_ready(act, it, st, s, "g")
                    nc.scalar.activation(hid[s][:, 5, :], lin_ap(st, s, "g"), ACT.Sigmoid).then_inc(
                        lin_free[lin_bank(st, s, "g")], 1)

            with act.Fori(0, ITERS) as it:
                for kind, u, s in UNITS:
                    if kind == "START":
                        act.wait_ge(gate_rows_out, 16)
                        for j, half in ((0, 0), (0, 1), (1, 0)):
                            narrow(it, j, half)
                    elif kind == "A":
                        if s == 0 and u + 1 < JOBS:
                            narrow(it, u + 1, 1)
                        exps(it, u, s)
                        if s == 3 and u + 2 < JOBS:
                            narrow(it, u + 2, 0)
                    elif kind == "B":
                        st, part = u
                        k = int(st[1:])
                        if u == ("l0", "t"):
                            act.wait_ge(group_tab, nth(it, 0, s, 1))
                        if part == "t":
                            norm(it, k, s)
                        elif st[0] == "p":
                            project(it, k, s, part)
                        elif st[0] == "m" and part != "y":
                            mlp(it, k, s, int(part[1:]))
                        elif st == "x3":
                            mixture(it, s, part)

        @block.vector
        def _(dve):
            v = nc.vector
            n_setup = [0]

            def chain(i):
                n_setup[0] += 1
                i.then_inc(setup_dve, 1)
                dve.wait_ge(setup_dve, n_setup[0])

            v.memset(rowb[:], 0.0).then_inc(lin_free[0], 1)
            for s in range(NS):
                v.memset(mcg[s][:], 0.0)
            v.memset(rden[:], 0.0).then_inc(lin_free[1], 1)
            v.memset(oneb[:], 1.0).then_inc(s_free, 2)
            v.memset(mhl[:], 0.0).then_inc(st_free, 2)
            chain(v.memset(mx[:], 0.0))
            v.memset(mT[:], 0.0).then_inc(av_free, 1)
            dve.wait_ge(consts_in, 16 * NCONST)
            v.tensor_copy(identb[:], ident[:])
            v.tensor_copy(indb[:], ind48[:].unsqueeze(2).broadcast_to([128, H, 128]))
            for dst, src in ((mqk, mqk8), (mkq, mkq8), (mcb, mc8)):
                v.tensor_scalar(dst[:], src[:], -1.0, BIG, ALU.add, ALU.mult)
            dve.wait_ge(mods_done, 1)
            chain(v.tensor_tensor(modv[:], sct[:, 0, 0:21 * B].rearrange("p (c b) -> p c b", b=B),
                                  col[:, 0:21].unsqueeze(2).broadcast_to([128, 21, B]), ALU.add))
            for k, site in enumerate(NORMS):
                if site is None:
                    for r, nm in enumerate(("g2", "b2") if k == 6 else ("gam", "bet")):
                        v.tensor_copy(tab[:, 2 * k + r, :], c_(nm).broadcast_to([128, B]))
                    continue
                shift, scale, wcol = site
                w = c_(wcol) if wcol else 1.0
                v.tensor_scalar(tab[:, 2 * k, :], modv[:, scale, :], 1.0, w, ALU.add, ALU.mult)
                v.tensor_copy(tab[:, 2 * k + 1, :], modv[:, shift, :])
            v.tensor_copy(tab[:, T_ANCHOR:T_ANCHOR + 7, :], modv[:, 14:21, :])
            chain(v.tensor_copy(tab[:, T_COND, :], condT[:]))
            dve.wait_ge(w_first_in, 16)
            for i in range(2):
                wv = wblk("qkv0", i).rearrange("p (h t j) -> p h t j", t=2, j=4)
                rv = Wrot[:, i, :].rearrange("p (h t j) -> p h t j", t=2, j=4)
                v.tensor_scalar(rv[:, :, 0, :], wv[:, :, 1, :], -1.0, None, ALU.mult)
                i_ = v.tensor_copy(rv[:, :, 1, :], wv[:, :, 0, :])
            i_.then_inc(tab_done, 1)
            dve.wait_ge(gates_mm, 1)
            for i in range(NG):
                i_ = v.tensor_tensor(grow[:, i * 128:(i + 1) * 128],
                                     (sct[0:B, 1, i * 128:(i + 1) * 128] if i < 4 else avp[0:B, 0:128]),
                                     gbrow[:, i * 128:(i + 1) * 128], ALU.add)
            i_.then_inc(grow_done, 1)
            dve.wait_ge(bias_mm, 1)
            chain(v.tensor_tensor(row, sco[0:NR, 0, 0:128], row, ALU.add))
            chain(v.tensor_copy(row_part[:, 0, :], row))
            chain(v.tensor_tensor(row_left, row, row_part[:, 0, :], ALU.subtract))
            chain(v.tensor_copy(row_part[:, 1, :], row_left))
            chain(v.tensor_tensor(row_left2, row_left, row_part[:, 1, :], ALU.subtract))
            v.tensor_copy(row_part[:, 2, :], row_left2).then_inc(rows_done, 1)

            def statistics(it, k, s):
                t = C if k == 4 else 128
                src = {0: xin, 4: ctxs}.get(k, xs)[s]
                if k == 4:
                    dve.wait_ge(ctx_in_s[s], it * 32 + 32)
                    hold(dve)
                if k == 0:
                    base = it * (NS * GB) + s * GB
                    dve.wait_ge(x_in_s[s], it * 16 + 16)
                    hold(dve)
                    v.tensor_copy(tabg[s][:], tab[:, :, bass.ds(base, GB)])
                    v.tensor_copy(mcg[s][0:1].rearrange("p b c -> p (b c)"),
                                  mcb[:, bass.ds(base * C, GB * C)]).then_inc(group_tab, 1)
                if k != 4:
                    res_ready(dve, it, f"l{k}", s)
                for b in range(GB):
                    i = v.bn_stats(bst[s][0:t, b, :], src[0:t, b, :])
                i.then_inc(ln_bn, 1)
                dve.wait_ge(ln_bn, norm_turn(it, k, s))
                hold(dve)
                for b in range(GB):
                    i = v.bn_aggr(mv[s][0:t, b, :], bst[s][0:t, b, :])
                i.then_inc(ln_stats, 1)

            def apply(it, k, s):
                t = C if k == 4 else 128
                src = {0: xin, 4: ctxs}.get(k, xs)[s]
                dve.wait_ge(ln_stats, norm_turn(it, k, s))
                dve.wait_ge(ln_rstd, norm_turn(it, k, s))
                for b in range(GB):
                    i = v.tensor_scalar((ctxs if k == 4 else xn)[s][0:t, b, :], src[0:t, b, :], mv[s][0:t, b, 0:1],
                                        rstd[s][0:t, 1, b:b + 1], ALU.subtract, ALU.mult)
                i.then_inc(ln_xn, 1)

            def values(it, a, s):
                st, kw = f"p{a}", ATT[a]["kw"]
                lin_ready(dve, it, st, s, "v")
                v.tensor_copy(diag(s, kw), lin_ap(st, s, "v", kw).rearrange(
                    "p (c h d) -> p c h d", h=4, d=8)).then_inc(lin_free[lin_bank(st, s, "v")], 1)

            def project(it, a, s, part):
                st = f"p{a}"
                if part == "v":
                    values(it, a, s)
                    return
                if a == 0:
                    r, dst, done = (0, qT, rope_q) if part == "q" else (1, kT, rope_k)
                    for u, (job, tbl) in enumerate(((part + "a", cosT), (part + "b", sinT))):
                        lin_ready(dve, it, st, s, job)
                        v.tensor_tensor(t1[s][:, 2 * r + u, :].rearrange("p (b t) -> p b t", b=GB),
                                        lin_ap(st, s, job).rearrange("p (b t) -> p b t", b=GB),
                                        tbl[:].unsqueeze(1).broadcast_to([128, GB, T]), ALU.mult).then_inc(
                                            lin_free[lin_bank(st, s, job)], 1)
                    lin_taken(dve, it, st, s, part + "a")
                    lin_taken(dve, it, st, s, part + "b")
                    v.tensor_tensor(dst[s][:], t1[s][:, 2 * r, :], t1[s][:, 2 * r + 1, :], ALU.add).then_inc(done, 1)
                if part == "q":
                    if a == 0:
                        dve.wait_ge(rope_q, nth(it, 0, s, 1))
                    else:
                        lin_taken(dve, it, st, s, "q")
                    v.tensor_copy(qb[s][:], qT[s][:]).then_inc(qb_ready, 1)

            def maxima(it, j, g):
                kw = ATT[job_of(j)[0]]["kw"]
                dve.wait_ge(s_full, job_turn(it, j, g, 4))
                v.tensor_reduce(mx[:, 4 * g:4 * g + 4],
                                sco[:, g % 2, 0:4 * kw].rearrange("p (h k) -> p h k", h=4), AX,
                                ALU.max).then_inc(s_free, 1)

            def split(it, j):
                dve.wait_ge(s_free, job_turn(it, j, 3, 4) + 2)
                v.tensor_copy(mhl[:, 0:16], mx[:]).then_inc(mhi_ready, 1)
                dve.wait_ge(mhi_ready, job_turn(it, j))
                v.tensor_tensor(mhl[:, 32:48], mx[:], mhl[:, 0:16], ALU.subtract).then_inc(m_split, 1)

            def turned(it, j):
                dve.wait_ge(mt_full, job_turn(it, j))
                v.tensor_copy(mT[:], mtp[:, 0:T]).then_inc(mt_ready, 1)

            def normalise(it, j):
                _, s, b = job_of(j)
                n = job_turn(it, j)
                dve.wait_ge(av_full, n)
                v.reciprocal(rden[:], avp[:, T:2 * T]).then_inc(rden_ready, 1)
                dve.wait_ge(rden_ready, n)
                v.tensor_tensor(oT[s][:, b * T:(b + 1) * T], avp[:, 0:T], rden[:], ALU.mult).then_inc(av_free, 1)

            def add_result(it, st, s, gate):
                lin_ready(dve, it, st, s, "y")
                y = lin_ap(st, s, "y").rearrange("p (b d) -> p b d", b=GB)
                free = lin_free[lin_bank(st, s, "y")]
                if gate is None:
                    v.tensor_tensor(xs[s][:], xs[s][:], y, ALU.add).then_inc(free, 1)
                else:
                    v.tensor_tensor(t1[s][:, 0, :].rearrange("p (b d) -> p b d", b=GB), y, gate, ALU.mult).then_inc(free, 1)
                    lin_taken(dve, it, st, s, "y")
                    v.tensor_tensor(xs[s][:], (xin if st == "o0" else xs)[s][:],
                                    t1[s][:, 0, :].rearrange("p (b d) -> p b d", b=GB), ALU.add).then_inc(x_ready, 1)

            def mixture(it, s, part):
                st = "x3"
                one = nth(it, 0, s, 1)
                if part == "q":
                    lin_ready(dve, it, st, s, "q")
                    v.tensor_copy(qT[s][:], lin_ap(st, s, "q")).then_inc(lin_free[lin_bank(st, s, "q")], 1)
                elif part == "v":
                    lin_ready(dve, it, st, s, "v")
                    v.tensor_copy(hid[s][0:C, 6, :], lin_ap(st, s, "v", C)).then_inc(lin_free[lin_bank(st, s, "v")], 1)
                elif part == "s":
                    lin_ready(dve, it, st, s, "s")
                    v.tensor_reduce(mx3[s][:, 0, :], lin_ap(st, s, "s")[:, 0:NC].rearrange("p (b c) -> p b c", b=GB), AX,
                                    ALU.max).then_inc(x3_max, 1)
                    dve.wait_ge(x3_max, one)
                    v.tensor_scalar(mx3[s][:, 1, :], mx3[s][:, 0, :], -float(D) ** -0.5, None,
                                    ALU.mult).then_inc(x3_neg, 1)
                elif part == "pt":
                    lin_taken(dve, it, st, s, "s")
                    v.tensor_reduce(mx3[s][:, 2, :], xn[s][:, :, 0:C], AX, ALU.add).then_inc(x3_sum, 1)
                    dve.wait_ge(x3_sum, one)
                    v.reciprocal(mx3[s][:, 3, :], mx3[s][:, 2, :]).then_inc(x3_rec, 1)
                    dve.wait_ge(x3_rec, one)
                    v.tensor_tensor(xn[s][:, :, 0:C], xn[s][:, :, 0:C],
                                    mx3[s][:, 3, :].unsqueeze(2).broadcast_to([128, GB, C]), ALU.mult).then_inc(x3_p, 1)
                    lin_ready(dve, it, st, s, "pt")
                    v.tensor_copy(oT[s][0:C, :], lin_ap(st, s, "pt", C)).then_inc(lin_free[lin_bank(st, s, "pt")], 1)
                elif part == "lt":
                    lin_ready(dve, it, st, s, "lt")
                    lt = lin_ap(st, s, "lt")[:, 0:3 * GB].rearrange("p (b e) -> p b e", e=3)
                    v.tensor_reduce(mx3[s][:, 0, :], lt, AX, ALU.max).then_inc(r3_max, 1)
                    dve.wait_ge(r3_max, one)
                    v.tensor_tensor(pr3[s][:, 0], lt, mx3[s][:, 0, :].unsqueeze(2).broadcast_to([128, GB, 3]),
                                    ALU.subtract).then_inc(lin_free[lin_bank(st, s, "lt")], 1)
                elif part == "h2":
                    dve.wait_ge(r3_exp, one)
                    v.tensor_reduce(mx3[s][:, 1, :], pr3[s][:, 1], AX, ALU.add).then_inc(r3_sum, 1)
                    dve.wait_ge(r3_sum, one)
                    v.reciprocal(mx3[s][:, 2, :], mx3[s][:, 1, :]).then_inc(r3_rec, 1)
                    dve.wait_ge(r3_rec, one)
                    v.tensor_tensor(pr3[s][:, 2], pr3[s][:, 1], mx3[s][:, 2, :].unsqueeze(2).broadcast_to([128, GB, 3]),
                                    ALU.mult).then_inc(r3_p, 1)
                elif part[0] == "e" and part != "ev":
                    e = int(part[1:])
                    if e == 0:
                        dve.wait_ge(r3_p, one)
                    else:
                        lin_taken(dve, it, st, s, f"e{e - 1}")
                    lin_ready(dve, it, st, s, part)
                    src = lin_ap(st, s, part)
                    for b in range(GB):
                        p = pr3[s][:, 2, b, e:e + 1]
                        if e == 0:
                            i = v.tensor_scalar(xn[s][:, b, :], src[:, b * D:(b + 1) * D], p, None, ALU.mult)
                        else:
                            i = v.scalar_tensor_tensor(out=xn[s][:, b, :], in0=src[:, b * D:(b + 1) * D], scalar=p,
                                                       in1=xn[s][:, b, :], op0=ALU.mult, op1=ALU.add)
                    i.then_inc(lin_free[lin_bank(st, s, part)], 1)
                elif part == "y":
                    lin_taken(dve, it, st, s, "g")
                    add_result(it, st, s, hid[s][:, 5, :].rearrange("p (b d) -> p b d", b=GB))

            with dve.Fori(0, ITERS) as it:
                for kind, u, s in UNITS:
                    if kind == "START":
                        for g in range(4):
                            maxima(it, 0, g)
                        split(it, 0)
                        turned(it, 0)
                    elif kind == "A":
                        if u + 1 < JOBS:
                            maxima(it, u + 1, s)
                        if s == 3:
                            if u + 1 < JOBS:
                                split(it, u + 1)
                                turned(it, u + 1)
                            if u > 0:
                                normalise(it, u - 1)
                    elif kind == "END":
                        normalise(it, JOBS - 1)
                    elif kind == "B":
                        st, part = u
                        k = int(st[1:])
                        if part == "stat":
                            statistics(it, k, s)
                        elif part == "apply":
                            apply(it, k, s)
                        elif st[0] == "p":
                            project(it, k, s, part)
                        elif st[0] in "om" and part == "y":
                            if st == "o0":
                                dve.wait_ge(g_in_s[s], it * 16 + 16)
                            g = gate_of.get(st)
                            add_result(it, st, s, None if g is None else gbc[s][:, :, g * 128:(g + 1) * 128])
                        elif st == "x3":
                            mixture(it, s, part)

        @block.tensor
        def _(pe):
            mm = nc.tensor.matmul
            pe.wait_ge(cond_in, 16 * NCOND)
            pe.wait_ge(silu_done, 1)
            for c, (blk, silu) in enumerate(MODS):
                i = mm(sct[:, 0, c * B:(c + 1) * B], WS[:, blk, :], (scondT if silu else condT)[:], start=True, stop=True)
            i.then_inc(mods_done, 1)
            for c, (blk, silu) in enumerate(GATES):
                dst = sct[0:B, 1, c * 128:(c + 1) * 128] if c < 4 else avp[0:B, 0:128]
                i = mm(dst, (scondT if silu else condT)[:], WS[:, blk, :], start=True, stop=True)
            i.then_inc(gates_mm, 1)
            pe.wait_ge(consts_in, 16 * NCONST)
            pe.wait_ge(w_first_in, 16)
            for c, (_, _, wn) in enumerate(FOLDED):
                i = mm(sco[0:NR, 0, 0:128], vcol[:, c, :], wblk(wn), start=(c == 0), stop=(c == len(FOLDED) - 1))
            i.then_inc(bias_mm, 1)
            pe.wait_ge(tab_done, 1)

            def take(it, st, s, job):
                pe.wait_ge(lin_free[lin_bank(st, s, job)], lin_turn(it, st, s, job))

            def give(st, s, job, i):
                i.then_inc(lin_full[lin_bank(st, s, job)], 1)

            def linear(it, st, s, job, parts, n, m=128):
                take(it, st, s, job)
                for c, (w, a) in enumerate(parts):
                    i = mm(lin_ap(st, s, job, m)[:, 0:n], w, a, start=(c == 0), stop=(c == len(parts) - 1))
                give(st, s, job, i)

            def tokens(it, st, s, job, src, wts, bias=None, t=T):
                take(it, st, s, job)
                o = lin_ap(st, s, job, t)
                if bias is not None:
                    mm(o.rearrange("p (b d) -> p b d", b=GB), oneb[:, 0:t],
                       rowb[:, bias, :].unsqueeze(1).broadcast_to([128, GB, 128]), start=True, stop=False,
                       skip_group_check=True)
                for b in range(GB):
                    for c, (a, w) in enumerate(zip(src, wts)):
                        i = mm(o[:, b * 128:(b + 1) * 128], a[:, b * t:(b + 1) * t], w,
                               start=(c == 0 and bias is None), stop=(c == len(wts) - 1), skip_group_check=True)
                give(st, s, job, i)

            def norm(it, k, s):
                st, t = f"l{k}", (C if k == 4 else 128)
                take(it, st, s, "t")
                pe.wait_ge(ln_xn, norm_turn(it, k, s))
                for b in range(GB):
                    i = nc.tensor.transpose(lin_ap(st, s, "t")[:, b * t:(b + 1) * t],
                                            (ctxs if k == 4 else xn)[s][0:t, b, :], ident[0:t, 0:t])
                give(st, s, "t", i)

            def project(it, a, s, part):
                st, A = f"p{a}", ATT[a]
                n = GB * A["kw"]
                own = a in (0, 3)
                norm_of = {0: "l0", 1: "l1", 2: "l3", 3: "l5", 4: "l6"}[a]
                if part == "q" or own:
                    lin_taken(pe, it, norm_of, s, "t")
                elif a == 2:
                    lin_taken(pe, it, "l4", s, "t")
                h = hT[s][:]
                kv = h if own else (hid[s][:, 5, 0:NC] if a == 2 else ctxT[s][:].rearrange("p b c -> p (b c)"))
                if a == 0 and part != "v":
                    i = 0 if part == "q" else 1
                    linear(it, st, s, part + "a", [(wblk("qkv0", i), h)], N)
                    linear(it, st, s, part + "b", [(Wrot[:, i, :], h)], N)
                elif part == "q":
                    linear(it, st, s, "q", [(wblk(A["q"]), h)], N)
                elif part == "k":
                    linear(it, st, s, "k", [(W[:, KBLK[a], :], kv)], n)
                else:
                    tokens(it, st, s, "v", [kv], [W[:, VBLK[a], :]], t=A["kw"])

            def scores(it, j, g):
                a, s, b = job_of(j)
                kw = ATT[a]["kw"]
                if b == 0 and g == 0:
                    pe.wait_ge(qb_ready, nth(it, a, s, NAT))
                    if a == 0:
                        pe.wait_ge(rope_q, nth(it, 0, s, 1))
                if g % 2 == 0:
                    pe.wait_ge(kbb_ready, job_turn(it, j, g // 2, 2))
                pe.wait_ge(s_free, job_turn(it, j, g, 4))
                o = sco[:, g % 2, 0:4 * kw].rearrange("p (h k) -> p h k", h=4)
                i = mm(o, qb[s][:, b * T:(b + 1) * T], kbb[:, j % 2, 4 * g:4 * g + 4, 0:kw], start=True, stop=(a > 1))
                if a == 0:
                    i = mm(o, identb[:], mqk[:].unsqueeze(1).broadcast_to([128, 4, T]), start=False, stop=True)
                elif a == 1:
                    i = mm(o, oneb[:, 0:T], mcg[s][:, b, :].unsqueeze(1).broadcast_to([128, 4, C]),
                           start=False, stop=True)
                i.then_inc(s_full, 1)

            def turn(it, j):
                pe.wait_ge(m_split, job_turn(it, j))
                nc.tensor.transpose(mtp[:, 0:T], mhl[:], identb[:]).then_inc(mt_full, 1)

            def scores_t(it, j, g):
                a, s, b = job_of(j)
                kw = ATT[a]["kw"]
                if g == 0:
                    pe.wait_ge(mt_ready, job_turn(it, j))
                pe.wait_ge(st_free, job_turn(it, j, g, 4))
                o = sct[0:kw, g % 2, :]
                for hh in range(4):
                    mm(o[:, hh * T:(hh + 1) * T], kbd[:, j % 3, 4 * g + hh, 0:kw], qT[s][:, b * T:(b + 1) * T],
                       start=(hh == 0), stop=False, skip_group_check=True)
                if a == 0:
                    mm(o.rearrange("p (h q) -> p h q", h=4), identb[:], mkq[:].unsqueeze(1).broadcast_to([128, 4, T]),
                       start=False, stop=False, skip_group_check=True)
                elif a == 1:
                    mm(o, mcg[s][:, b, :], oneb[:], start=False, stop=False, skip_group_check=True)
                for hh in range(4):
                    i = mm(o[:, hh * T:(hh + 1) * T], indb[:, 4 * g + hh, 0:kw], mT[:], start=False,
                           stop=(hh == 3), skip_group_check=True)
                i.then_inc(st_full, 1)

            def av(it, j, part):
                a, s, b = job_of(j)
                kw = ATT[a]["kw"]
                if part == 0:
                    lin_taken(pe, it, f"p{a}", s, "v")
                    pe.wait_ge(st_free, job_turn(it, j, 3, 4) + 2)
                    pe.wait_ge(av_free, job_turn(it, j))
                for hh in range(4):
                    for g in range(4):
                        w = Vp[s][0:kw, b, 4 * g + hh, :] if part == 0 else onesp[0:kw, hh, :]
                        i = mm(avp[32 * g:32 * g + 32, part * T:(part + 1) * T], w,
                               P[j % 2][0:kw, 4 * g + hh, :], start=(hh == 0), stop=(hh == 3), skip_group_check=True)
                if part == 1:
                    i.then_inc(av_full, 1)

            def outproj(it, a, s):
                pe.wait_ge(av_free, job_turn(it, (a * NS + s) * GB + GB - 1) + 1)
                tokens(it, f"o{a}", s, "y", [oT[s][:]], [wblk(ATT[a]["o"])], ATT[a]["row"])

            def mlp(it, k, s, part):
                st = f"m{k}"
                w1, w2 = ("m10", "m20") if k == 0 else ("m12", "m22")
                if part != "y":
                    if part == "h0":
                        lin_taken(pe, it, "l2" if k == 0 else "l7", s, "t")
                    linear(it, st, s, part, [(wblk(w1, int(part[1:])), hT[s][:])], N)
                    return
                for c in range(4):
                    lin_taken(pe, it, st, s, f"h{c}")
                tokens(it, st, s, "y", [hid[s][:, c, :] for c in range(4)], [wblk(w2, c) for c in range(4)],
                       R_M0 if k == 0 else R_M2)

            def mixture(it, s, part):
                st = "x3"
                h, ev, ct = hT[s][:], kT[s][:], ctxT[s][:].rearrange("p b c -> p (b c)")
                if part == "q":
                    lin_taken(pe, it, "l8", s, "t")
                    linear(it, st, s, "q", [(wblk("q3"), h)], N)
                elif part == "k":
                    linear(it, st, s, "k", [(wblk("k3"), ct)], NC)
                elif part == "v":
                    tokens(it, st, s, "v", [ct], [wblk("v3")], t=C)
                elif part == "s":
                    for job in ("q", "k"):
                        lin_taken(pe, it, st, s, job)
                    take(it, st, s, "s")
                    for b in range(GB):
                        i = mm(lin_ap(st, s, "s")[:, b * C:(b + 1) * C], qT[s][:, b * T:(b + 1) * T],
                               kT[s][:, b * C:(b + 1) * C], start=True, stop=True)
                    give(st, s, "s", i)
                elif part == "pt":
                    take(it, st, s, "pt")
                    pe.wait_ge(x3_p, nth(it, 0, s, 1))
                    for b in range(GB):
                        i = nc.tensor.transpose(lin_ap(st, s, "pt", C)[:, b * T:(b + 1) * T], xn[s][:, b, 0:C], ident[:])
                    give(st, s, "pt", i)
                elif part == "ev":
                    for job in ("v", "pt"):
                        lin_taken(pe, it, st, s, job)
                    take(it, st, s, "ev")
                    for b in range(GB):
                        i = mm(lin_ap(st, s, "ev")[:, b * T:(b + 1) * T], hid[s][0:C, 6, b * D:(b + 1) * D],
                               oT[s][0:C, b * T:(b + 1) * T], start=True, stop=True)
                    give(st, s, "ev", i)
                elif part == "lg":
                    lin_taken(pe, it, st, s, "ev")
                    anchor = tabg[s][:, T_COND, :].unsqueeze(2).broadcast_to([128, GB, T])
                    linear(it, st, s, "lg", [(rw[:, 0, :], h), (rw[:, 1, :], ev), (rw[:, 2, :], anchor)], N, m=3)
                elif part == "lt":
                    lin_taken(pe, it, st, s, "lg")
                    take(it, st, s, "lt")
                    hold(pe)
                    for b in range(GB):
                        i = nc.tensor.transpose(lin_ap(st, s, "lt")[:, 3 * b:3 * b + 3], lgT[s][:, b * T:(b + 1) * T],
                                                ident[0:3, 0:3])
                    give(st, s, "lt", i)
                elif part[0] == "h":
                    c = int(part[1:])
                    e, r = c // 2, c % 2
                    w0, w1 = (wblk("e1", 4 * e + r), wblk("e1", 4 * e + 2 + r)) if c < 6 else (wblk("g1", 0), wblk("g1", 1))
                    linear(it, st, s, part, [(w0, h), (w1, ev)], N)
                elif part[0] == "e":
                    e = int(part[1:])
                    for r in range(2):
                        lin_taken(pe, it, st, s, f"h{2 * e + r}")
                    tokens(it, st, s, part, [hid[s][:, 2 * e + r, :] for r in range(2)],
                           [wblk("e2", 2 * e + r) for r in range(2)], R_E + e)
                elif part == "rt":
                    lin_taken(pe, it, st, s, "e2")
                    take(it, st, s, "rt")
                    for b in range(GB):
                        i = nc.tensor.transpose(lin_ap(st, s, "rt")[:, b * T:(b + 1) * T], xn[s][:, b, :], ident[:])
                    give(st, s, "rt", i)
                elif part == "g":
                    lin_taken(pe, it, st, s, "h6")
                    tokens(it, st, s, "g", [hid[s][:, 6, :]], [wblk("g2")], R_GATE)
                elif part == "y":
                    lin_taken(pe, it, st, s, "rt")
                    tokens(it, st, s, "y", [oT[s][:]], [wblk("ow3")], R_OUT)

            with pe.Fori(0, ITERS) as it:
                for kind, u, s in UNITS:
                    if kind == "START":
                        pe.wait_ge(rows_done, 1)
                        pe.wait_ge(rows_in, 48)
                        for g in range(4):
                            scores(it, 0, g)
                        turn(it, 0)
                    elif kind == "A":
                        if s == 3 and u + 1 < JOBS:
                            scores(it, u + 1, s)
                        scores_t(it, u, s)
                        if s < 3 and u + 1 < JOBS:
                            scores(it, u + 1, s)
                        if s == 3:
                            if u > 0:
                                av(it, u - 1, 0)
                            if u + 1 < JOBS:
                                turn(it, u + 1)
                            if u > 0:
                                av(it, u - 1, 1)
                    elif kind == "END":
                        av(it, JOBS - 1, 0)
                        av(it, JOBS - 1, 1)
                    elif kind == "B":
                        st, part = u
                        k = int(st[1:])
                        if u == ("p1", "k"):
                            pe.wait_ge(group_tab, nth(it, 0, s, 1))
                            pe.wait_ge(ctx_in_s[s], it * 32 + 32)
                            hold(pe)
                            if s == 1:
                                pe.wait_ge(w_rest_in, 16 * NREST)
                        if part == "t":
                            norm(it, k, s)
                        elif st[0] == "p":
                            project(it, k, s, part)
                        elif st[0] == "o":
                            outproj(it, k, s)
                        elif st[0] == "m":
                            mlp(it, k, s, part)
                        elif st == "x3":
                            mixture(it, s, part)


def shape_constants():
    inv = 1.0 / 10000.0 ** (np.arange(0, HD, 2, dtype=np.float32) / HD)
    freqs = np.outer(np.arange(HALF, dtype=np.float32), inv)
    emb = np.concatenate([freqs, freqs], axis=-1)
    cos = np.tile(np.cos(emb).astype(np.float32).T, (H, 2))
    sin = np.tile(np.sin(emb).astype(np.float32).T, (H, 2))
    ind = np.zeros((128, H), np.float32)
    ind[np.arange(H), np.arange(H)] = -1.0
    ind[32 + np.arange(H), np.arange(H)] = -1.0
    onesp = np.zeros((128, 4, 32), np.float32)
    for hh in range(4):
        onesp[:, hh, 8 * hh:8 * hh + 8] = 1.0
    hmask = (np.arange(128)[:, None] // HD == np.arange(H)[None, :]).astype(np.float32)
    return np.ascontiguousarray(cos), np.ascontiguousarray(sin), np.eye(128, dtype=np.float32), ind, onesp, hmask


def kernel(**inputs):
    import concourse.bacc as bacc
    from concourse.bass_utils import run_bass_kernel_spmd

    a = {k: np.asarray(v) for k, v in inputs.items()}
    cos, sin, ident, ind, onesp, hmask = shape_constants()

    def blocks(w):
        r, c = w.shape[0] // 128, w.shape[1] // 128
        return w.reshape(r, 128, c, 128).transpose(1, 0, 2, 3).reshape(128, r * c, 128)

    e1, e2 = a["L3_xcond_e_w1"], a["L3_xcond_e_w2"]
    parts = {"ada0": a["L0_xcond_adaLN_W"], "qkv0": a["L0_xcond_qkv_W"], "ao0": a["L0_xcond_attn_out_W"],
             "cq0": a["L0_xcond_cq_W"], "ck0": a["L0_xcond_ck_W"], "cv0": a["L0_xcond_cv_W"],
             "co0": a["L0_xcond_co_W"], "m10": a["L0_xcond_mlp_W1"], "m20": a["L0_xcond_mlp_W2"],
             "wq1": a["L1_xcond_Wq"], "wkv1": a["L1_xcond_Wkv"], "wp1": a["L1_xcond_Wp"],
             "ssq": a["L1_xcond_Wss_q"], "sskv": a["L1_xcond_Wss_kv"], "ada2": a["L2_xcond_ada_w"],
             "qkv2": a["L2_xcond_qkv_w"], "so2": a["L2_xcond_self_o_w"], "q2": a["L2_xcond_q_w"],
             "kv2": a["L2_xcond_kv_w"], "co2": a["L2_xcond_cross_o_w"], "m12": a["L2_xcond_mlp_w1"],
             "m22": a["L2_xcond_mlp_w2"], "q3": a["L3_xcond_Wq"], "k3": a["L3_xcond_Wk"], "v3": a["L3_xcond_Wv"],
             "g2": a["L3_xcond_gate_w2"], "ow3": a["L3_xcond_out_w"]}
    parts = {name: blocks(v) for name, v in parts.items()}
    parts.update(e1=np.concatenate([blocks(e1[e][:256]) for e in range(3)], axis=1),
                 e1a=np.concatenate([blocks(e1[e][256:]) for e in range(3)], axis=1),
                 g1=blocks(a["L3_xcond_gate_w1"][:256]), g1a=blocks(a["L3_xcond_gate_w1"][256:]),
                 e2=np.concatenate([blocks(e2[e]) for e in range(3)], axis=1))
    assert all(parts[name].shape[1] == n for name, n in S_PARTS + W_PARTS)
    ws, w = (np.ascontiguousarray(np.concatenate([parts[name] for name, _ in p], axis=1)) for p in (S_PARTS, W_PARTS))

    def cols(v):
        return v.reshape(-1, 128).T

    b0, b2 = a["L0_xcond_adaLN_b"].reshape(9, 128), a["L2_xcond_ada_b"].reshape(6, 128)
    modb = np.concatenate([b0[[0, 1, 3, 4, 6, 7]], a["L1_xcond_bss_q"].reshape(2, 128),
                           a["L1_xcond_bss_kv"].reshape(2, 128), b2[[0, 1, 3, 4]],
                           a["L3_xcond_e_b1"].reshape(6, 128), a["L3_xcond_gate_b1"].reshape(1, 128)])
    cparts = {"modb": modb, "n1": a["L0_xcond_norm1_w"], "nc": a["L0_xcond_normc_w"], "n2": a["L0_xcond_norm2_w"],
              "g2": a["L2_xcond_norm2_g"], "b2": a["L2_xcond_norm2_b"], "gam": a["L3_xcond_ln_gamma"],
              "bet": a["L3_xcond_ln_beta"], "bq1": a["L1_xcond_bq"], "bk1": a["L1_xcond_bkv"][:128],
              "bv1": a["L1_xcond_bkv"][128:], "qb2": a["L2_xcond_qkv_b"][:128], "kb2": a["L2_xcond_qkv_b"][128:256],
              "vb2": a["L2_xcond_qkv_b"][256:], "cq2": a["L2_xcond_q_b"], "ck2": a["L2_xcond_kv_b"][:128],
              "cv2": a["L2_xcond_kv_b"][128:], "m10": a["L0_xcond_mlp_b1"], "m12": a["L2_xcond_mlp_b1"]}
    col = np.ascontiguousarray(np.concatenate([hmask if n == "hmask" else cols(cparts[n]) for n, _ in C_PARTS], axis=1))
    row = np.ascontiguousarray(np.stack([a["L0_xcond_mlp_b2"], a["L1_xcond_bp"], a["L2_xcond_self_o_b"],
                                         a["L2_xcond_cross_o_b"], a["L2_xcond_mlp_b2"], a["L3_xcond_out_b"],
                                         a["L3_xcond_gate_b2"], *a["L3_xcond_e_b2"]]))
    vcol = np.zeros((128, len(FOLDED), NR), np.float32)
    for c, (r, name, _) in enumerate(FOLDED):
        vcol[:, c, r] = cparts[name]
    gb = np.concatenate([b0[2], b0[5], b0[8], b2[2], b2[5]])
    gb = np.ascontiguousarray(np.broadcast_to(gb[None], (B, NG * 128)))
    rw = np.ascontiguousarray(a["L3_xcond_router_W"].reshape(3, 128, 3).transpose(1, 0, 2))
    rb = np.ascontiguousarray(a["L3_xcond_router_b"].reshape(3, 1))
    m2, mc = a["mask_SxS_bk0"], a["mask_BxS2_bf1"]
    arrays = [("x", np.ascontiguousarray(a["x"].transpose(1, 0, 2))),
              ("ctx", np.ascontiguousarray(a["ctx_1024"].transpose(1, 0, 2))),
              ("ctxT", np.ascontiguousarray(a["ctx_1024"].transpose(2, 0, 1))),
              ("condT", np.ascontiguousarray(a["cond_1024"].T)), ("ws", ws), ("w", w), ("col", col), ("vcol", vcol), ("row", row), ("rw", rw),
              ("rb", rb), ("gb", gb), ("mqk", np.ascontiguousarray(m2)), ("mkq", np.ascontiguousarray(m2.T)),
              ("mc", np.ascontiguousarray(mc.reshape(1, B * C))), ("cos", cos), ("sin", sin),
              ("ident", ident), ("ind", ind), ("onesp", onesp)]
    nc = bacc.Bacc("TRN2", target_bir_lowering=False, num_devices=1)
    ins, args = {}, []
    for name, arr in arrays:
        ins[f"in_{name}"] = arr
        dt = U8 if arr.dtype == bool else mybir.dt.from_np(arr.dtype)
        args.append(nc.dram_tensor(f"in_{name}", arr.shape, dt, kind="ExternalInput").ap())
    out = nc.dram_tensor("out", (T, B, D), F32, kind="ExternalOutput").ap()
    build(nc, *args, out)
    r = run_bass_kernel_spmd(nc, [ins], core_ids=[0])
    return np.ascontiguousarray(r.results[0]["out"].transpose(1, 0, 2))
```
